# Optimizing a Trainium2 kernel written in Bass

```python
import numpy as np
import jax
import jax.numpy as jnp

def _softmax(x, axis=-1):
    return jax.nn.softmax(x, axis=axis)

def _gelu(x):
    return jax.nn.gelu(x, approximate=True)

def _silu(x):
    return jax.nn.silu(x)

def _sigmoid(x):
    return jax.nn.sigmoid(x)

def _layernorm(x, axis=-1, eps=1e-05):
    m = jnp.mean(x, axis=axis, keepdims=True)
    v = jnp.var(x, axis=axis, keepdims=True)
    return (x - m) / jnp.sqrt(v + eps)

def _scatter_add(tgt, idx, src, axis=0):
    return tgt.at[idx].add(src)

def _segment_sum(src, seg, n):
    return jax.ops.segment_sum(src, seg, n)
kernel_name = 'mk_gps_d2_gnn_r32_3c14df'

def setup_inputs(seed: int=0):
    np.random.seed(seed)
    _w = jnp.asarray

    def _rec_inputs():
        import jax
        import jax.numpy as jnp
        _gk = jax.random.key(seed)
        x = -0.0002117 + 1 * jax.random.normal(jax.random.fold_in(_gk, 1), (3125, 256), jnp.float32)
        src = jax.random.randint(jax.random.fold_in(_gk, 2), (50000,), 0, 3125, jnp.int32)
        dst = jnp.minimum((3125 * jax.random.uniform(jax.random.fold_in(_gk, 3), (50000,)) ** 2.0).astype(jnp.int32), 99999)
        _o = jnp.argsort(dst, stable=True)
        src = src[_o]
        dst = dst[_o]
        return (x, src, dst)
    x, src, dst = _rec_inputs()

    def _L0_gnn_setup():
        import jax, jax.numpy as jnp
        import numpy as np
        NEG_SLOPE = 0.2
        key = jax.random.key(seed)
        ks = jax.random.split(key, 8)
        N, E, D, H = (3125, 9375, 256, 256)
        x = jax.random.normal(ks[0], (N, D), dtype=jnp.float32)
        edge_index = jax.random.randint(ks[1], (2, E), 0, N, dtype=jnp.int64)
        s = 0.06
        W = jax.random.normal(ks[2], (H, D), dtype=jnp.float32) * s
        att_src = jax.random.normal(ks[3], (H,), dtype=jnp.float32) * s
        att_dst = jax.random.normal(ks[4], (H,), dtype=jnp.float32) * s
        bias = jnp.zeros((H,), dtype=jnp.float32)
        W_ih = jax.random.normal(ks[5], (4 * H, H), dtype=jnp.float32) * s
        W_hh = jax.random.normal(ks[6], (4 * H, H), dtype=jnp.float32) * s
        return {'x': x, 'edge_index': edge_index, 'W': W, 'att_src': att_src, 'att_dst': att_dst, 'bias': bias, 'W_ih': W_ih, 'W_hh': W_hh}
    _L0_gnn_all = _L0_gnn_setup()
    _L0_gnn_in = {k: v for k, v in _L0_gnn_all.items() if k in ('W', 'att_src', 'att_dst', 'bias', 'W_ih', 'W_hh')}
    del _L0_gnn_all

    def _L0_mix_setup():
        import jax, jax.numpy as jnp
        import numpy as np
        MIDC = 256
        HEADS = 8
        HEADC = MIDC // HEADS
        EPS = 1e-05

        def _ln(x, gamma, beta):
            mu = jnp.mean(x, axis=-1, keepdims=True)
            var = jnp.var(x, axis=-1, keepdims=True)
            return (x - mu) * jax.lax.rsqrt(var + EPS) * gamma + beta
        key = jax.random.key(seed)
        ks = jax.random.split(key, 8)
        B, HW, C = (8, 128, MIDC)
        s = 1.0 / np.sqrt(C)
        return {'x': jax.random.normal(ks[0], (B, HW, C), jnp.float32), 'w_qkv': jax.random.normal(ks[1], (C, 3 * C), jnp.float32) * s, 'b_qkv': jnp.zeros((3 * C,), jnp.float32), 'kln_g': jnp.ones((HEADC,), jnp.float32), 'kln_b': jnp.zeros((HEADC,), jnp.float32), 'vln_g': jnp.ones((HEADC,), jnp.float32), 'vln_b': jnp.zeros((HEADC,), jnp.float32), 'w1': jax.random.normal(ks[2], (C, C), jnp.float32) * s, 'b1': jnp.zeros((C,), jnp.float32), 'w2': jax.random.normal(ks[3], (C, C), jnp.float32) * s, 'b2': jnp.zeros((C,), jnp.float32)}
    _L0_mix_all = _L0_mix_setup()
    _L0_mix_in = {k: v for k, v in _L0_mix_all.items() if k in ('w_qkv', 'b_qkv', 'kln_g', 'kln_b', 'vln_g', 'vln_b', 'w1', 'b1', 'w2', 'b2')}
    del _L0_mix_all

    def _L0_ffn_setup():
        import jax, jax.numpy as jnp
        import numpy as np
        B, T, D, H, E = (16, 128, 256, 512, 8)
        key = jax.random.key(seed)
        ks = jax.random.split(key, 5)
        x = jax.random.normal(ks[0], (B, T, D), dtype=jnp.float32)
        gate_w = jax.random.normal(ks[1], (D, E), dtype=jnp.float32) * 0.02
        gate_b = jnp.zeros((E,), dtype=jnp.float32)
        W1 = jax.random.normal(ks[2], (E, D, H), dtype=jnp.float32) * 0.02
        b1 = jnp.zeros((E, H), dtype=jnp.float32)
        W2 = jax.random.normal(ks[3], (E, H, D), dtype=jnp.float32) * 0.02
        b2 = jnp.zeros((E, D), dtype=jnp.float32)
        return {'x': x, 'gate_w': gate_w, 'gate_b': gate_b, 'W1': W1, 'b1': b1, 'W2': W2, 'b2': b2}
    _L0_ffn_all = _L0_ffn_setup()
    _L0_ffn_in = {k: v for k, v in _L0_ffn_all.items() if k in ('gate_w', 'gate_b', 'W1', 'b1', 'W2', 'b2')}
    del _L0_ffn_all

    def _L1_gnn_setup():
        import jax, jax.numpy as jnp
        import numpy as np
        N, E, IN_DIM, H, D = (50000, 25000, 256, 8, 32)
        ALPHA = 0.2
        key = jax.random.key(seed)
        ks = jax.random.split(key, 6)
        feat = jax.random.normal(ks[0], (N, IN_DIM), dtype=jnp.float32)
        src = jax.random.randint(ks[1], (E,), 0, N, dtype=jnp.int32)
        dst = jax.random.randint(ks[2], (E,), 0, N, dtype=jnp.int32)
        W = jax.random.normal(ks[3], (IN_DIM, H * D), dtype=jnp.float32) * 0.05
        attn_l = jax.random.normal(ks[4], (H, D), dtype=jnp.float32)
        attn_r = jax.random.normal(ks[5], (H, D), dtype=jnp.float32)
        return {'feat': feat, 'src': src, 'dst': dst, 'W': W, 'attn_l': attn_l, 'attn_r': attn_r}
    _L1_gnn_all = _L1_gnn_setup()
    _L1_gnn_in = {k: v for k, v in _L1_gnn_all.items() if k in ('W', 'attn_l', 'attn_r')}
    del _L1_gnn_all

    def _L1_mix_setup():
        import jax, jax.numpy as jnp
        import numpy as np
        B, N, C, H = (8, 512, 256, 8)
        D = C // H
        GH = C // 4
        key = jax.random.key(seed)
        ks = jax.random.split(key, 6)
        s = 0.02
        return {'x': jax.random.normal(ks[0], (B, N, C), dtype=jnp.float32), 'Wqkv': jax.random.normal(ks[1], (C, 3 * C), dtype=jnp.float32) * s, 'Wproj': jax.random.normal(ks[2], (C, C), dtype=jnp.float32) * s, 'bproj': jnp.zeros((C,), dtype=jnp.float32), 'ln_g': jnp.ones((C,), dtype=jnp.float32), 'ln_b': jnp.zeros((C,), dtype=jnp.float32), 'Wg1': jax.random.normal(ks[3], (C, GH), dtype=jnp.float32) * s, 'bg1': jnp.zeros((GH,), dtype=jnp.float32), 'Wg2': jax.random.normal(ks[4], (GH, C), dtype=jnp.float32) * s, 'bg2': jnp.zeros((C,), dtype=jnp.float32)}
    _L1_mix_all = _L1_mix_setup()
    _L1_mix_in = {k: v for k, v in _L1_mix_all.items() if k in ('Wqkv', 'Wproj', 'bproj', 'ln_g', 'ln_b', 'Wg1', 'bg1', 'Wg2', 'bg2')}
    del _L1_mix_all

    def _L1_ffn_setup():
        import jax, jax.numpy as jnp
        import numpy as np
        B, S, D, E, H, K = (4, 128, 256, 8, 512, 2)
        key = jax.random.key(seed)
        ks = jax.random.split(key, 6)
        x = jax.random.normal(ks[0], (B, S, D), jnp.float32)
        Wg = jax.random.normal(ks[1], (D, E), jnp.float32) * 0.02
        bg = jnp.zeros((E,), jnp.float32)
        W1 = jax.random.normal(ks[2], (E, D, H), jnp.float32) * 0.02
        b1 = jnp.zeros((E, H), jnp.float32)
        W2 = jax.random.normal(ks[3], (E, H, D), jnp.float32) * 0.02
        b2 = jnp.zeros((E, D), jnp.float32)
        return {'x': x, 'Wg': Wg, 'bg': bg, 'W1': W1, 'b1': b1, 'W2': W2, 'b2': b2}
    _L1_ffn_all = _L1_ffn_setup()
    _L1_ffn_in = {k: v for k, v in _L1_ffn_all.items() if k in ('Wg', 'bg', 'W1', 'b1', 'W2', 'b2')}
    del _L1_ffn_all
    return {'x': x, 'src': src, 'dst': dst, 'L0_gnn_W': _L0_gnn_in['W'], 'L0_gnn_att_src': _L0_gnn_in['att_src'], 'L0_gnn_att_dst': _L0_gnn_in['att_dst'], 'L0_gnn_bias': _L0_gnn_in['bias'], 'L0_gnn_W_ih': _L0_gnn_in['W_ih'], 'L0_gnn_W_hh': _L0_gnn_in['W_hh'], 'L0_mix_w_qkv': _L0_mix_in['w_qkv'], 'L0_mix_b_qkv': _L0_mix_in['b_qkv'], 'L0_mix_kln_g': _L0_mix_in['kln_g'], 'L0_mix_kln_b': _L0_mix_in['kln_b'], 'L0_mix_vln_g': _L0_mix_in['vln_g'], 'L0_mix_vln_b': _L0_mix_in['vln_b'], 'L0_mix_w1': _L0_mix_in['w1'], 'L0_mix_b1': _L0_mix_in['b1'], 'L0_mix_w2': _L0_mix_in['w2'], 'L0_mix_b2': _L0_mix_in['b2'], 'L0_ffn_gate_w': _L0_ffn_in['gate_w'], 'L0_ffn_gate_b': _L0_ffn_in['gate_b'], 'L0_ffn_W1': _L0_ffn_in['W1'], 'L0_ffn_b1': _L0_ffn_in['b1'], 'L0_ffn_W2': _L0_ffn_in['W2'], 'L0_ffn_b2': _L0_ffn_in['b2'], 'L1_gnn_W': _L1_gnn_in['W'], 'L1_gnn_attn_l': _L1_gnn_in['attn_l'], 'L1_gnn_attn_r': _L1_gnn_in['attn_r'], 'L1_mix_Wqkv': _L1_mix_in['Wqkv'], 'L1_mix_Wproj': _L1_mix_in['Wproj'], 'L1_mix_bproj': _L1_mix_in['bproj'], 'L1_mix_ln_g': _L1_mix_in['ln_g'], 'L1_mix_ln_b': _L1_mix_in['ln_b'], 'L1_mix_Wg1': _L1_mix_in['Wg1'], 'L1_mix_bg1': _L1_mix_in['bg1'], 'L1_mix_Wg2': _L1_mix_in['Wg2'], 'L1_mix_bg2': _L1_mix_in['bg2'], 'L1_ffn_Wg': _L1_ffn_in['Wg'], 'L1_ffn_bg': _L1_ffn_in['bg'], 'L1_ffn_W1': _L1_ffn_in['W1'], 'L1_ffn_b1': _L1_ffn_in['b1'], 'L1_ffn_W2': _L1_ffn_in['W2'], 'L1_ffn_b2': _L1_ffn_in['b2']}

def reference(x, src, dst, L0_gnn_W, L0_gnn_att_src, L0_gnn_att_dst, L0_gnn_bias, L0_gnn_W_ih, L0_gnn_W_hh, L0_mix_w_qkv, L0_mix_b_qkv, L0_mix_kln_g, L0_mix_kln_b, L0_mix_vln_g, L0_mix_vln_b, L0_mix_w1, L0_mix_b1, L0_mix_w2, L0_mix_b2, L0_ffn_gate_w, L0_ffn_gate_b, L0_ffn_W1, L0_ffn_b1, L0_ffn_W2, L0_ffn_b2, L1_gnn_W, L1_gnn_attn_l, L1_gnn_attn_r, L1_mix_Wqkv, L1_mix_Wproj, L1_mix_bproj, L1_mix_ln_g, L1_mix_ln_b, L1_mix_Wg1, L1_mix_bg1, L1_mix_Wg2, L1_mix_bg2, L1_ffn_Wg, L1_ffn_bg, L1_ffn_W1, L1_ffn_b1, L1_ffn_W2, L1_ffn_b2):
    import jax
    import jax.numpy as jnp

    def _L0_gnn_ref(x, edge_index, W, att_src, att_dst, bias, W_ih, W_hh):
        import jax, jax.numpy as jnp
        import numpy as np
        NEG_SLOPE = 0.2
        N = x.shape[0]
        loops = jnp.arange(N, dtype=edge_index.dtype)
        src = jnp.concatenate([edge_index[0], loops])
        dst = jnp.concatenate([edge_index[1], loops])
        xp = x @ W.T
        a_src = xp @ att_src
        a_dst = xp @ att_dst
        e = jax.nn.leaky_relu(a_src[src] + a_dst[dst], NEG_SLOPE)
        emax = jax.ops.segment_max(e, dst, num_segments=N)
        ex = jnp.exp(e - emax[dst])
        denom = jax.ops.segment_sum(ex, dst, num_segments=N)
        alpha = ex / denom[dst]
        agg = jax.ops.segment_sum(alpha[:, None] * xp[src], dst, num_segments=N)
        hb = jnp.tanh(agg + bias)
        h0 = jnp.zeros_like(hb)
        gates = hb @ W_ih.T + h0 @ W_hh.T
        i, f, g, o = jnp.split(gates, 4, axis=-1)
        c1 = jax.nn.sigmoid(i) * jnp.tanh(g)
        h1 = jax.nn.sigmoid(o) * jnp.tanh(c1)
        return h1

    def _L0_mix_ref(x, w_qkv, b_qkv, kln_g, kln_b, vln_g, vln_b, w1, b1, w2, b2):
        import jax, jax.numpy as jnp
        import numpy as np
        MIDC = 256
        HEADS = 8
        HEADC = MIDC // HEADS
        EPS = 1e-05

        def _ln(x, gamma, beta):
            mu = jnp.mean(x, axis=-1, keepdims=True)
            var = jnp.var(x, axis=-1, keepdims=True)
            return (x - mu) * jax.lax.rsqrt(var + EPS) * gamma + beta
        B, HW, C = x.shape
        bias = x
        qkv = (x @ w_qkv + b_qkv).reshape(B, HW, HEADS, 3 * HEADC)
        qkv = qkv.transpose(0, 2, 1, 3)
        q, k, v = jnp.split(qkv, 3, axis=-1)
        k = _ln(k, kln_g, kln_b)
        v = _ln(v, vln_g, vln_b)
        kv = jnp.einsum('bhnd,bhne->bhde', k, v) / HW
        out = jnp.einsum('bhnd,bhde->bhne', q, kv)
        out = out.transpose(0, 2, 1, 3).reshape(B, HW, C)
        ret = out + bias
        h = jax.nn.gelu(ret @ w1 + b1, approximate=False)
        return h @ w2 + b2 + bias

    def _L0_ffn_ref(x, gate_w, gate_b, W1, b1, W2, b2):
        import jax, jax.numpy as jnp
        import numpy as np
        B, T, D, H, E = (16, 128, 256, 512, 8)
        Bb, Tt, Dd = x.shape
        Ee = gate_w.shape[1]
        xf = x.reshape(-1, Dd)
        N = xf.shape[0]
        logits = xf @ gate_w + gate_b
        probs = jax.nn.softmax(logits, axis=-1)
        top2_vals, top2_idx = jax.lax.top_k(probs, 2)
        cw = jnp.zeros((N, Ee), dtype=xf.dtype).at[jnp.arange(N)[:, None], top2_idx].add(top2_vals)

        def step(acc, params):
            w1, bb1, w2, bb2, we = params
            h = jax.nn.gelu(xf @ w1 + bb1, approximate=False)
            y = h @ w2 + bb2
            return (acc + we[:, None] * y, None)
        out, _ = jax.lax.scan(step, jnp.zeros_like(xf), (W1, b1, W2, b2, cw.T))
        return out.reshape(Bb, Tt, Dd)

    def _L1_gnn_ref(feat, src, dst, W, attn_l, attn_r):
        import jax, jax.numpy as jnp
        import numpy as np
        N, E, IN_DIM, H, D = (50000, 25000, 256, 8, 32)
        ALPHA = 0.2
        n = feat.shape[0]
        ft = (feat @ W).reshape(n, H, D)
        a1 = jnp.einsum('nhd,hd->nh', ft, attn_l)
        a2 = jnp.einsum('nhd,hd->nh', ft, attn_r)
        e = jax.nn.leaky_relu(a1[src] + a2[dst], negative_slope=ALPHA)
        m = jax.ops.segment_max(e, dst, num_segments=n)
        ex = jnp.exp(e - m[dst])
        s = jax.ops.segment_sum(ex, dst, num_segments=n)
        alpha = ex / s[dst]
        msg = ft[src] * alpha[:, :, None]
        out = jax.ops.segment_sum(msg, dst, num_segments=n)
        return jax.nn.elu(out.reshape(n, H * D))

    def _L1_mix_ref(x, Wqkv, Wproj, bproj, ln_g, ln_b, Wg1, bg1, Wg2, bg2):
        import jax, jax.numpy as jnp
        import numpy as np
        B, N, C, H = (8, 512, 256, 8)
        D = C // H
        GH = C // 4
        b, n, c = x.shape
        h, d = (H, D)
        qkv = (x @ Wqkv).reshape(b, n, 3, h, d)
        q, k, v = (qkv[:, :, 0], qkv[:, :, 1], qkv[:, :, 2])
        k = jax.nn.softmax(k, axis=1)
        context = jnp.einsum('bnhd,bnhv->bhdv', k, v)
        out = jnp.einsum('bnhd,bhdv->bnhv', q, context).reshape(b, n, c)
        mu = jnp.mean(x, axis=-1, keepdims=True)
        var = jnp.var(x, axis=-1, keepdims=True)
        xn = (x - mu) * jax.lax.rsqrt(var + 1e-05) * ln_g + ln_b
        hgate = jax.nn.gelu(xn @ Wg1 + bg1, approximate=False)
        gate = jax.nn.sigmoid(hgate @ Wg2 + bg2)
        return out * gate @ Wproj + bproj

    def _L1_ffn_ref(x, Wg, bg, W1, b1, W2, b2):
        import jax, jax.numpy as jnp
        import numpy as np
        B, S, D, E, H, K = (4, 128, 256, 8, 512, 2)
        Bv, Sv, Dv = x.shape
        gate_scores = x @ Wg + bg
        _, idx = jax.lax.top_k(gate_scores, K)
        mask = jax.nn.one_hot(idx, E, dtype=x.dtype).sum(axis=-2)
        xf = x.reshape(-1, Dv)
        mf = mask.reshape(-1, E)
        h = jax.nn.gelu(jnp.einsum('td,edh->teh', xf, W1) + b1[None], approximate=False)
        y = jnp.einsum('teh,ehd->ted', h, W2) + b2[None]
        out = jnp.einsum('ted,te->td', y, mf)
        return out.reshape(Bv, Sv, Dv)
    edge_index = jnp.stack([src, dst])
    xn = _layernorm(x, axis=-1)
    x = x + _L0_gnn_ref(xn, edge_index, L0_gnn_W, L0_gnn_att_src, L0_gnn_att_dst, L0_gnn_bias, L0_gnn_W_ih, L0_gnn_W_hh) + _L0_mix_ref(xn[None], L0_mix_w_qkv, L0_mix_b_qkv, L0_mix_kln_g, L0_mix_kln_b, L0_mix_vln_g, L0_mix_vln_b, L0_mix_w1, L0_mix_b1, L0_mix_w2, L0_mix_b2)[0]
    x = x + _L0_ffn_ref(_layernorm(x, axis=-1)[None], L0_ffn_gate_w, L0_ffn_gate_b, L0_ffn_W1, L0_ffn_b1, L0_ffn_W2, L0_ffn_b2)[0]
    xn = _layernorm(x, axis=-1)
    x = x + _L1_gnn_ref(xn, src, dst, L1_gnn_W, L1_gnn_attn_l, L1_gnn_attn_r) + _L1_mix_ref(xn[None], L1_mix_Wqkv, L1_mix_Wproj, L1_mix_bproj, L1_mix_ln_g, L1_mix_ln_b, L1_mix_Wg1, L1_mix_bg1, L1_mix_Wg2, L1_mix_bg2)[0]
    x = x + _L1_ffn_ref(_layernorm(x, axis=-1)[None], L1_ffn_Wg, L1_ffn_bg, L1_ffn_W1, L1_ffn_b1, L1_ffn_W2, L1_ffn_b2)[0]
    return x

_drawn_inputs = setup_inputs


def setup_inputs(seed=0):
    import zlib

    import numpy as np

    out = dict(_drawn_inputs(seed))
    spreads = {'L0_gnn_bias': (0.0, 0.576),
     'L0_mix_b_qkv': (0.0, 0.1),
     'L0_mix_kln_g': (1.0, 0.586),
     'L0_mix_kln_b': (0.0, 0.348),
     'L0_mix_vln_g': (1.0, 0.2),
     'L0_mix_vln_b': (0.0, 0.319),
     'L0_mix_b1': (0.0, 0.1),
     'L0_mix_b2': (0.0, 0.1),
     'L0_ffn_gate_b': (0.0, 0.641),
     'L0_ffn_b1': (0.0, 0.8),
     'L0_ffn_b2': (0.0, 0.514),
     'L1_mix_bproj': (0.0, 0.8),
     'L1_mix_ln_g': (1.0, 0.6),
     'L1_mix_ln_b': (0.0, 0.8),
     'L1_mix_bg1': (0.0, 0.8),
     'L1_mix_bg2': (0.0, 0.8),
     'L1_ffn_bg': (0.0, 0.528),
     'L1_ffn_b1': (0.0, 2.0),
     'L1_ffn_b2': (0.0, 0.6)}
    factors = {'L0_gnn_att_src': 2.743,
     'L0_gnn_att_dst': 7.657,
     'L0_ffn_gate_w': 3.485,
     'L0_ffn_W1': 4.706,
     'L0_ffn_W2': 4.377,
     'L1_mix_Wqkv': 6.482,
     'L1_mix_Wproj': 6.627,
     'L1_mix_Wg1': 8.0,
     'L1_mix_Wg2': 8.0,
     'L1_gnn_attn_r': 15.097,
     'L1_ffn_W1': 4.867}
    for name, (base, spread) in spreads.items():
        noise = np.random.default_rng([zlib.crc32(name.encode()), seed]).standard_normal(out[name].shape)
        drawn = base * np.exp(spread * noise) if base else spread * noise
        out[name] = jnp.asarray(drawn.astype(out[name].dtype))
    for name, factor in factors.items():
        out[name] = (out[name] * factor).astype(out[name].dtype)
    return out
```

```python
from contextlib import ExitStack

import concourse.bass as bass
from concourse import mybir

F32 = mybir.dt.float32
I32 = mybir.dt.int32
ALU = mybir.AluOpType
ACT = mybir.ActivationFunctionType
AX = mybir.AxisListType
MAX = bass.bass_isa.ReduceOp.max

N, E = 3125, 50000
P, NT = 125, 25
D = 256
KD = D // 128
HEADS, HC = 8, 32
NE, HID = 8, 512
KH = HID // 128
EPS = 1e-5
SLOPE = 0.2
BIG = 3.0e38
SAFE = 60.0

PAD = 256
FAR = 8000
WIN = 2
GE = WIN * 128
NG = (E + NT * (GE - 1)) // GE + 1
NG += -NG % 8

ROWS = 256
NB = (2 * N + NE * (ROWS - 1)) // ROWS
EC = E // P


class Chain:

    def __init__(self, eng, sem, per):
        self.eng, self.sem, self.per = eng, sem, per
        self.base, self.n = 0, 0

    def step(self, t):
        self.base, self.n = t * self.per, 0

    def link(self, ins):
        ins.then_inc(self.sem, 1)
        self.n += 1
        self.eng.wait_ge(self.sem, self.base + self.n)

    def close(self):
        assert self.n == self.per, self.n


class Stage(ExitStack):

    def __init__(self, nc):
        super().__init__()
        self.nc, self.sems = nc, []

    def sem(self, name):
        self.sems.append(self.nc.alloc_semaphore(name))
        return self.sems[-1]

    def __exit__(self, *error):
        super().__exit__(*error)
        if not error[0]:
            self.nc.clear_and_free_semaphores(self.sems)
            self.nc.all_engine_barrier()


class Memory:
    pass


def tile_cols(t):
    return bass.ds(t * P, P)


def over_tiles(eng, step):
    with eng.Fori(0, NT // 2) as b:
        step(b * 2, 0)
        step(b * 2 + 1, 1)
    step(NT - 1, (NT - 1) % 2)


def constants(nc, m):
    with Stage(nc) as c, nc.Block() as block:
        const_set = c.sem("const_set")

        @block.gpsimd
        def _(pool):
            c = Chain(pool, const_set, 0)
            c.link(pool.memset(m.ident[:, :], 0.0))
            c.link(pool.affine_select(out=m.ident[:, :], in_=m.ident[:, :], pattern=[[-1, 128]],
                                      compare_op=ALU.not_equal, fill=1.0, base=0, channel_multiplier=1))
            c.link(pool.memset(m.ones[:, :], 1.0))
            c.link(pool.memset(m.before[:, :], 1.0))
            c.link(pool.affine_select(out=m.before[:, :], in_=m.before[:, :], pattern=[[1, P]],
                                      compare_op=ALU.is_ge, fill=0.0, base=-1, channel_multiplier=-1))
            c.link(pool.memset(m.headmask[:, :], 1.0))
            hm = m.headmask[:, :].rearrange("p (g c) -> p g c", c=HC)
            c.link(pool.affine_select(out=hm, in_=hm, pattern=[[-HC, 4], [0, HC]], compare_op=ALU.is_ge,
                                      fill=0.0, base=0, channel_multiplier=1))
            c.link(pool.affine_select(out=hm, in_=hm, pattern=[[HC, 4], [0, HC]], compare_op=ALU.is_ge,
                                      fill=0.0, base=HC - 1, channel_multiplier=-1))
            c.link(pool.iota(m.nodes[:, :], pattern=[[1, N]], base=0, channel_multiplier=0,
                             allow_small_or_imprecise_dtypes=True))
            c.link(pool.memset(m.half[:, :], -0.5))


def edge_tables(nc, m, src, dst):
    with Stage(nc) as c:
        def sb(n, s, d=F32):
            return c.enter_context(nc.sbuf_tensor(n, s, d))

        def sem(n):
            return c.sem(n)

        pairs = sb("edge_pairs", [P, EC, 2], I32)
        ends = sb("edge_ends", [P, 2, EC], I32)
        dstf = sb("edge_dstf", [P, EC])
        hit = sb("edge_hit", [P, EC])
        cnt = sb("edge_cnt", [P, NT + 1])
        pad = sb("edge_pad", [128, PAD // 128, 2], I32)
        first = sb("edge_first", [128, NT + 1])
        size_i = sb("edge_size_i", [128, NT], I32)
        groups = sb("edge_groups", [128, NT])
        gend = sb("edge_gend", [128, NT])
        base = sb("edge_base", [128, NT + 1])
        gcol = sb("edge_gcol", [128, 2, NT])
        gnum = sb("edge_gnum", [128, 2])
        past = sb("edge_past", [128, 2, NT])
        gt = sb("edge_gt", [128, 2, 2])
        zero = sb("edge_zero", [128, NT])
        row = sb("edge_row", [2, 2, 128])
        loaded, chain, counted, summed = sem("edge_loaded"), sem("edge_chain"), sem("edge_counted"), sem("edge_summed")
        joined, stored, setup, tabled, turned = sem("edge_joined"), sem("edge_stored"), sem("edge_setup"), sem("edge_tabled"), sem("edge_turned")
        rows_set, moved = sem("edge_rows_set"), sem("edge_moved")
        GH = NG // 2
        with nc.Block() as block:
            @block.sync
            def _(sp):
                sp.dma_start(ends[:, 0, :], src.rearrange("(p c) -> p c", c=EC)).then_inc(loaded, 16)
                sp.dma_start(ends[:, 1, :], dst.rearrange("(p c) -> p c", c=EC)).then_inc(loaded, 16)
                sp.wait_ge(joined, 2)
                sp.dma_start(m.edges[0:E, :].rearrange("(p c) x -> p c x", c=EC), pairs[:, :, :]).then_inc(stored, 16)
                sp.wait_ge(setup, 4)
                sp.dma_start(m.edges[E:E + PAD, :].rearrange("(p c) x -> p c x", p=128), pad[:, :, :]).then_inc(stored, 16)
                sp.wait_ge(stored, 32)
                sp.wait_ge(rows_set, 1)
                for h in range(2):
                    sp.dma_start(m.gtab[0:1, 0, h * GH:(h + 1) * GH], m.grow[0:1, h, 0, 0:GH]).then_inc(moved, 16)
                    sp.dma_start(m.gtab[0:1, 1, h * GH:(h + 1) * GH], m.grow[0:1, h, 1, 0:GH]).then_inc(moved, 16)
                sp.wait_ge(moved, 64)

            @block.gpsimd
            def _(pool):
                pool.memset(pad[:, :, 0], 0).then_inc(setup, 1)
                pool.memset(pad[:, :, 1], FAR).then_inc(setup, 1)
                pool.memset(zero[:, :], 0.0).then_inc(setup, 1)
                pool.iota(gnum[:, :], pattern=[[GH, 2]], base=0, channel_multiplier=1,
                          allow_small_or_imprecise_dtypes=True).then_inc(setup, 1)

            @block.vector
            def _(v):
                k = Chain(v, chain, 0)
                v.wait_ge(loaded, 32)
                v.tensor_copy(pairs[:, :, 0], ends[:, 0, :]).then_inc(joined, 1)
                v.tensor_copy(pairs[:, :, 1], ends[:, 1, :]).then_inc(joined, 1)
                k.link(v.tensor_copy(dstf[:, :], ends[:, 1, :]))
                v.memset(cnt[:, 0:1], 0.0).then_inc(counted, 1)
                for t in range(1, NT + 1):
                    k.link(v.tensor_scalar(hit[:, :], dstf[:, :], float(t * P), 0.0, ALU.is_lt, ALU.add,
                                           accum_out=cnt[:, t:t + 1]))
                v.sem_inc(counted, 1)
                v.wait_ge(summed, 1)
                k.link(v.tensor_copy(first[:, :], m.bank[0][:, 0:NT + 1]))
                k.link(v.tensor_tensor(groups[:, :], first[:, 1:NT + 1], first[:, 0:NT], ALU.subtract))
                k.link(v.tensor_scalar(size_i[:, :], groups[:, :], float(GE - 1), None, ALU.add))
                k.link(v.tensor_scalar(size_i[:, :], size_i[:, :], 8, None, ALU.arith_shift_right))
                k.link(v.tensor_copy(groups[:, :], size_i[:, :]))
                v.wait_ge(setup, 4)
                k.link(v.tensor_tensor_scan(gend[:, :], groups[:, :], zero[:, :], 0.0, ALU.add, ALU.add))
                k.link(v.tensor_copy(base[:, 0:1], first[:, 0:1]))
                k.link(v.scalar_tensor_tensor(base[:, 1:NT + 1], gend[:, :], -float(GE), first[:, 1:NT + 1],
                                              ALU.mult, ALU.add))
                for h in range(2):
                    k.link(v.tensor_scalar(past[:, h, :], gend[:, :], gnum[:, h:h + 1], None, ALU.is_le))
                    k.link(v.tensor_reduce(gt[:, 0, h:h + 1], past[:, h, :], AX.X, ALU.add))
                    k.link(v.tensor_scalar(gt[:, 0, h:h + 1], gt[:, 0, h:h + 1], float(NT - 1), None, ALU.min))
                    k.link(v.tensor_tensor(gcol[:, h, :], base[:, 1:NT + 1], base[:, 0:NT], ALU.subtract))
                    k.link(v.tensor_tensor(gcol[:, h, :], gcol[:, h, :], past[:, h, :], ALU.mult))
                    k.link(v.tensor_reduce(gt[:, 1, h:h + 1], gcol[:, h, :], AX.X, ALU.add))
                    k.link(v.scalar_tensor_tensor(gt[:, 1, h:h + 1], gnum[:, h:h + 1], float(GE), gt[:, 1, h:h + 1],
                                                  ALU.mult, ALU.add))
                    k.link(v.tensor_scalar(gt[:, 1, h:h + 1], gt[:, 1, h:h + 1], float(E), None, ALU.min))
                v.sem_inc(tabled, 1)
                v.wait_ge(turned, 1)
                v.tensor_copy(m.grow[:, :, :, :].rearrange("o h x g -> o (h x g)"),
                              m.bank[1][0:1, 0:512]).then_inc(rows_set, 1)

            @block.tensor
            def _(pe):
                pe.wait_ge(counted, 2)
                pe.matmul(m.bank[0][:, 0:NT + 1], m.ones[0:P, :], cnt[:, :], start=True, stop=True).then_inc(summed, 1)
                pe.wait_ge(tabled, 1)
                for h in range(2):
                    for x in range(2):
                        at = (h * 2 + x) * 128
                        ins = pe.transpose(m.bank[1][0:1, at:at + 128], gt[:, x, h:h + 1], m.ident[:, :])
                ins.then_inc(turned, 1)


def moments(v, chained, stats, mean, var, half, other):
    k = Chain(v, chained, 0)
    k.link(v.tensor_tensor(mean, stats[:, :, 1], stats[:, :, 4], ALU.add))
    k.link(v.tensor_tensor(half, stats[:, :, 1], stats[:, :, 4], ALU.subtract))
    k.link(v.tensor_scalar(mean, mean, 0.5, None, ALU.mult))
    k.link(v.tensor_scalar(half, half, 0.5, None, ALU.mult))
    k.link(v.tensor_tensor(half, half, half, ALU.mult))
    k.link(v.tensor_tensor(other, stats[:, :, 2], stats[:, :, 5], ALU.add))
    k.link(v.scalar_tensor_tensor(var, other, 1.0 / D, half, ALU.mult, ALU.add))
    k.link(v.tensor_scalar(var, var, EPS, None, ALU.add))


def normalise(nc, m, tag, src):
    with Stage(nc) as c:
        stats = c.enter_context(nc.sbuf_tensor(tag + "_stats", [P, NT, 6], F32))
        half = c.enter_context(nc.sbuf_tensor(tag + "_half", [P, NT], F32))
        other = c.enter_context(nc.sbuf_tensor(tag + "_other", [P, NT], F32))
        stated, meaned, powered = [c.sem(tag + n) for n in ("_stated", "_meaned", "_powered")]
        with nc.Block() as block:
            @block.vector
            def _(v):
                with v.Fori(0, NT // 5) as b:
                    for u in range(5):
                        v.bn_stats(row_of(stats, b * 5 + u), row_of(src, b * 5 + u)).then_inc(stated, 1)
                v.wait_ge(stated, NT)
                moments(v, meaned, stats, m.mean[:, :], m.rstd[:, :], half[:, :], other[:, :])

            @block.gpsimd
            def _(pool):
                pool.wait_ge(meaned, 8)
                pool.tensor_tensor(m.rstd[:, :], m.rstd[:, :], m.half[0:P, 0:NT], ALU.pow).then_inc(powered, 1)
                pool.wait_ge(powered, 1)


def load_x(nc, m, x):
    zrow = 16
    with Stage(nc) as c, nc.sbuf_tensor("zrows", [128, zrow, D], F32) as zrows, nc.Block() as block:
        zeroed, cleared, x_loaded = c.sem("zeroed"), c.sem("cleared"), c.sem("x_loaded")

        @block.vector
        def _(v):
            v.memset(zrows[:, :, :], 0.0).then_inc(zeroed, 1)

        @block.scalar
        def _(a):
            a.wait_ge(zeroed, 1)
            for i in range(NB * ROWS // (128 * zrow)):
                a.dma_start(m.xsort[i * 128 * zrow:(i + 1) * 128 * zrow, :].rearrange("(p w) d -> p w d", p=128),
                            zrows[:, :, :]).then_inc(cleared, 16)
            a.wait_ge(cleared, 16 * (NB * ROWS // (128 * zrow)))


        @block.sync
        def _(sp):
            sp.dma_start(m.xs[:, :, :], x.rearrange("(t p) d -> p t d", p=P)).then_inc(x_loaded, 16)
            sp.wait_ge(x_loaded, 16)


def store_x(nc, m, out):
    with Stage(nc) as c, nc.Block() as block:
        out_stored = c.sem("out_stored")

        @block.sync
        def _(sp):
            sp.dma_start(out.rearrange("(t p) d -> p t d", p=P), m.xs[:, :, :]).then_inc(out_stored, 16)
            sp.wait_ge(out_stored, 16)


def weights0(nc, m, c, w):
    def sb(n, s):
        return c.enter_context(nc.sbuf_tensor(n, s, F32))

    m.nodew = sb("w0_node", [128, KD, D + 2])
    m.gatew = sb("w0_gates", [128, KD, 3 * D])
    m.gbias = sb("w0_gbias", [P, D])
    m.wq = sb("w0_q", [128, KD, D])
    m.wkv = sb("w0_kv", [128, KD, 2 * D])
    m.bq = sb("w0_bq", [128, KD])
    m.bkv = sb("w0_bkv", [P, 2 * D])
    m.lng = sb("w0_lng", [P, 2 * D])
    m.lnb = sb("w0_lnb", [P, 2 * D])
    m.w1 = sb("w0_w1", [128, KD, D])
    m.b1 = sb("w0_b1", [128, KD])
    m.w2 = sb("w0_w2", [128, KD, D])
    m.b2 = sb("w0_b2", [P, D])
    with Stage(nc) as c2:
        wn = c2.enter_context(nc.sbuf_tensor("w0_nat", [128, KD, D], F32))
        an = c2.enter_context(nc.sbuf_tensor("w0_att", [128, KD, 2], F32))
        gn = c2.enter_context(nc.sbuf_tensor("w0_gnat", [128, 6, D], F32))
        loaded, turned, kept = [c2.sem("w0_" + n) for n in ("loaded", "turned", "kept")]
        jobs = [(wn[:, :, :], w["L0_gnn_W"].rearrange("(k p) d -> p k d", p=128)),
                (an[:, :, 0], w["L0_gnn_att_src"].rearrange("(k p) -> p k", p=128)),
                (an[:, :, 1], w["L0_gnn_att_dst"].rearrange("(k p) -> p k", p=128)),
                (gn[:, 0:2, :], w["L0_gnn_W_ih"][0:D, :].rearrange("(k p) d -> p k d", p=128)),
                (gn[:, 2:4, :], w["L0_gnn_W_ih"][3 * D:4 * D, :].rearrange("(k p) d -> p k d", p=128)),
                (gn[:, 4:6, :], w["L0_gnn_W_ih"][2 * D:3 * D, :].rearrange("(k p) d -> p k d", p=128)),
                (m.gbias[:, :], w["L0_gnn_bias"].partition_broadcast(P)),
                (m.w1[:, :, :], w["L0_mix_w1"].rearrange("(k p) d -> p k d", p=128)),
                (m.w2[:, :, :], w["L0_mix_w2"].rearrange("(k p) d -> p k d", p=128)),
                (m.b1[:, :], w["L0_mix_b1"].rearrange("(k p) -> p k", p=128)),
                (m.b2[:, :], w["L0_mix_b2"].partition_broadcast(P))]
        qkv = w["L0_mix_w_qkv"].rearrange("(k p) (h x c) -> k p x h c", p=128, x=3, c=HC)
        bqkv = w["L0_mix_b_qkv"].rearrange("(h x c) -> x h c", x=3, c=HC)
        for k in range(KD):
            jobs.append((m.wq[:, k, :].rearrange("p (h c) -> p h c", c=HC), qkv[k, :, 0]))
            for x in range(2):
                jobs.append((m.wkv[:, k, x * D:(x + 1) * D].rearrange("p (h c) -> p h c", c=HC), qkv[k, :, 1 + x]))
            for h in range(4):
                jobs.append((m.bq[h * HC:(h + 1) * HC, k:k + 1], bqkv[0, 4 * k + h, :].rearrange("(c o) -> c o", o=1)))
        for x in range(2):
            jobs.append((m.bkv[:, x * D:(x + 1) * D].rearrange("p (h c) -> p h c", c=HC), bqkv[1 + x].partition_broadcast(P)))
        for x, (g, b) in enumerate((("kln_g", "kln_b"), ("vln_g", "vln_b"))):
            for t, n in ((m.lng, g), (m.lnb, b)):
                jobs.append((t[:, x * D:(x + 1) * D].rearrange("p (h c) -> p h c", c=HC),
                             w["L0_mix_" + n].rearrange("(o c) -> o c", o=1).to_broadcast([HEADS, HC]).partition_broadcast(P)))
        with nc.Block() as block:
            @block.sync
            def _(sp):
                for dst, src in jobs:
                    sp.dma_start(dst, src).then_inc(loaded, 16)
                sp.wait_ge(loaded, 16 * len(jobs))

            @block.tensor
            def _(pe):
                pe.wait_ge(loaded, 16 * len(jobs))
                for k in range(KD):
                    for h in range(KD):
                        pe.transpose(m.bank[k][:, h * 128:(h + 1) * 128], wn[:, h, k * 128:(k + 1) * 128], m.ident[:, :])
                    for h in range(KD):
                        ins = pe.matmul(m.bank[k][:, D:D + 2], wn[:, h, k * 128:(k + 1) * 128], an[:, h, :],
                                        start=(h == 0), stop=(h == KD - 1))
                    ins.then_inc(turned, 1)
                for k in range(KD):
                    for u in range(6):
                        at = 2 + 2 * k + u // 4
                        ins = pe.transpose(m.bank[at][:, (u % 4) * 128:(u % 4 + 1) * 128], gn[:, u, k * 128:(k + 1) * 128], m.ident[:, :])
                    ins.then_inc(turned, 1)

            @block.vector
            def _(v):
                for k in range(KD):
                    v.wait_ge(turned, k + 1)
                    v.tensor_copy(m.nodew[:, k, :], m.bank[k][:, 0:D + 2]).then_inc(kept, 1)
                for k in range(KD):
                    v.wait_ge(turned, KD + k + 1)
                    v.tensor_copy(m.gatew[:, k, 0:2 * D], m.bank[2 + 2 * k][:, 0:512]).then_inc(kept, 1)
                    v.tensor_copy(m.gatew[:, k, 2 * D:3 * D], m.bank[3 + 2 * k][:, 0:D]).then_inc(kept, 1)


def node_tables(nc, m, tag, H, gate=None):
    W = D + 2 * H
    with Stage(nc) as c:
        def sb(n, s):
            return c.enter_context(nc.sbuf_tensor(tag + n, s, F32))

        def sem(n):
            return c.sem(tag + n)

        shift = sb("_shift", [P, NT])
        xn = sb("_xn", [P, 2, D])
        xst = sb("_xst", [128, 2, KD, P])
        chain, normed, turned, staged, xn_used = sem("_chain"), sem("_normed"), sem("_turned"), sem("_staged"), sem("_xn_used")
        rowed, row_kept, ts_free, stored, chain2 = sem("_rowed"), sem("_row_kept"), sem("_ts_free"), sem("_stored"), sem("_chain2")
        with nc.Block() as block:
            @block.vector
            def _(v):
                v.sem_inc(row_kept, 2)
                v.scalar_tensor_tensor(shift[:, :], m.mean[:, :], -1.0, m.rstd[:, :], ALU.mult, ALU.mult).then_inc(chain, 1)
                v.wait_ge(chain, 1)

                def norm(t, s):
                    v.wait_ge(xn_used, t + 1)
                    v.tensor_scalar(xn[:, s, :], m.xs[:, bass.ds(t, 1), :].rearrange("p a d -> p (a d)"),
                                    m.rstd[:, bass.ds(t, 1)], shift[:, bass.ds(t, 1)], ALU.mult, ALU.add).then_inc(normed, 1)
                    if gate is None:
                        v.wait_ge(normed, t + 1)
                        x_t = m.xs[:, bass.ds(t, 1), :].rearrange("p a d -> p (a d)")
                        v.tensor_tensor(x_t, x_t, xn[:, s, :], ALU.add).then_inc(chain2, 1)

                def keep(t, s):
                    v.wait_ge(rowed, t + 1)
                    v.tensor_copy(m.acc[:, bass.ds(t, 1), 0:W].rearrange("p a d -> p (a d)"),
                                  m.bank[2 + s][0:P, 0:W]).then_inc(row_kept, 1)

                norm(0, 0)
                with v.Fori(0, NT // 2) as b:
                    norm(b * 2 + 1, 1)
                    keep(b * 2, 0)
                    norm(b * 2 + 2, 0)
                    keep(b * 2 + 1, 1)
                keep(NT - 1, 0)

            @block.scalar
            def _(a):
                a.sem_inc(staged, 2)

                def stage(t, s):
                    a.wait_ge(turned, t + 1)
                    a.wait_ge(ts_free, t + 1)
                    turn = m.bank[s][:, 0:256].rearrange("p (k n) -> p k n", k=KD)[:, :, 0:P]
                    a.activation(xst[:, s, :, :], turn, ACT.Copy)
                    a.activation(m.xT[:, :, tile_cols(t)], turn, ACT.Copy).then_inc(staged, 1)

                over_tiles(a, stage)

            @block.tensor
            def _(pe):
                pe.sem_inc(xn_used, 2)
                pe.sem_inc(ts_free, 2)

                def turn(t, s):
                    pe.wait_ge(normed, t + 1)
                    pe.wait_ge(staged, t + 1)
                    for k in range(KD):
                        ins = pe.transpose(m.bank[s][:, k * 128:k * 128 + P], xn[:, s, k * 128:(k + 1) * 128],
                                           m.ident[0:P, 0:P])
                    ins.then_inc(turned, 1)
                    pe.wait_ge(turned, t + 1)
                    pe.sem_inc(xn_used, 1)

                def rows(t, s):
                    pe.wait_ge(staged, t + 3)
                    pe.wait_ge(row_kept, t + 1)
                    for k in range(KD):
                        ins = pe.matmul(m.bank[2 + s][0:P, 0:W], xst[:, s, k, :], m.nodew[:, k, 0:W],
                                        start=(k == 0), stop=(k == KD - 1))
                    ins.then_inc(rowed, 1)
                    pe.wait_ge(rowed, t + 1)
                    pe.sem_inc(ts_free, 1)

                turn(0, 0)
                with pe.Fori(0, NT // 2) as b:
                    turn(b * 2 + 1, 1)
                    rows(b * 2, 0)
                    turn(b * 2 + 2, 0)
                    rows(b * 2 + 1, 1)
                rows(NT - 1, 0)

            @block.sync
            def _(sp):
                sp.wait_ge(row_kept, NT + 2)
                sp.dma_start(m.table[H].rearrange("(t p) w -> p t w", p=P), m.acc[:, :, 0:W]).then_inc(stored, 16)
                sp.wait_ge(stored, 16)


def score_bounds(nc, m, tag, H):
    with Stage(nc) as c:
        def sb(n, s):
            return c.enter_context(nc.sbuf_tensor(tag + n, s, F32))

        def sem(n):
            return c.sem(tag + n)

        top = sb("_top", [P, H])
        gmax = sb("_gmax", [P, H])
        z = sb("_z", [P, NT, H])
        es = sb("_es", [P, NT, H])
        chain, topped, maxed, zed, exped, scaled = sem("_chain"), sem("_topped"), sem("_maxed"), sem("_zed"), sem("_exped"), sem("_scaled")
        asrc, adst = m.acc[:, :, D:D + H], m.acc[:, :, D + H:D + 2 * H]
        adm_a = m.adm[:, :, 0:H]
        adm_m = m.adm[:, :, H:2 * H]
        gb = gmax[:, :].unsqueeze(1).to_broadcast([P, NT, H])
        with nc.Block() as block:
            @block.vector
            def _(v):
                k = Chain(v, chain, 0)
                v.tensor_reduce(top[:, :], asrc.rearrange("p t h -> p h t"), AX.X, ALU.max).then_inc(topped, 1)
                k.link(v.tensor_copy(adm_a, adst))
                v.wait_ge(maxed, 1)
                k.link(v.tensor_tensor(adm_m, adm_a, gb, ALU.add))
                k.link(v.tensor_scalar(z[:, :, :], adm_m, SLOPE, None, ALU.mult))
                k.link(v.tensor_tensor(adm_m, adm_m, z[:, :, :], ALU.max))
                if H == 1:
                    k.link(v.tensor_tensor(z[:, :, :], asrc, adst, ALU.add))
                    k.link(v.tensor_scalar(es[:, :, :], z[:, :, :], SLOPE, None, ALU.mult))
                    k.link(v.tensor_tensor(z[:, :, :], z[:, :, :], es[:, :, :], ALU.max))
                    v.tensor_tensor(z[:, :, :], z[:, :, :], adm_m, ALU.subtract).then_inc(zed, 1)
                    v.wait_ge(exped, 1)
                    k.link(v.tensor_copy(m.acc[:, :, D:D + 1], es[:, :, :]))
                    with v.Fori(0, NT // 5) as b:
                        for u in range(5):
                            t = b * 5 + u
                            row = m.acc[:, bass.ds(t, 1), 0:D].rearrange("p a d -> p (a d)")
                            v.tensor_scalar(row, row, es[:, bass.ds(t, 1), :].rearrange("p a h -> p (a h)"),
                                            None, ALU.mult).then_inc(scaled, 1)
                else:
                    k.link(v.memset(m.acc[:, :, :], 0.0))

            @block.scalar
            def _(a):
                if H == 1:
                    a.wait_ge(zed, 1)
                    a.activation(es[:, :, :], z[:, :, :], ACT.Exp).then_inc(exped, 1)

            @block.gpsimd
            def _(pool):
                pool.wait_ge(topped, 1)
                pool.partition_all_reduce(gmax[:, :], top[:, :], P, MAX).then_inc(maxed, 1)


def edge_sums(nc, m, tag, H, load_edges):
    W = D + 2 * H
    PW = 2 * WIN
    NP = NG // 2
    NT4 = NP // 4
    with Stage(nc) as c:
        def sb(n, s, d=F32):
            return c.enter_context(nc.sbuf_tensor(tag + n, s, d))

        def sem(n):
            return c.sem(tag + n)

        idx = sb("_idx", [128, 4, PW], I32)
        rows = sb("_rows", [128, 4, PW, W])
        one = sb("_one", [128, 4, PW, P])
        oneT = sb("_oneT", [P, 2, PW * 128])
        stage = sb("_stage", [P, 4, 2, 2 * H])
        msg = sb("_msg", [128, 4, PW, D + H])
        z = sb("_z", [128, 2, PW, H])
        y = sb("_y", [128, 2, PW, H])
        edges_in = [sem(f"_edges_in{s}") for s in range(8)]
        gathered = [sem(f"_gathered{r}") for r in range(4)]
        staged, turned, kept, scored, zed, exped = sem("_staged"), sem("_turned"), sem("_kept"), sem("_scored"), sem("_zed"), sem("_exped")
        msged, summed, added, chain, go = sem("_msged"), sem("_summed"), sem("_added"), sem("_chain"), sem("_go")
        turn_bank, score_bank, sum_banks = m.bank[0], m.bank[1], m.bank[2:4]
        scores_of = score_bank[:, 0:PW * 2 * H].rearrange("p (w x) -> p w x", w=PW)

        def valid(q):
            return not isinstance(q, int) or 0 <= q < NP

        def wait(eng, sem, value):
            if not isinstance(value, int) or value > 0:
                eng.wait_ge(sem, value)

        def rounds(eng, body):
            for u in range(4):
                body(0, u)
            with eng.Fori(1, NT4) as b:
                for u in range(4):
                    body(b, u)
            for u in range(3):
                body(NT4, u)

        with nc.Block() as block:
            if load_edges:
                @block.sync
                def _(sp):
                    with sp.Fori(0, NG // 8) as b:
                        _, e0 = nc.values_load_multi_w_load_instructions(m.gtab[0:1, 1, bass.ds(b * 8, 8)], engines=[sp.engine],
                                                                         min_val=0, max_val=E)
                        for s in range(8):
                            sp.wait_ge(edges_in[s], b * 16)
                            sp.dma_start(m.eall[:, bass.ds((b * 8 + s) * 4, 4)],
                                         m.edges[bass.ds(e0[s], GE), :].rearrange("(p w) x -> p (w x)", w=WIN)).then_inc(edges_in[s], 16)
                    for s in range(8):
                        sp.wait_ge(edges_in[s], 16 * (NG // 8))

            @block.gpsimd
            def _(pool):
                with pool.Fori(0, NT4) as b:
                    for r in range(4):
                        q = b * 4 + r
                        pool.wait_ge(staged, q + 1)
                        pool.wait_ge(msged, q + 1)
                        pool.sem_inc(go, 1)
                        for w in range(PW):
                            pool.indirect_dma_start(rows[:, r, w, :], None, m.table[H],
                                                    bass.IndirectOffsetOnAxis(ap=idx[:, r, w:w + 1], axis=0)).then_inc(gathered[r], 16)

            @block.tensor
            def _(pe):
                def body(b, u):
                    q = b * 4 + u
                    if valid(q):
                        pe.wait_ge(staged, q + 1)
                        wait(pe, kept, q)
                        for w in range(PW):
                            ins = pe.transpose(turn_bank[0:P, w * 128:(w + 1) * 128], one[:, u, w, :], m.ident[:, :])
                        ins.then_inc(turned, 1)
                    q2, r2 = q - 2, (u - 2) % 4
                    if valid(q2):
                        pe.wait_ge(msged, q2 + 5)
                        wait(pe, added, q2 * 2)
                        for w in range(PW):
                            ins = pe.matmul(sum_banks[w // WIN][0:P, 0:D + H], one[:, r2, w, :], msg[:, r2, w, :],
                                            start=(w % WIN == 0), stop=(w % WIN == WIN - 1))
                        ins.then_inc(summed, 1)
                    if valid(q):
                        pe.wait_ge(kept, q + 1)
                        wait(pe, zed, q)
                        for w in range(PW):
                            ins = pe.matmul(scores_of[:, w, :], oneT[:, u % 2, w * 128:(w + 1) * 128],
                                            stage[:, u, w // WIN, :], start=True, stop=True)
                        ins.then_inc(scored, 1)

                rounds(pe, body)

            @block.scalar
            def _(a):
                def body(b, u):
                    q = b * 4 + u
                    if valid(q):
                        a.wait_ge(turned, q + 1)
                        wait(a, scored, q - 1)
                        a.activation(oneT[:, u % 2, :], turn_bank[0:P, 0:PW * 128], ACT.Copy).then_inc(kept, 1)
                    q2, r2 = q - 2, (u - 2) % 4
                    if valid(q2):
                        a.wait_ge(zed, q2 + 1)
                        a.activation(msg[:, r2, :, D:D + H], z[:, r2 % 2, :, :], ACT.Exp).then_inc(exped, 1)

                rounds(a, body)

            @block.vector
            def _(v):
                v.sem_inc(msged, 4)

                def body(b, u):
                    q = b * 4 + u
                    if isinstance(b, int):
                        lo, hi = (0, 8) if b == 0 else (b * 8 - 6, NG)
                        at = lo
                    else:
                        lo, hi, at = -6, 8, b * 8 - 6
                    if u == 0:
                        _, regs = nc.values_load_multi_w_load_instructions(
                            m.gtab[0:1, 0, bass.ds(at, hi - lo)], engines=[v.engine], min_val=0, max_val=NT - 1)
                        v_tiles.clear()
                        first = lo - b * 8 if isinstance(b, int) else lo
                        for n, reg in enumerate(regs):
                            v_tiles[first + n] = reg
                    if valid(q):
                        for i in range(2):
                            g, tile = q * 2 + i, v_tiles[2 * u + i]
                            if load_edges:
                                v.wait_ge(edges_in[2 * u + i], b * 16 + 16)
                            v.tensor_copy(idx[:, u, 2 * i:2 * i + 2],
                                          m.eall[:, bass.ds(g * 4, 4)].rearrange("p (w x) -> p w x", x=2)[:, :, 0])
                            for w in range(WIN):
                                v.tensor_scalar(one[:, u, 2 * i + w, :], m.nodes[:, bass.ds(tile * P, P)],
                                                m.eall[:, bass.ds(g * 4 + 2 * w + 1, 1)], None, ALU.is_equal)
                            ins = v.tensor_copy(stage[:, u, i, :], m.adm[:, bass.ds(tile, 1), 0:2 * H].rearrange("p a x -> p (a x)"))
                        ins.then_inc(staged, 1)
                    q2, r2 = q - 2, (u - 2) % 4
                    b2 = b if u >= 2 else b - 1
                    if valid(q2):
                        zq, yq = z[:, r2 % 2, :, :], y[:, r2 % 2, :, :]
                        v.wait_ge(scored, q2 + 1)
                        v.wait_ge(gathered[r2], b2 * 16 * PW + 16 * PW)
                        v.tensor_tensor(zq, rows[:, r2, :, D:D + H], scores_of[:, :, 0:H], ALU.add).then_inc(chain, 1)
                        v.wait_ge(chain, q2 * 3 + 1)
                        v.scalar_tensor_tensor(yq, zq, SLOPE, zq, ALU.mult, ALU.max).then_inc(chain, 1)
                        v.wait_ge(chain, q2 * 3 + 2)
                        v.tensor_tensor(zq, yq, scores_of[:, :, H:2 * H], ALU.subtract).then_inc(chain, 1)
                        v.wait_ge(chain, q2 * 3 + 3)
                        v.tensor_scalar(zq, zq, 0.0, None, ALU.min).then_inc(zed, 1)
                    q3, u3 = q - 3, u - 3
                    if valid(q3):
                        for i in range(2):
                            tile = v_tiles[2 * u3 + i]
                            v.wait_ge(summed, q3 + 1)
                            wait(v, added, q3 * 2 + i)
                            acc = m.acc[:, bass.ds(tile, 1), 0:D + H].rearrange("p a x -> p (a x)")
                            v.tensor_tensor(acc, acc, sum_banks[i][0:P, 0:D + H], ALU.add).then_inc(added, 1)
                    if valid(q2):
                        v.wait_ge(exped, q2 + 1)
                        for w in range(PW):
                            ins = v.tensor_tensor(msg[:, r2, w, 0:D].rearrange("p (h x) -> p h x", h=H),
                                                  rows[:, r2, w, 0:D].rearrange("p (h x) -> p h x", h=H),
                                                  msg[:, r2, w, D:D + H].unsqueeze(2).to_broadcast([128, H, D // H]), ALU.mult)
                        ins.then_inc(msged, 1)

                v_tiles = {}
                rounds(v, body)
                v.wait_ge(added, 2 * NP)


def graph_attention0(nc, m):
    with Stage(nc) as c:
        def sb(n, s):
            return c.enter_context(nc.sbuf_tensor("cell_" + n, s, F32))

        def sem(n):
            return c.sem("cell_" + n)

        rden = sb("rden", [P, NT])
        hb = sb("hb", [P, 2, D])
        hbT = sb("hbT", [128, 2, KD, P])
        gio = sb("gio", [P, 2, 2 * D])
        gg = sb("gg", [P, 2, D])
        cc = sb("cc", [P, 2, D])
        tc = sb("tc", [P, 2, D])
        inv, agged, tanhed, turned, kept, gated, acted = sem("inv"), sem("agged"), sem("tanhed"), sem("turned"), sem("kept"), sem("gated"), sem("acted")
        celled, ctanhed, hid, addd = sem("celled"), sem("ctanhed"), sem("hid"), sem("addd")
        with nc.Block() as block:
            @block.vector
            def _(v):
                v.reciprocal(rden[:, :], m.acc[:, :, D]).then_inc(inv, 1)
                v.wait_ge(inv, 1)

                def step(t, s):
                    if not isinstance(t, int) or t >= 2:
                        v.wait_ge(tanhed, t * 1)
                    v.scalar_tensor_tensor(hb[:, s, :], m.acc[:, bass.ds(t, 1), 0:D].rearrange("p a d -> p (a d)"),
                                           rden[:, bass.ds(t, 1)], m.gbias[:, :], ALU.mult, ALU.add).then_inc(agged, 1)
                    v.wait_ge(acted, t + 1)
                    v.tensor_tensor(cc[:, s, :], gio[:, s, 0:D], gg[:, s, :], ALU.mult).then_inc(celled, 1)
                    v.wait_ge(ctanhed, t + 1)
                    v.tensor_tensor(cc[:, s, :], gio[:, s, D:2 * D], tc[:, s, :], ALU.mult).then_inc(hid, 1)
                    v.wait_ge(hid, t + 1)
                    x = m.xs[:, bass.ds(t, 1), :].rearrange("p a d -> p (a d)")
                    v.tensor_tensor(x, x, cc[:, s, :], ALU.add).then_inc(addd, 1)

                over_tiles(v, step)

            @block.scalar
            def _(a):
                def step(t, s):
                    a.wait_ge(agged, t + 1)
                    a.activation(hb[:, s, :], hb[:, s, :], ACT.Tanh).then_inc(tanhed, 1)
                    a.wait_ge(turned, t + 1)
                    a.activation(hbT[:, s, :, :], m.bank[s][:, 0:256].rearrange("p (k n) -> p k n", k=KD)[:, :, 0:P],
                                 ACT.Copy).then_inc(kept, 1)
                    a.wait_ge(gated, t + 1)
                    a.activation(gio[:, s, :], m.bank[2 + 2 * s][0:P, 0:2 * D], ACT.Sigmoid)
                    a.activation(gg[:, s, :], m.bank[3 + 2 * s][0:P, 0:D], ACT.Tanh).then_inc(acted, 1)
                    a.wait_ge(celled, t + 1)
                    a.activation(tc[:, s, :], cc[:, s, :], ACT.Tanh).then_inc(ctanhed, 1)

                over_tiles(a, step)

            @block.tensor
            def _(pe):
                def step(t, s):
                    pe.wait_ge(tanhed, t + 1)
                    for k in range(KD):
                        ins = pe.transpose(m.bank[s][:, k * 128:k * 128 + P], hb[:, s, k * 128:(k + 1) * 128], m.ident[0:P, 0:P])
                    ins.then_inc(turned, 1)
                    pe.wait_ge(kept, t + 1)
                    for k in range(KD):
                        pe.matmul(m.bank[2 + 2 * s][0:P, 0:2 * D], hbT[:, s, k, :], m.gatew[:, k, 0:2 * D], start=(k == 0), stop=(k == KD - 1))
                    for k in range(KD):
                        ins = pe.matmul(m.bank[3 + 2 * s][0:P, 0:D], hbT[:, s, k, :], m.gatew[:, k, 2 * D:3 * D], start=(k == 0), stop=(k == KD - 1))
                    ins.then_inc(gated, 1)

                over_tiles(pe, step)


def valid(t):
    return not isinstance(t, int) or 0 <= t < NT


def pipelined(eng, body, lag):
    first = max(1, lag)
    for t in range(2 * first):
        body(t, t % 2)
    with eng.Fori(first, NT // 2) as b:
        body(b * 2, 0)
        body(b * 2 + 1, 1)
    for t in range(NT - 1, NT + lag):
        body(t, t % 2)


def wait_count(eng, sem, value):
    if not isinstance(value, int) or value > 0:
        eng.wait_ge(sem, value)


def row_of(t3, t):
    return t3[:, bass.ds(t, 1), :].rearrange("p a d -> p (a d)")


def by_feature(bank):
    return bank[:, 0:KD * 128].rearrange("p (k n) -> p k n", k=KD)[:, :, 0:P]


def mix0_keys(nc, m):
    G = 2 * HEADS
    with Stage(nc) as c:
        def sb(n, s):
            return c.enter_context(nc.sbuf_tensor("keys_" + n, s, F32))

        def sem(n):
            return c.sem("keys_" + n)

        xst = sb("xst", [128, 2, KD, P])
        kv = sb("kv", [P, 2, 2 * D])
        sq = sb("sq", [P, 2, 2 * D])
        mu = sb("mu", [P, 2, G])
        var = sb("var", [P, 2, G])
        rs = sb("rs", [P, 2, G])
        zeros = sb("zeros", [P, 128])
        xstaged, made, chain, squared, varred, powered, normed, summed, zeroed, done = [
            sem(n) for n in ("staged", "made", "chain", "squared", "varred", "powered", "normed", "summed", "zeroed", "done")]
        norm_chain, kept = sem("norm_chain"), sem("kept")
        with nc.Block() as block:
            @block.scalar
            def _(a):
                def body(t, s):
                    if valid(t):
                        wait_count(a, made, t - 1)
                        a.activation(xst[:, s, :, :], m.xT[:, :, tile_cols(t)], ACT.Copy).then_inc(xstaged, 1)
                    if valid(t - 1):
                        a.wait_ge(chain, (t - 1) * 4 + 4)
                        a.activation(sq[:, 1 - s, :], kv[:, 1 - s, :], ACT.Square).then_inc(squared, 1)

                pipelined(a, body, 1)

            @block.tensor
            def _(pe):
                pe.wait_ge(zeroed, 1)
                pe.matmul(m.bank[2][:, 0:D], zeros[:, :], zeros[:, :].unsqueeze(1).to_broadcast([P, KD, 128]), start=True, stop=False)

                def body(t, s):
                    if valid(t):
                        pe.wait_ge(xstaged, t + 1)
                        wait_count(pe, chain, (t - 2) * 4 + 1)
                        for k in range(KD):
                            ins = pe.matmul(m.bank[s][0:P, :], xst[:, s, k, :], m.wkv[:, k, :], start=(k == 0), stop=(k == KD - 1))
                        ins.then_inc(made, 1)
                    if valid(t - 1):
                        pe.wait_ge(normed, t)
                        for k in range(KD):
                            ins = pe.matmul(m.bank[2][:, k * 128:(k + 1) * 128], kv[:, 1 - s, k * 128:(k + 1) * 128],
                                            kv[:, 1 - s, D + k * 128:D + (k + 1) * 128], start=False, stop=False, skip_group_check=True)
                        ins.then_inc(summed, 1)

                pipelined(pe, body, 1)
                pe.matmul(m.bank[2][:, 0:D], zeros[:, :], zeros[:, :].unsqueeze(1).to_broadcast([P, KD, 128]),
                          start=False, stop=True).then_inc(summed, 1)

            @block.gpsimd
            def _(pool):
                def body(t, s):
                    pool.wait_ge(varred, t + 1)
                    pool.tensor_tensor(rs[:, s, :], var[:, s, :], m.half[0:P, 0:G], ALU.pow).then_inc(powered, 1)

                pipelined(pool, body, 0)

            @block.vector
            def _(v):
                v.memset(zeros[:, :], 0.0).then_inc(zeroed, 1)

                def grouped(x):
                    return x.rearrange("p (g c) -> p g c", c=HC)

                def spread(x):
                    return x.unsqueeze(2).to_broadcast([P, G, HC])

                k = Chain(v, chain, 4)

                def body(t, s):
                    if valid(t - 1):
                        v.wait_ge(squared, t)
                        v.tensor_reduce(mu[:, 1 - s, :], grouped(sq[:, 1 - s, :]), AX.X, ALU.add).then_inc(done, 1)
                        v.wait_ge(done, t)
                        v.tensor_scalar(var[:, 1 - s, :], mu[:, 1 - s, :], 1.0 / HC, EPS, ALU.mult, ALU.add).then_inc(varred, 1)
                    if valid(t):
                        k.step(t)
                        v.wait_ge(made, t + 1)
                        wait_count(v, summed, t - 1)
                        k.link(v.tensor_tensor(kv[:, s, :], m.bank[s][0:P, :], m.bkv[:, :], ALU.add))
                        k.link(v.tensor_reduce(mu[:, s, :], grouped(kv[:, s, :]), AX.X, ALU.add))
                        k.link(v.tensor_scalar(mu[:, s, :], mu[:, s, :], 1.0 / HC, None, ALU.mult))
                        k.link(v.tensor_tensor(grouped(kv[:, s, :]), grouped(kv[:, s, :]), spread(mu[:, s, :]), ALU.subtract))
                        k.close()
                    if valid(t - 1):
                        o = 1 - s
                        v.wait_ge(powered, t)
                        v.tensor_tensor(grouped(kv[:, o, :]), grouped(kv[:, o, :]), spread(rs[:, o, :]), ALU.mult).then_inc(norm_chain, 1)
                        v.wait_ge(norm_chain, t * 2 - 1)
                        v.tensor_tensor(kv[:, o, :], kv[:, o, :], m.lng[:, :], ALU.mult).then_inc(norm_chain, 1)
                        v.wait_ge(norm_chain, t * 2)
                        v.tensor_tensor(kv[:, o, :], kv[:, o, :], m.lnb[:, :], ALU.add).then_inc(normed, 1)

                pipelined(v, body, 1)
                v.wait_ge(summed, NT + 1)
                v.tensor_scalar(m.kv[:, :, :].rearrange("p k n -> p (k n)"), m.bank[2][:, 0:D], 1.0 / N, None, ALU.mult).then_inc(kept, 1)
                v.wait_ge(kept, 1)
                v.tensor_tensor(m.kv[:, :, :], m.kv[:, :, :], m.headmask[:, :].unsqueeze(1).to_broadcast([128, KD, 128]), ALU.mult)


def mix0_queries(nc, m):
    with Stage(nc) as c:
        def sb(n, s):
            return c.enter_context(nc.sbuf_tensor("query_" + n, s, F32))

        def sem(n):
            return c.sem("query_" + n)

        qT = sb("qT", [128, 2, KD, P])
        ret = sb("ret", [128, 2, KD, P])
        queried, qkept, mixed, returned, hidden, hkept = [sem(n) for n in ("queried", "qkept", "mixed", "returned", "hidden", "hkept")]
        with nc.Block() as block:
            @block.tensor
            def _(pe):
                def body(t, s):
                    if valid(t):
                        wait_count(pe, qkept, t - 1)
                        for o in range(KD):
                            for k in range(KD):
                                ins = pe.matmul(m.bank[s][:, o * 128:o * 128 + P], m.wq[:, k, o * 128:(o + 1) * 128],
                                                m.xT[:, k, tile_cols(t)], start=(k == 0), stop=(k == KD - 1))
                        ins.then_inc(queried, 1)
                    if valid(t - 1):
                        pe.wait_ge(qkept, t)
                        wait_count(pe, returned, t - 2)
                        for k in range(KD):
                            ins = pe.matmul(m.bank[3 - s][:, k * 128:k * 128 + P], m.kv[:, k, :], qT[:, 1 - s, k, :], start=True, stop=True)
                        ins.then_inc(mixed, 1)
                    if valid(t - 2):
                        pe.wait_ge(returned, t - 1)
                        wait_count(pe, hkept, t - 3)
                        for o in range(KD):
                            for k in range(KD):
                                ins = pe.matmul(m.bank[4 + s][:, o * 128:o * 128 + P], m.w1[:, k, o * 128:(o + 1) * 128],
                                                ret[:, s, k, :], start=(k == 0), stop=(k == KD - 1))
                        ins.then_inc(hidden, 1)

                pipelined(pe, body, 2)

            @block.scalar
            def _(a):
                def body(t, s):
                    if valid(t):
                        a.wait_ge(queried, t + 1)
                        wait_count(a, mixed, t - 1)
                        for k in range(KD):
                            ins = a.activation(qT[:, s, k, :], m.bank[s][:, k * 128:k * 128 + P], ACT.Identity, bias=m.bq[:, k:k + 1])
                        ins.then_inc(qkept, 1)
                    if valid(t - 2):
                        a.wait_ge(hidden, t - 1)
                        a.activation(m.xT[:, :, tile_cols(t - 2)], by_feature(m.bank[4 + s]), ACT.Copy).then_inc(hkept, 1)

                pipelined(a, body, 2)

            @block.vector
            def _(v):
                def body(t, s):
                    v.wait_ge(mixed, t + 1)
                    wait_count(v, hidden, t - 1)
                    v.tensor_tensor(ret[:, s, :, :], by_feature(m.bank[2 + s]), m.xT[:, :, tile_cols(t)], ALU.add).then_inc(returned, 1)

                pipelined(v, body, 0)


def mix0_out(nc, m):
    with Stage(nc) as c:
        def sb(n, s):
            return c.enter_context(nc.sbuf_tensor("mixout_" + n, s, F32))

        def sem(n):
            return c.sem("mixout_" + n)

        hT = sb("hT", [128, 2, KD, P])
        bent, made, biased, added = [sem(n) for n in ("bent", "made", "biased", "added")]
        with nc.Block() as block:
            @block.scalar
            def _(a):
                def body(t, s):
                    wait_count(a, made, t - 1)
                    for k in range(KD):
                        ins = a.activation(hT[:, s, k, :], m.xT[:, k, tile_cols(t)], ACT.Gelu, bias=m.b1[:, k:k + 1])
                    ins.then_inc(bent, 1)

                pipelined(a, body, 0)

            @block.tensor
            def _(pe):
                def body(t, s):
                    pe.wait_ge(bent, t + 1)
                    wait_count(pe, added, t - 1)
                    for k in range(KD):
                        ins = pe.matmul(m.bank[s][0:P, 0:D], hT[:, s, k, :], m.w2[:, k, :], start=(k == 0), stop=(k == KD - 1))
                    ins.then_inc(made, 1)

                pipelined(pe, body, 0)

            @block.vector
            def _(v):
                def body(t, s):
                    x = row_of(m.xs, t)
                    v.tensor_tensor(x, x, m.b2[:, :], ALU.add).then_inc(biased, 1)
                    v.wait_ge(biased, t + 1)
                    v.wait_ge(made, t + 1)
                    v.tensor_tensor(x, x, m.bank[s][0:P, 0:D], ALU.add).then_inc(added, 1)

                pipelined(v, body, 0)


def experts_route(nc, m, tag, gw, gb, weighted):
    with Stage(nc) as c:
        def sb(n, s, d=F32):
            return c.enter_context(nc.sbuf_tensor(tag + n, s, d))

        def sem(n):
            return c.sem(tag + n)

        gws = sb("_gws", [128, KD, NE])
        gbs = sb("_gbs", [P, NE])
        shift = sb("_shift", [P, NT])
        xn = sb("_xn", [P, 2, D])
        xst = sb("_xst", [128, 2, KD, P])
        lg = sb("_lg", [P, NT, NE])
        ie = sb("_ie", [128, NE])
        jn = sb("_jn", [128, 1])
        loaded, chain, normed, turned, staged, logged, kept, numbered, copied = [
            sem(n) for n in ("_loaded", "_chain", "_normed", "_turned", "_staged", "_logged", "_kept", "_numbered", "_copied")]
        with nc.Block() as block:
            @block.sync
            def _(sp):
                sp.dma_start(gws[:, :, :], gw.rearrange("(k p) e -> p k e", p=128)).then_inc(loaded, 16)
                sp.dma_start(gbs[:, :], gb.partition_broadcast(P)).then_inc(loaded, 16)

            @block.gpsimd
            def _(pool):
                pool.iota(ie[:, :], pattern=[[1, NE]], base=0, channel_multiplier=0,
                          allow_small_or_imprecise_dtypes=True).then_inc(numbered, 1)
                pool.iota(jn[:, :], pattern=[[0, 1]], base=0, channel_multiplier=1,
                          allow_small_or_imprecise_dtypes=True).then_inc(numbered, 1)

                def body(t, s):
                    pool.wait_ge(normed, t + 1)
                    pool.tensor_copy(m.acc[:, bass.ds(t, 1), 0:D].rearrange("p a d -> p (a d)"), xn[:, s, :]).then_inc(copied, 1)

                pipelined(pool, body, 0)

            @block.vector
            def _(v):
                v.scalar_tensor_tensor(shift[:, :], m.mean[:, :], -1.0, m.rstd[:, :], ALU.mult, ALU.mult).then_inc(chain, 1)
                v.wait_ge(chain, 1)
                v.wait_ge(loaded, 32)

                def body(t, s):
                    if valid(t):
                        wait_count(v, turned, t - 1)
                        wait_count(v, copied, t - 1)
                        v.tensor_scalar(xn[:, s, :], row_of(m.xs, t), m.rstd[:, bass.ds(t, 1)], shift[:, bass.ds(t, 1)],
                                        ALU.mult, ALU.add).then_inc(normed, 1)
                    if valid(t - 1):
                        v.wait_ge(logged, t)
                        v.tensor_tensor(row_of(lg, t - 1), m.bank[3 - s][0:P, 0:NE], gbs[:, :], ALU.add).then_inc(kept, 1)

                pipelined(v, body, 1)

            @block.tensor
            def _(pe):
                pe.wait_ge(loaded, 32)

                def body(t, s):
                    if valid(t):
                        pe.wait_ge(normed, t + 1)
                        wait_count(pe, staged, t - 1)
                        for k in range(KD):
                            ins = pe.transpose(m.bank[s][:, k * 128:k * 128 + P], xn[:, s, k * 128:(k + 1) * 128], m.ident[0:P, 0:P])
                        ins.then_inc(turned, 1)
                    if valid(t - 1):
                        pe.wait_ge(staged, t)
                        wait_count(pe, kept, t - 2)
                        for k in range(KD):
                            ins = pe.matmul(m.bank[3 - s][0:P, 0:NE], xst[:, 1 - s, k, :], gws[:, k, :], start=(k == 0), stop=(k == KD - 1))
                        ins.then_inc(logged, 1)

                pipelined(pe, body, 1)

            @block.scalar
            def _(a):
                def body(t, s):
                    a.wait_ge(turned, t + 1)
                    wait_count(a, logged, t - 1)
                    a.activation(xst[:, s, :, :], by_feature(m.bank[s]), ACT.Copy).then_inc(staged, 1)

                pipelined(a, body, 0)

        one = [sb(f"_one{i}", [P, NT, NE]) for i in range(2)]
        eq = sb("_eq", [P, NT, NE])
        mask = sb("_mask", [P, NT, NE])
        best = sb("_best", [P, 2, NT])
        low = sb("_low", [P, NT])
        ex = sb("_ex", [P, NT, NE])
        e2 = sb("_e2", [P, NT])
        zsum = sb("_zsum", [P, NT])
        tot = sb("_tot", [128, NT, NE])
        incl = sb("_incl", [128, NE, NT])
        excl = sb("_excl", [128, NT, NE])
        zero = sb("_zero", [128, NT])
        placef = sb("_placef", [P, 2, NT])
        nbi = sb("_nbi", [128, NE], I32)
        nb = sb("_nb", [128, NE])
        bend = sb("_bend", [128, NE])
        past = sb("_past", [128, NE])
        bt = sb("_bt", [128, 1])
        masked, exped, counted, tabled, turned2, c2 = [sem(n) for n in ("_masked", "_exped", "_counted", "_tabled", "_turned2", "_chain2")]

        def over(x):
            return x.unsqueeze(2).to_broadcast([P, NT, NE])

        with nc.Block() as block:
            @block.vector
            def _(v):
                k = Chain(v, c2, 0)
                src = lg
                for i in range(2):
                    k.link(v.tensor_reduce(best[:, i, :], src[:, :, :], AX.X, ALU.max))
                    k.link(v.tensor_tensor(eq[:, :, :], src[:, :, :], over(best[:, i, :]), ALU.is_equal))
                    k.link(v.tensor_scalar(eq[:, :, :], eq[:, :, :], -100.0, None, ALU.mult))
                    k.link(v.tensor_tensor(eq[:, :, :], eq[:, :, :], ie[0:P, :].unsqueeze(1).to_broadcast([P, NT, NE]), ALU.add))
                    k.link(v.tensor_reduce(low[:, :], eq[:, :, :], AX.X, ALU.min))
                    k.link(v.tensor_tensor(one[i][:, :, :], eq[:, :, :], over(low[:, :]), ALU.is_equal))
                    if i == 0:
                        k.link(v.scalar_tensor_tensor(mask[:, :, :], one[0][:, :, :], -BIG, lg[:, :, :], ALU.mult, ALU.add))
                        src = mask
                k.link(v.tensor_tensor(mask[:, :, :], one[0][:, :, :], one[1][:, :, :], ALU.add))
                if weighted:
                    k.link(v.tensor_tensor(ex[:, :, :], lg[:, :, :], over(best[:, 0, :]), ALU.subtract))
                    k.link(v.tensor_tensor(e2[:, :], best[:, 1, :], best[:, 0, :], ALU.subtract))
                v.sem_inc(masked, 1)
                if weighted:
                    v.wait_ge(exped, 2)
                    k.link(v.tensor_reduce(zsum[:, :], ex[:, :, :], AX.X, ALU.add))
                    k.link(v.reciprocal(m.cw[:, 0, :], zsum[:, :]))
                    k.link(v.tensor_tensor(m.cw[:, 1, :], m.cw[:, 0, :], e2[:, :], ALU.mult))
                k.link(v.memset(zero[:, :], 0.0))
                v.wait_ge(counted, 1)
                k.link(v.tensor_copy(tot[:, :, :].rearrange("p t e -> p (t e)"), m.bank[1][:, 0:NT * NE]))
                for e in range(NE):
                    k.link(v.tensor_tensor_scan(incl[:, e, :], tot[:, :, e], zero[:, :], 0.0, ALU.add, ALU.add))
                k.link(v.tensor_tensor(excl[:, :, :], incl[:, :, :].rearrange("p e t -> p t e"), tot[:, :, :], ALU.subtract))
                k.link(v.tensor_scalar(nbi[:, :], incl[:, :, NT - 1], float(ROWS - 1), None, ALU.add))
                k.link(v.tensor_scalar(nbi[:, :], nbi[:, :], 8, None, ALU.arith_shift_right))
                k.link(v.tensor_copy(nb[:, :], nbi[:, :]))
                k.link(v.tensor_tensor_scan(bend[:, :], nb[:, :], zero[:, 0:NE], 0.0, ALU.add, ALU.add))
                k.link(v.tensor_tensor(past[:, :], bend[:, :], nb[:, :], ALU.subtract))
                k.link(v.tensor_scalar(past[:, :], past[:, :], float(ROWS), None, ALU.mult))
                k.link(v.tensor_tensor(excl[:, :, :], excl[:, :, :], past[:, :].unsqueeze(1).to_broadcast([128, NT, NE]), ALU.add))
                k.link(v.tensor_tensor(eq[:, :, :].rearrange("p t e -> p (t e)"), m.bank[0][0:P, 0:NT * NE],
                                       excl[0:P, :, :].rearrange("p t e -> p (t e)"), ALU.add))
                for i in range(2):
                    k.link(v.tensor_tensor(mask[:, :, :], eq[:, :, :], one[i][:, :, :], ALU.mult))
                    k.link(v.tensor_reduce(placef[:, i, :], mask[:, :, :], AX.X, ALU.add))
                    k.link(v.tensor_copy(m.slots[:, :, i], placef[:, i, :]))
                k.link(v.tensor_scalar(past[:, :], bend[:, :], jn[:, 0:1], None, ALU.is_le))
                k.link(v.tensor_reduce(bt[:, 0:1], past[:, :], AX.X, ALU.add))
                k.link(v.tensor_scalar(bt[:, 0:1], bt[:, 0:1], float(NE - 1), None, ALU.min))
                v.sem_inc(tabled, 1)
                v.wait_ge(turned2, 1)
                k.link(v.tensor_copy(m.btab[:, :], m.bank[2][0:1, 0:NB]))

            @block.scalar
            def _(a):
                if weighted:
                    a.wait_ge(masked, 1)
                    a.activation(ex[:, :, :], ex[:, :, :], ACT.Exp).then_inc(exped, 1)
                    a.activation(e2[:, :], e2[:, :], ACT.Exp).then_inc(exped, 1)

            @block.tensor
            def _(pe):
                pe.wait_ge(masked, 1)
                flat = mask[:, :, :].rearrange("p t e -> p (t e)")
                pe.matmul(m.bank[0][0:P, 0:NT * NE], m.before[:, :], flat, start=True, stop=True)
                pe.matmul(m.bank[1][:, 0:NT * NE], m.ones[0:P, :], flat, start=True, stop=True).then_inc(counted, 1)
                pe.wait_ge(tabled, 1)
                pe.transpose(m.bank[2][0:1, 0:128], bt[:, 0:1], m.ident[:, :]).then_inc(turned2, 1)


def experts_scatter(nc, m, tag):
    with Stage(nc) as c:
        scattered = c.sem(tag + "_scattered")
        with nc.Block() as block:
            @block.gpsimd
            def _(pool):
                for t in range(NT):
                    for i in range(2):
                        pool.indirect_dma_start(m.xsort, bass.IndirectOffsetOnAxis(ap=m.slots[:, t, i:i + 1], axis=0),
                                                m.acc[:, t, 0:D], None).then_inc(scattered, 16)
                pool.wait_ge(scattered, 16 * 2 * NT)


def experts_run(nc, m, tag, W1, b1, W2, b2):
    RW = ROWS // 128
    with Stage(nc) as c:
        def sb(n, s):
            return c.enter_context(nc.sbuf_tensor(tag + n, s, F32))

        def sem(n):
            return c.sem(tag + n)

        xb = sb("_xb", [128, 2, RW, D])
        w1 = sb("_w1", [128, 2, KD, HID])
        w2 = sb("_w2", [128, 2, KH, D])
        b1s = sb("_b1s", [128, 2, KH])
        b2s = sb("_b2s", [128, 2, D])
        xbT = sb("_xbT", [128, 2, KD, ROWS])
        hT = sb("_hT", [128, 2, KH, ROWS])
        y = sb("_y", [128, 2, RW, D])
        b1t = sb("_b1t", [128, NE, KH])
        b1n = sb("_b1n", [NE * KH, 128])
        loads = [sem(f"_loads{s}") for s in range(2)]
        stored = [sem(f"_stored{s}") for s in range(2)]
        b1_in, b1_turned, b1_kept = sem("_b1_in"), sem("_b1_turned"), sem("_b1_kept")
        turned, staged, hidden, bent, made, summed = [sem(n) for n in ("_turned", "_staged", "_hidden", "_bent", "_made", "_summed")]
        LOADS = 5

        def ok(j):
            return not isinstance(j, int) or 0 <= j < NB

        def blocks(eng, body, lag):
            body(0, 0, 0)
            body(1, 1, 0)
            with eng.Fori(1, NB // 2) as b:
                body(b * 2, 0, b)
                body(b * 2 + 1, 1, b)
            for j in range(NB, NB + lag):
                body(j, j % 2, j // 2)

        assert NB % 2 == 0
        with nc.Block() as block:
            @block.sync
            def _(sp):
                sp.dma_start(b1n[:, :], b1.rearrange("e (k p) -> (e k) p", p=128)).then_inc(b1_in, 16)
                sp.wait_ge(b1_kept, 1)

                def load(j, s, e):
                    wait_count(sp, turned, j - 1)
                    wait_count(sp, bent, j - 1)
                    wait_count(sp, made, j - 1)
                    wait_count(sp, summed, j - 1)
                    sp.dma_start(xb[:, s, :, :], m.xsort[bass.ds(j * ROWS, ROWS), :].rearrange("(p w) d -> p w d", p=128)).then_inc(loads[s], 16)
                    sp.dma_start(w1[:, s, :, :], W1[bass.ds(e, 1), :, :].rearrange("a (k p) h -> p (a k) h", p=128)).then_inc(loads[s], 16)
                    sp.dma_start(w2[:, s, :, :], W2[bass.ds(e, 1), :, :].rearrange("a (k p) d -> p (a k) d", p=128)).then_inc(loads[s], 16)
                    sp.dma_start(b1s[:, s, :], b1t[:, bass.ds(e, 1), :].rearrange("p a k -> p (a k)")).then_inc(loads[s], 16)
                    sp.dma_start(b2s[:, s, :], b2[bass.ds(e, 1), :].rearrange("a d -> (a d)").partition_broadcast(128)).then_inc(loads[s], 16)

                def store(j, s):
                    sp.wait_ge(summed, j + 1)
                    sp.dma_start(m.ysort[bass.ds(j * ROWS, ROWS), :].rearrange("(p w) d -> p w d", p=128), y[:, s, :, :]).then_inc(stored[s], 16)

                def experts_of(at):
                    _, e = nc.values_load_multi_w_load_instructions(m.btab[0:1, bass.ds(at, 2)], engines=[sp.engine], min_val=0, max_val=NE - 1)
                    return e

                e = experts_of(0)
                load(0, 0, e[0])
                load(1, 1, e[1])
                with sp.Fori(0, NB // 2 - 1) as b:
                    e = experts_of(b * 2 + 2)
                    for s in range(2):
                        store(b * 2 + s, s)
                        load(b * 2 + 2 + s, s, e[s])
                store(NB - 2, 0)
                store(NB - 1, 1)
                for s in range(2):
                    sp.wait_ge(stored[s], 16 * NB // 2)

            @block.tensor
            def _(pe):
                pe.wait_ge(b1_in, 16)
                pe.transpose(m.bank[0][:, 0:NE * KH], b1n[:, :], m.ident[0:NE * KH, 0:NE * KH]).then_inc(b1_turned, 1)
                pe.wait_ge(b1_kept, 1)

                def body(j, s, b):
                    if ok(j):
                        pe.wait_ge(loads[s], (b + 1) * (16 * LOADS))
                        wait_count(pe, staged, j)
                        for w in range(RW):
                            for k in range(KD):
                                at = k * ROWS + w * 128
                                ins = pe.transpose(m.bank[0][:, at:at + 128], xb[:, s, w, k * 128:(k + 1) * 128], m.ident[:, :])
                        ins.then_inc(turned, 1)
                        pe.wait_ge(staged, j + 1)
                        wait_count(pe, bent, j - 1)
                        for h in range(KH):
                            bank = m.bank[1 + 2 * s + h // 2]
                            for k in range(KD):
                                ins = pe.matmul(bank[:, (h % 2) * ROWS:(h % 2 + 1) * ROWS], w1[:, s, k, h * 128:(h + 1) * 128],
                                                xbT[:, s, k, :], start=(k == 0), stop=(k == KD - 1))
                        ins.then_inc(hidden, 1)
                    if ok(j - 1):
                        o = 1 - s
                        pe.wait_ge(bent, j)
                        wait_count(pe, summed, j - 2)
                        for w in range(RW):
                            for h in range(KH):
                                ins = pe.matmul(m.bank[5 + o][:, w * D:(w + 1) * D], hT[:, o, h, w * 128:(w + 1) * 128], w2[:, o, h, :],
                                                start=(h == 0), stop=(h == KH - 1))
                        ins.then_inc(made, 1)

                blocks(pe, body, 1)

            @block.scalar
            def _(a):
                def body(j, s, b):
                    a.wait_ge(hidden, j + 1)
                    wait_count(a, made, j - 1)
                    for h in range(KH):
                        ins = a.activation(hT[:, s, h, :], m.bank[1 + 2 * s + h // 2][:, (h % 2) * ROWS:(h % 2 + 1) * ROWS], ACT.Gelu,
                                           bias=b1s[:, s, h:h + 1])
                    ins.then_inc(bent, 1)

                blocks(a, body, 0)

            @block.vector
            def _(v):
                v.wait_ge(b1_turned, 1)
                v.tensor_copy(b1t[:, :, :].rearrange("p e k -> p (e k)"), m.bank[0][:, 0:NE * KH]).then_inc(b1_kept, 1)

                def body(j, s, b):
                    if ok(j):
                        v.wait_ge(turned, j + 1)
                        wait_count(v, hidden, j - 1)
                        v.tensor_copy(xbT[:, s, :, :].rearrange("p k n -> p (k n)"), m.bank[0][:, :]).then_inc(staged, 1)
                    if ok(j - 1):
                        o = 1 - s
                        v.wait_ge(made, j)
                        wait_count(v, stored[o], b * 16 - (16 if s == 0 else 0))
                        v.tensor_tensor(y[:, o, :, :], m.bank[5 + o][:, :].rearrange("p (w d) -> p w d", w=RW),
                                        b2s[:, o, :].unsqueeze(1).to_broadcast([128, RW, D]), ALU.add).then_inc(summed, 1)

                blocks(v, body, 1)


def experts_combine(nc, m, tag, weighted):
    R = 5
    with Stage(nc) as c:
        y = c.enter_context(nc.sbuf_tensor(tag + "_yy", [P, R, 2, D], F32))
        fetched = [c.sem(f"{tag}_fetched{r}") for r in range(R)]
        used, half = [c.sem(tag + n) for n in ("_used", "_halfway")]
        with nc.Block() as block:
            @block.gpsimd
            def _(pool):
                for t in range(NT):
                    if t >= R:
                        pool.wait_ge(used, t - R + 1)
                    for i in range(2):
                        pool.indirect_dma_start(y[:, t % R, i, :], None, m.ysort,
                                                bass.IndirectOffsetOnAxis(ap=m.slots[:, t, i:i + 1], axis=0)).then_inc(fetched[t % R], 16)

            @block.vector
            def _(v):
                with v.Fori(0, NT // R) as b:
                    for r in range(R):
                        t = b * R + r
                        x = row_of(m.xs, t)
                        v.wait_ge(fetched[r], b * 32 + 32)
                        for i, done in ((0, half), (1, used)):
                            if weighted:
                                v.scalar_tensor_tensor(x, y[:, r, i, :], m.cw[:, i, bass.ds(t, 1)], x, ALU.mult, ALU.add).then_inc(done, 1)
                            else:
                                v.tensor_tensor(x, x, y[:, r, i, :], ALU.add).then_inc(done, 1)
                            if i == 0:
                                v.wait_ge(half, t + 1)


def experts(nc, m, tag, gw, gb, W1, b1, W2, b2, weighted):
    normalise(nc, m, tag + "_ln", m.xs)
    experts_route(nc, m, tag + "_route", gw, gb, weighted)
    experts_scatter(nc, m, tag + "_scatter")
    experts_run(nc, m, tag + "_run", W1, b1, W2, b2)
    experts_combine(nc, m, tag + "_combine", weighted)


def weights1(nc, m, c, w):
    def sb(n, s):
        return c.enter_context(nc.sbuf_tensor(n, s, F32))

    GH = D // 4
    m.nodew = sb("w1_node", [128, KD, D + 2 * HEADS])
    m.wqkv = sb("w1_qkv", [128, KD, 3 * D])
    m.wproj = sb("w1_proj", [128, KD, D])
    m.bproj = sb("w1_bproj", [P, D])
    m.wg1 = sb("w1_g1", [128, KD, GH])
    m.wg2 = sb("w1_g2", [GH, D])
    m.bg1 = sb("w1_bg1", [GH, 1])
    m.nbg2 = sb("w1_nbg2", [128, KD])
    m.lngT = sb("w1_lng", [128, KD])
    m.lnbT = sb("w1_lnb", [128, KD])
    with Stage(nc) as c2:
        al = c2.enter_context(nc.sbuf_tensor("w1_attn", [128, 2, D], F32))
        pr = c2.enter_context(nc.sbuf_tensor("w1_prod", [128, KD, 2, D], F32))
        loaded, chain = [c2.sem("w1_" + n) for n in ("loaded", "chain")]
        jobs = [(m.nodew[:, :, 0:D], w["L1_gnn_W"].rearrange("(k p) d -> p k d", p=128)),
                (al[:, 0, :], w["L1_gnn_attn_l"].rearrange("h c -> (h c)").partition_broadcast(128)),
                (al[:, 1, :], w["L1_gnn_attn_r"].rearrange("h c -> (h c)").partition_broadcast(128)),
                (m.wqkv[:, :, :], w["L1_mix_Wqkv"].rearrange("(k p) d -> p k d", p=128)),
                (m.wproj[:, :, :], w["L1_mix_Wproj"].rearrange("(k p) d -> p k d", p=128)),
                (m.bproj[:, :], w["L1_mix_bproj"].partition_broadcast(P)),
                (m.wg1[:, :, :], w["L1_mix_Wg1"].rearrange("(k p) d -> p k d", p=128)),
                (m.wg2[:, :], w["L1_mix_Wg2"]),
                (m.bg1[:, :], w["L1_mix_bg1"].rearrange("(p o) -> p o", o=1)),
                (m.nbg2[:, :], w["L1_mix_bg2"].rearrange("(k p) -> p k", p=128)),
                (m.lngT[:, :], w["L1_mix_ln_g"].rearrange("(k p) -> p k", p=128)),
                (m.lnbT[:, :], w["L1_mix_ln_b"].rearrange("(k p) -> p k", p=128))]
        with nc.Block() as block:
            @block.sync
            def _(sp):
                for dst, src in jobs:
                    sp.dma_start(dst, src).then_inc(loaded, 16)
                sp.wait_ge(loaded, 16 * len(jobs))

            @block.vector
            def _(v):
                k = Chain(v, chain, 0)
                v.wait_ge(loaded, 16 * len(jobs))
                k.link(v.tensor_scalar(m.nbg2[:, :], m.nbg2[:, :], -1.0, None, ALU.mult))
                for b in range(KD):
                    for x in range(2):
                        k.link(v.tensor_tensor(pr[:, b, x, :], m.nodew[:, b, 0:D], al[:, x, :], ALU.mult))
                        at = D + x * HEADS
                        k.link(v.tensor_reduce(m.nodew[:, b, at:at + HEADS], pr[:, b, x, :].rearrange("p (h c) -> p h c", c=HC), AX.X, ALU.add))


def gate_hidden(nc, m):
    GH = D // 4
    with Stage(nc) as c:
        def sb(n, s):
            return c.enter_context(nc.sbuf_tensor("gate_" + n, s, F32))

        def sem(n):
            return c.sem("gate_" + n)

        shift = sb("shift", [P, NT])
        xn = sb("xn", [P, 2, D])
        st = sb("st", [P, NT, 6])
        mean2 = sb("mean2", [P, NT])
        rstd2 = sb("rstd2", [P, NT])
        scale3 = sb("scale3", [P, NT])
        shift3 = sb("shift3", [P, NT])
        x3 = sb("x3", [P, 2, D])
        x3T = sb("x3T", [128, 2, KD, P])
        chain, renormed, stated, normed, turned, scaled, made, bent, powered, rows3 = [
            sem(n) for n in ("chain", "renormed", "stated", "normed", "turned", "scaled", "made", "bent", "powered", "rows3")]
        restated = sem("restated")
        with nc.Block() as block:
            @block.vector
            def _(v):
                k = Chain(v, chain, 0)
                k.link(v.scalar_tensor_tensor(shift[:, :], m.mean[:, :], -1.0, m.rstd[:, :], ALU.mult, ALU.mult))

                def stats(t, s):
                    if valid(t):
                        wait_count(v, stated, t - 1)
                        v.tensor_scalar(xn[:, s, :], row_of(m.xs, t), m.rstd[:, bass.ds(t, 1)], shift[:, bass.ds(t, 1)],
                                        ALU.mult, ALU.add).then_inc(renormed, 1)
                    if valid(t - 1):
                        v.wait_ge(renormed, t)
                        v.bn_stats(row_of(st, t - 1), xn[:, 1 - s, :]).then_inc(stated, 1)

                pipelined(v, stats, 1)
                v.wait_ge(stated, NT)
                moments(v, restated, st, mean2[:, :], rstd2[:, :], scale3[:, :], shift3[:, :])
                v.wait_ge(powered, 1)
                k.link(v.tensor_tensor(scale3[:, :], m.rstd[:, :], rstd2[:, :], ALU.mult))
                k.link(v.tensor_tensor(shift3[:, :], shift[:, :], mean2[:, :], ALU.subtract))
                k.link(v.tensor_tensor(shift3[:, :], shift3[:, :], rstd2[:, :], ALU.mult))

                def rows(t, s):
                    if valid(t):
                        wait_count(v, turned, t - 1)
                        v.tensor_scalar(x3[:, s, :], row_of(m.xs, t), scale3[:, bass.ds(t, 1)], shift3[:, bass.ds(t, 1)],
                                        ALU.mult, ALU.add).then_inc(rows3, 1)
                    if valid(t - 1):
                        v.wait_ge(turned, t)
                        wait_count(v, made, t - 2)
                        for b in range(KD):
                            ins = v.tensor_scalar(x3T[:, 1 - s, b, :], m.bank[1 - s][:, b * 128:b * 128 + P], m.lngT[:, b:b + 1],
                                                  m.lnbT[:, b:b + 1], ALU.mult, ALU.add)
                        ins.then_inc(scaled, 1)

                pipelined(v, rows, 1)

            @block.gpsimd
            def _(pool):
                pool.wait_ge(restated, 8)
                pool.tensor_tensor(rstd2[:, :], rstd2[:, :], m.half[0:P, 0:NT], ALU.pow).then_inc(powered, 1)

            @block.tensor
            def _(pe):
                def body(t, s):
                    if valid(t):
                        pe.wait_ge(rows3, t + 1)
                        wait_count(pe, scaled, t - 1)
                        for b in range(KD):
                            ins = pe.transpose(m.bank[s][:, b * 128:b * 128 + P], x3[:, s, b * 128:(b + 1) * 128], m.ident[0:P, 0:P])
                        ins.then_inc(turned, 1)
                    if valid(t - 1):
                        pe.wait_ge(scaled, t)
                        wait_count(pe, bent, t - 2)
                        for b in range(KD):
                            ins = pe.matmul(m.bank[3 - s][0:GH, 0:P], m.wg1[:, b, :], x3T[:, 1 - s, b, :], start=(b == 0), stop=(b == KD - 1))
                        ins.then_inc(made, 1)

                pipelined(pe, body, 1)

            @block.scalar
            def _(a):
                def body(t, s):
                    a.wait_ge(made, t + 1)
                    a.activation(m.hgT[:, tile_cols(t)], m.bank[2 + s][0:GH, 0:P], ACT.Gelu, bias=m.bg1[:, 0:1]).then_inc(bent, 1)

                pipelined(a, body, 0)


def mix1_keys(nc, m):
    with Stage(nc) as c:
        made, kept, topped = [c.sem("keys1_" + n) for n in ("made", "kept", "topped")]
        with nc.Block() as block:
            @block.tensor
            def _(pe):
                def body(t, s):
                    wait_count(pe, kept, t - 1)
                    for o in range(KD):
                        for k in range(KD):
                            ins = pe.matmul(m.bank[s][:, o * 128:o * 128 + P], m.wqkv[:, k, D + o * 128:D + (o + 1) * 128],
                                            m.xT[:, k, tile_cols(t)], start=(k == 0), stop=(k == KD - 1))
                    ins.then_inc(made, 1)

                pipelined(pe, body, 0)

            @block.scalar
            def _(a):
                def body(t, s):
                    a.wait_ge(made, t + 1)
                    a.activation(m.kT[:, :, tile_cols(t)], by_feature(m.bank[s]), ACT.Copy).then_inc(kept, 1)

                pipelined(a, body, 0)

            @block.vector
            def _(v):
                v.wait_ge(kept, NT)
                v.tensor_reduce(m.nmax[:, :], m.kT[:, :, :], AX.X, ALU.max).then_inc(topped, 1)
                v.wait_ge(topped, 1)
                v.tensor_scalar(m.nmax[:, :], m.nmax[:, :], -1.0, None, ALU.mult)


def mix1_context(nc, m):
    with Stage(nc) as c:
        def sb(n, s):
            return c.enter_context(nc.sbuf_tensor("ctx_" + n, s, F32))

        def sem(n):
            return c.sem("ctx_" + n)

        xst = sb("xst", [128, 2, KD, P])
        ekT = sb("ekT", [128, 2, KD, P])
        ek = sb("ek", [P, 2, D])
        vv = sb("v", [P, 2, D])
        part = sb("part", [128, KD, NT])
        den = sb("den", [128, KD])
        zeros = sb("zeros", [P, 128])
        staged, exped, turned, made, ekept, vkept, summed, zeroed, chain = [
            sem(n) for n in ("staged", "exped", "turned", "made", "ekept", "vkept", "summed", "zeroed", "chain")]
        with nc.Block() as block:
            @block.scalar
            def _(a):
                def body(t, s):
                    wait_count(a, turned, t - 1)
                    for k in range(KD):
                        ins = a.activation(ekT[:, s, k, :], m.kT[:, k, tile_cols(t)], ACT.Exp, bias=m.nmax[:, k:k + 1],
                                           accum_out=part[:, k, bass.ds(t, 1)])
                    ins.then_inc(exped, 1)
                    wait_count(a, made, t - 1)
                    a.activation(xst[:, s, :, :], m.xT[:, :, tile_cols(t)], ACT.Copy).then_inc(staged, 1)

                pipelined(a, body, 0)

            @block.tensor
            def _(pe):
                pe.wait_ge(zeroed, 1)
                pe.matmul(m.bank[4][:, 0:D], zeros[:, :], zeros[:, :].unsqueeze(1).to_broadcast([P, KD, 128]), start=True, stop=False)

                def body(t, s):
                    if valid(t):
                        pe.wait_ge(exped, t + 1)
                        wait_count(pe, ekept, t - 1)
                        for k in range(KD):
                            ins = pe.transpose(m.bank[s][0:P, k * 128:(k + 1) * 128], ekT[:, s, k, :], m.ident[:, :])
                        ins.then_inc(turned, 1)
                        pe.wait_ge(staged, t + 1)
                        wait_count(pe, vkept, t - 1)
                        for k in range(KD):
                            ins = pe.matmul(m.bank[2 + s][0:P, 0:D], xst[:, s, k, :], m.wqkv[:, k, 2 * D:3 * D], start=(k == 0), stop=(k == KD - 1))
                        ins.then_inc(made, 1)
                    if valid(t - 1):
                        pe.wait_ge(vkept, t)
                        for k in range(KD):
                            ins = pe.matmul(m.bank[4][:, k * 128:(k + 1) * 128], ek[:, 1 - s, k * 128:(k + 1) * 128],
                                            vv[:, 1 - s, k * 128:(k + 1) * 128], start=False, stop=False, skip_group_check=True)
                        ins.then_inc(summed, 1)

                pipelined(pe, body, 1)
                pe.matmul(m.bank[4][:, 0:D], zeros[:, :], zeros[:, :].unsqueeze(1).to_broadcast([P, KD, 128]),
                          start=False, stop=True).then_inc(summed, 1)

            @block.vector
            def _(v):
                v.memset(zeros[:, :], 0.0).then_inc(zeroed, 1)

                def body(t, s):
                    v.wait_ge(turned, t + 1)
                    wait_count(v, summed, t - 1)
                    v.tensor_copy(ek[:, s, :], m.bank[s][0:P, 0:D]).then_inc(ekept, 1)
                    v.wait_ge(made, t + 1)
                    v.tensor_copy(vv[:, s, :], m.bank[2 + s][0:P, 0:D]).then_inc(vkept, 1)

                pipelined(v, body, 0)
                k = Chain(v, chain, 0)
                v.wait_ge(exped, NT)
                k.link(v.tensor_reduce(den[:, :], part[:, :, :], AX.X, ALU.add))
                k.link(v.reciprocal(den[:, :], den[:, :]))
                v.wait_ge(summed, NT + 1)
                for b in range(KD):
                    k.link(v.scalar_tensor_tensor(m.kv[:, b, :], m.bank[4][:, b * 128:(b + 1) * 128], den[:, b:b + 1],
                                                  m.headmask[:, :], ALU.mult, ALU.mult))


def mix1_out(nc, m):
    GH = D // 4
    with Stage(nc) as c:
        def sb(n, s):
            return c.enter_context(nc.sbuf_tensor("out1_" + n, s, F32))

        def sem(n):
            return c.sem("out1_" + n)

        qT = sb("qT", [128, 2, KD, P])
        eg = sb("eg", [128, 2, KD, P])
        goT = sb("goT", [128, 2, KD, P])
        queried, qkept, mixed, gated, exped, chain, gone, made, added, biased = [
            sem(n) for n in ("queried", "qkept", "mixed", "gated", "exped", "chain", "gone", "made", "added", "biased")]
        with nc.Block() as block:
            @block.tensor
            def _(pe):
                def body(t, s):
                    if valid(t):
                        wait_count(pe, qkept, t - 1)
                        for o in range(KD):
                            for k in range(KD):
                                ins = pe.matmul(m.bank[s][:, o * 128:o * 128 + P], m.wqkv[:, k, o * 128:(o + 1) * 128],
                                                m.xT[:, k, tile_cols(t)], start=(k == 0), stop=(k == KD - 1))
                        ins.then_inc(queried, 1)
                        wait_count(pe, exped, t)
                        for o in range(KD):
                            ins = pe.matmul(m.bank[6][:, o * 128:o * 128 + P], m.wg2[:, o * 128:(o + 1) * 128], m.hgT[:, tile_cols(t)],
                                            start=True, stop=True)
                        ins.then_inc(gated, 1)
                    if valid(t - 1):
                        pe.wait_ge(qkept, t)
                        wait_count(pe, gone, t - 2)
                        for k in range(KD):
                            ins = pe.matmul(m.bank[3 - s][:, k * 128:k * 128 + P], m.kv[:, k, :], qT[:, 1 - s, k, :], start=True, stop=True)
                        ins.then_inc(mixed, 1)
                    if valid(t - 2):
                        pe.wait_ge(gone, t - 1)
                        wait_count(pe, added, t - 3)
                        for k in range(KD):
                            ins = pe.matmul(m.bank[4 + s][0:P, 0:D], goT[:, s, k, :], m.wproj[:, k, :], start=(k == 0), stop=(k == KD - 1))
                        ins.then_inc(made, 1)

                pipelined(pe, body, 2)

            @block.scalar
            def _(a):
                def body(t, s):
                    a.wait_ge(queried, t + 1)
                    wait_count(a, mixed, t - 1)
                    a.activation(qT[:, s, :, :], by_feature(m.bank[s]), ACT.Copy).then_inc(qkept, 1)
                    a.wait_ge(gated, t + 1)
                    wait_count(a, gone, t - 1)
                    for k in range(KD):
                        ins = a.activation(eg[:, s, k, :], m.bank[6][:, k * 128:k * 128 + P], ACT.Exp, bias=m.nbg2[:, k:k + 1], scale=-1.0)
                    ins.then_inc(exped, 1)

                pipelined(a, body, 0)

            @block.vector
            def _(v):
                k = Chain(v, chain, 2)

                def body(t, s):
                    if valid(t):
                        k.step(t)
                        v.wait_ge(exped, t + 1)
                        k.link(v.tensor_scalar(eg[:, s, :, :], eg[:, s, :, :], 1.0, None, ALU.add))
                        k.link(v.reciprocal(eg[:, s, :, :], eg[:, s, :, :]))
                        k.close()
                        v.wait_ge(mixed, t + 1)
                        wait_count(v, made, t - 1)
                        v.tensor_tensor(goT[:, s, :, :], by_feature(m.bank[2 + s]), eg[:, s, :, :], ALU.mult).then_inc(gone, 1)
                        x = row_of(m.xs, t)
                        v.tensor_tensor(x, x, m.bproj[:, :], ALU.add).then_inc(biased, 1)
                    if valid(t - 1):
                        x = row_of(m.xs, t - 1)
                        v.wait_ge(biased, t)
                        v.wait_ge(made, t)
                        v.tensor_tensor(x, x, m.bank[5 - s][0:P, 0:D], ALU.add).then_inc(added, 1)

                pipelined(v, body, 1)


def graph_attention1(nc, m):
    C = 5
    with Stage(nc) as c:
        def sb(n, s):
            return c.enter_context(nc.sbuf_tensor("elu_" + n, s, F32))

        def sem(n):
            return c.sem("elu_" + n)

        rden = sb("rden", [P, NT, HEADS])
        neg = sb("neg", [P, C, D])
        chain, lowered, exped = sem("chain"), sem("lowered"), sem("exped")
        with nc.Block() as block:
            @block.vector
            def _(v):
                k = Chain(v, chain, 0)
                k.link(v.tensor_scalar(rden[:, :, :], m.acc[:, :, D:D + HEADS], 1e-37, None, ALU.max))
                k.link(v.reciprocal(rden[:, :, :], rden[:, :, :]))
                for i in range(NT // C):
                    for t in range(i * C, (i + 1) * C):
                        o = m.acc[:, t, 0:D].rearrange("p (h c) -> p h c", c=HC)
                        ins = v.tensor_tensor(o, o, rden[:, t, :].unsqueeze(2).to_broadcast([P, HEADS, HC]), ALU.mult)
                    k.link(ins)
                    o = m.acc[:, i * C:(i + 1) * C, 0:D]
                    x = m.xs[:, i * C:(i + 1) * C, :]
                    v.tensor_scalar(neg[:, :, :], o, 0.0, None, ALU.min).then_inc(lowered, 1)
                    k.link(v.tensor_scalar(x, x, -1.0, None, ALU.add))
                    v.wait_ge(exped, i + 1)
                    k.link(v.scalar_tensor_tensor(o, o, 0.0, neg[:, :, :], ALU.max, ALU.add))
                    k.link(v.tensor_tensor(x, x, o, ALU.add))

            @block.scalar
            def _(a):
                for i in range(NT // C):
                    a.wait_ge(lowered, i + 1)
                    a.activation(neg[:, :, :], neg[:, :, :], ACT.Exp).then_inc(exped, 1)


def program(nc, w, out):
    m = Memory()
    m.edges = nc.dram_tensor("edge_list", [E + PAD, 2], I32).ap()
    m.table = {1: nc.dram_tensor("table0", [N, D + 2], F32).ap(), HEADS: nc.dram_tensor("table1", [N, D + 2 * HEADS], F32).ap()}
    m.xsort = nc.dram_tensor("xsort", [NB * ROWS, D], F32).ap()
    m.ysort = nc.dram_tensor("ysort", [NB * ROWS, D], F32).ap()
    with ExitStack() as c:
        c.enter_context(nc.allow_non_contiguous_dma(reason="biases of a few hundred elements, one per partition"))

        def sb(n, s, d=F32):
            return c.enter_context(nc.sbuf_tensor(n, s, d))

        m.bank = [c.enter_context(nc.psum_tensor(f"bank{i}", [128, 512], F32)) for i in range(8)]
        m.ident = sb("ident", [128, 128])
        m.ones = sb("ones", [128, 128])
        m.before = sb("before", [P, P])
        m.headmask = sb("headmask", [128, 128])
        m.nodes = sb("nodes", [128, N])
        m.half = sb("half", [128, 64])
        m.xs = sb("xs", [P, NT, D])
        m.xT = sb("xT", [128, KD, N])
        m.acc = sb("acc", [P, NT, D + 2 * HEADS])
        m.adm = sb("adm", [P, NT, 2 * HEADS])
        m.mean = sb("mean", [P, NT])
        m.rstd = sb("rstd", [P, NT])
        m.grow = sb("grow", [1, 2, 2, 128], I32)
        m.gtab = sb("gtab", [1, 2, NG], I32)
        m.kv = sb("kv", [128, KD, 128])
        m.cw = sb("cw", [P, 2, NT])
        m.slots = sb("slots", [P, NT, 2], I32)
        m.btab = sb("btab", [1, NB], I32)
        m.eall = sb("eall", [128, NG * 4], I32)
        constants(nc, m)
        load_x(nc, m, w["x"])
        edge_tables(nc, m, w["src"], w["dst"])
        with ExitStack() as layer:
            weights0(nc, m, layer, w)
            normalise(nc, m, "ln0", m.xs)
            node_tables(nc, m, "nt0", 1)
            score_bounds(nc, m, "sb0", 1)
            edge_sums(nc, m, "es0", 1, True)
            graph_attention0(nc, m)
            mix0_keys(nc, m)
            mix0_queries(nc, m)
            mix0_out(nc, m)
        experts(nc, m, "ffn0", w["L0_ffn_gate_w"], w["L0_ffn_gate_b"], w["L0_ffn_W1"], w["L0_ffn_b1"],
                w["L0_ffn_W2"], w["L0_ffn_b2"], True)
        with ExitStack() as layer:
            weights1(nc, m, layer, w)
            m.kT = layer.enter_context(nc.sbuf_tensor("kT", [128, KD, N], F32))
            m.hgT = layer.enter_context(nc.sbuf_tensor("hgT", [D // 4, N], F32))
            m.nmax = layer.enter_context(nc.sbuf_tensor("nmax", [128, KD], F32))
            normalise(nc, m, "ln1", m.xs)
            gate_hidden(nc, m)
            node_tables(nc, m, "nt1", HEADS, True)
            score_bounds(nc, m, "sb1", HEADS)
            edge_sums(nc, m, "es1", HEADS, False)
            mix1_keys(nc, m)
            mix1_context(nc, m)
            mix1_out(nc, m)
            graph_attention1(nc, m)
        experts(nc, m, "ffn1", w["L1_ffn_Wg"], w["L1_ffn_bg"], w["L1_ffn_W1"], w["L1_ffn_b1"],
                w["L1_ffn_W2"], w["L1_ffn_b2"], False)
        store_x(nc, m, out)


_INS = ["x", "src", "dst", "L0_gnn_W", "L0_gnn_att_src", "L0_gnn_att_dst", "L0_gnn_bias", "L0_gnn_W_ih",
        "L0_mix_w_qkv", "L0_mix_b_qkv", "L0_mix_kln_g", "L0_mix_kln_b", "L0_mix_vln_g", "L0_mix_vln_b",
        "L0_mix_w1", "L0_mix_b1", "L0_mix_w2", "L0_mix_b2", "L0_ffn_gate_w", "L0_ffn_gate_b", "L0_ffn_W1",
        "L0_ffn_b1", "L0_ffn_W2", "L0_ffn_b2", "L1_gnn_W", "L1_gnn_attn_l", "L1_gnn_attn_r", "L1_mix_Wqkv",
        "L1_mix_Wproj", "L1_mix_bproj", "L1_mix_ln_g", "L1_mix_ln_b", "L1_mix_Wg1", "L1_mix_bg1",
        "L1_mix_Wg2", "L1_mix_bg2", "L1_ffn_Wg", "L1_ffn_bg", "L1_ffn_W1", "L1_ffn_b1", "L1_ffn_W2", "L1_ffn_b2"]


def kernel(**inputs):
    import numpy as np
    import concourse.bacc as bacc
    from concourse.bass_utils import run_bass_kernel_spmd

    nc = bacc.Bacc("TRN2", target_bir_lowering=False, num_devices=1)
    arrays, args = {}, {}
    for name in _INS:
        a = np.ascontiguousarray(inputs[name])
        arrays[f"in_{name}"] = a
        args[name] = nc.dram_tensor(f"in_{name}", a.shape, mybir.dt.from_np(a.dtype), kind="ExternalInput").ap()
    out = nc.dram_tensor("out_x", (N, D), F32, kind="ExternalOutput").ap()
    program(nc, args, out)
    r = run_bass_kernel_spmd(nc, [arrays], core_ids=[0])
    return r.results[0]["out_x"]
```

```python
from contextlib import ExitStack

import concourse.bass as bass
from concourse import mybir

F32 = mybir.dt.float32
I32 = mybir.dt.int32
ALU = mybir.AluOpType
ACT = mybir.ActivationFunctionType
AX = mybir.AxisListType
MAX = bass.bass_isa.ReduceOp.max

N, E = 3125, 50000
P, NT = 125, 25
D = 256
KD = D // 128
HEADS, HC = 8, 32
NE, HID = 8, 512
KH = HID // 128
EPS = 1e-5
SLOPE = 0.2
BIG = 3.0e38
SAFE = 60.0
FLOOR = 1.0e30

PAD = 256
FAR = 8000
WIN = 2
GE = WIN * 128
NG = (E + NT * (GE - 1)) // GE + 1
NG += -NG % 8

ROWS = 256
NB = (2 * N + NE * (ROWS - 1)) // ROWS
EC = E // P


class Chain:

    def __init__(self, eng, sem, per):
        self.eng, self.sem, self.per = eng, sem, per
        self.base, self.n = 0, 0

    def step(self, t):
        self.base, self.n = t * self.per, 0

    def link(self, ins):
        ins.then_inc(self.sem, 1)
        self.n += 1
        self.eng.wait_ge(self.sem, self.base + self.n)

    def close(self):
        assert self.n == self.per, self.n


class Stage(ExitStack):

    def __init__(self, nc):
        super().__init__()
        self.nc, self.sems = nc, []

    def sem(self, name):
        self.sems.append(self.nc.alloc_semaphore(name))
        return self.sems[-1]

    def __exit__(self, *error):
        super().__exit__(*error)
        if not error[0]:
            self.nc.clear_and_free_semaphores(self.sems)
            self.nc.all_engine_barrier()


class Memory:
    pass


def tile_cols(t):
    return bass.ds(t * P, P)


def over_tiles(eng, step):
    with eng.Fori(0, NT // 2) as b:
        step(b * 2, 0)
        step(b * 2 + 1, 1)
    step(NT - 1, (NT - 1) % 2)


def valid(t):
    return not isinstance(t, int) or 0 <= t < NT


def pipelined(eng, body, lag):
    first = 2 if lag else 1
    for t in range(2 * first):
        body(t, t % 2)
    with eng.Fori(first, NT // 2) as b:
        body(b * 2, 0)
        body(b * 2 + 1, 1)
    for t in range(NT - 1, NT + lag):
        body(t, t % 2)


def wait_count(eng, sem, value):
    if not isinstance(value, int) or value > 0:
        eng.wait_ge(sem, value)


def row_of(t3, t):
    return t3[:, bass.ds(t, 1), :].rearrange("p a d -> p (a d)")


def by_feature(bank):
    return bank[:, 0:KD * 128].rearrange("p (k n) -> p k n", k=KD)[:, :, 0:P]


def constants(nc, m):
    with Stage(nc) as c, nc.Block() as block:
        const_set = c.sem("const_set")

        @block.gpsimd
        def _(pool):
            c = Chain(pool, const_set, 0)
            c.link(pool.memset(m.ident[:, :], 0.0))
            c.link(pool.affine_select(out=m.ident[:, :], in_=m.ident[:, :], pattern=[[-1, 128]],
                                      compare_op=ALU.not_equal, fill=1.0, base=0, channel_multiplier=1))
            c.link(pool.memset(m.ones[:, :], 1.0))
            c.link(pool.memset(m.before[:, :], 1.0))
            c.link(pool.affine_select(out=m.before[:, :], in_=m.before[:, :], pattern=[[1, P]],
                                      compare_op=ALU.is_ge, fill=0.0, base=-1, channel_multiplier=-1))
            c.link(pool.memset(m.headmask[:, :], 1.0))
            hm = m.headmask[:, :].rearrange("p (g c) -> p g c", c=HC)
            c.link(pool.affine_select(out=hm, in_=hm, pattern=[[-HC, 4], [0, HC]], compare_op=ALU.is_ge,
                                      fill=0.0, base=0, channel_multiplier=1))
            c.link(pool.affine_select(out=hm, in_=hm, pattern=[[HC, 4], [0, HC]], compare_op=ALU.is_ge,
                                      fill=0.0, base=HC - 1, channel_multiplier=-1))
            c.link(pool.iota(m.nodes[:, :], pattern=[[1, N]], base=0, channel_multiplier=0,
                             allow_small_or_imprecise_dtypes=True))
            c.link(pool.memset(m.half[:, :], -0.5))


def edge_tables(nc, m, src, dst):
    with Stage(nc) as c:
        def sb(n, s, d=F32):
            return c.enter_context(nc.sbuf_tensor(n, s, d))

        def sem(n):
            return c.sem(n)

        pairs = sb("edge_pairs", [P, EC, 2], I32)
        ends = sb("edge_ends", [P, 2, EC], I32)
        dstf = sb("edge_dstf", [P, EC])
        hit = sb("edge_hit", [P, EC])
        cnt = sb("edge_cnt", [P, NT + 1])
        pad = sb("edge_pad", [128, PAD // 128, 2], I32)
        first = sb("edge_first", [128, NT + 1])
        size_i = sb("edge_size_i", [128, NT], I32)
        groups = sb("edge_groups", [128, NT])
        gend = sb("edge_gend", [128, NT])
        base = sb("edge_base", [128, NT + 1])
        gcol = sb("edge_gcol", [128, 2, NT])
        gnum = sb("edge_gnum", [128, 2])
        past = sb("edge_past", [128, 2, NT])
        gt = sb("edge_gt", [128, 2, 2])
        zero = sb("edge_zero", [128, NT])
        next_first = sb("edge_next_first", [P, 1], I32)
        next_f = sb("edge_next_f", [P, 1])
        wrong = sb("edge_wrong", [P, 2])
        unordered = sb("edge_unordered", [1, 2], I32)
        loaded, chain, counted, summed = sem("edge_loaded"), sem("edge_chain"), sem("edge_counted"), sem("edge_summed")
        joined, stored, setup, tabled, turned = sem("edge_joined"), sem("edge_stored"), sem("edge_setup"), sem("edge_tabled"), sem("edge_turned")
        rows_set, moved, last_set = sem("edge_rows_set"), sem("edge_moved"), sem("edge_last_set")
        GH = NG // 2
        with nc.Block() as block:
            @block.sync
            def _(sp):
                sp.dma_start(ends[:, 0, :], src.rearrange("(p c) -> p c", c=EC)).then_inc(loaded, 16)
                sp.dma_start(ends[:, 1, :], dst.rearrange("(p c) -> p c", c=EC)).then_inc(loaded, 16)
                sp.wait_ge(last_set, 1)
                sp.dma_start(next_first[0:P - 1, :], dst.rearrange("(p c) -> p c", c=EC)[1:P, 0:1]).then_inc(loaded, 16)
                sp.wait_ge(joined, 2)
                sp.dma_start(m.edges[0:E, :].rearrange("(p c) x -> p c x", c=EC), pairs[:, :, :]).then_inc(stored, 16)
                sp.wait_ge(setup, 4)
                sp.dma_start(m.edges[E:E + PAD, :].rearrange("(p c) x -> p c x", p=128), pad[:, :, :]).then_inc(stored, 16)
                sp.wait_ge(stored, 32)
                sp.wait_ge(rows_set, 1)
                for h in range(2):
                    sp.dma_start(m.gtab[0:1, 0, h * GH:(h + 1) * GH], m.grow[0:1, h, 0, 0:GH]).then_inc(moved, 16)
                    sp.dma_start(m.gtab[0:1, 1, h * GH:(h + 1) * GH], m.grow[0:1, h, 1, 0:GH]).then_inc(moved, 16)
                sp.wait_ge(moved, 64)

            @block.gpsimd
            def _(pool):
                pool.memset(next_first[:, :], N).then_inc(last_set, 1)
                pool.memset(pad[:, :, 0], 0).then_inc(setup, 1)
                pool.memset(pad[:, :, 1], FAR).then_inc(setup, 1)
                pool.memset(zero[:, :], 0.0).then_inc(setup, 1)
                pool.iota(gnum[:, :], pattern=[[GH, 2]], base=0, channel_multiplier=1,
                          allow_small_or_imprecise_dtypes=True).then_inc(setup, 1)

            @block.vector
            def _(v):
                k = Chain(v, chain, 0)
                v.wait_ge(loaded, 48)
                v.tensor_copy(pairs[:, :, 0], ends[:, 0, :]).then_inc(joined, 1)
                v.tensor_copy(pairs[:, :, 1], ends[:, 1, :]).then_inc(joined, 1)
                k.link(v.tensor_copy(dstf[:, :], ends[:, 1, :]))
                k.link(v.tensor_copy(next_f[:, :], next_first[:, :]))
                k.link(v.tensor_tensor(wrong[:, 0:1], next_f[:, :], dstf[:, EC - 1:EC], ALU.is_lt))
                k.link(v.tensor_tensor(hit[:, 0:EC - 1], dstf[:, 1:EC], dstf[:, 0:EC - 1], ALU.is_lt))
                k.link(v.tensor_reduce(wrong[:, 1:2], hit[:, 0:EC - 1], AX.X, ALU.max))
                v.memset(cnt[:, 0:1], 0.0).then_inc(counted, 1)
                for t in range(1, NT + 1):
                    k.link(v.tensor_scalar(hit[:, :], dstf[:, :], float(t * P), 0.0, ALU.is_lt, ALU.add,
                                           accum_out=cnt[:, t:t + 1]))
                v.sem_inc(counted, 1)
                v.wait_ge(summed, 1)
                k.link(v.tensor_copy(first[:, :], m.bank[0][:, 0:NT + 1]))
                k.link(v.tensor_copy(unordered[:, :], m.bank[0][0:1, 64:66]))
                k.link(v.tensor_tensor(groups[:, :], first[:, 1:NT + 1], first[:, 0:NT], ALU.subtract))
                k.link(v.tensor_scalar(size_i[:, :], groups[:, :], float(GE - 1), None, ALU.add))
                k.link(v.tensor_scalar(size_i[:, :], size_i[:, :], 8, None, ALU.arith_shift_right))
                k.link(v.tensor_copy(groups[:, :], size_i[:, :]))
                v.wait_ge(setup, 4)
                k.link(v.tensor_tensor_scan(gend[:, :], groups[:, :], zero[:, :], 0.0, ALU.add, ALU.add))
                k.link(v.tensor_copy(base[:, 0:1], first[:, 0:1]))
                k.link(v.scalar_tensor_tensor(base[:, 1:NT + 1], gend[:, :], -float(GE), first[:, 1:NT + 1],
                                              ALU.mult, ALU.add))
                for h in range(2):
                    k.link(v.tensor_scalar(past[:, h, :], gend[:, :], gnum[:, h:h + 1], None, ALU.is_le))
                    k.link(v.tensor_reduce(gt[:, 0, h:h + 1], past[:, h, :], AX.X, ALU.add))
                    k.link(v.tensor_scalar(gt[:, 0, h:h + 1], gt[:, 0, h:h + 1], float(NT - 1), None, ALU.min))
                    k.link(v.tensor_tensor(gcol[:, h, :], base[:, 1:NT + 1], base[:, 0:NT], ALU.subtract))
                    k.link(v.tensor_tensor(gcol[:, h, :], gcol[:, h, :], past[:, h, :], ALU.mult))
                    k.link(v.tensor_reduce(gt[:, 1, h:h + 1], gcol[:, h, :], AX.X, ALU.add))
                    k.link(v.scalar_tensor_tensor(gt[:, 1, h:h + 1], gnum[:, h:h + 1], float(GE), gt[:, 1, h:h + 1],
                                                  ALU.mult, ALU.add))
                    k.link(v.tensor_scalar(gt[:, 1, h:h + 1], gt[:, 1, h:h + 1], float(E), None, ALU.min))
                v.sem_inc(tabled, 1)
                v.wait_ge(turned, 1)
                v.tensor_copy(m.grow[:, :, :, :].rearrange("o h x g -> o (h x g)"),
                              m.bank[1][0:1, 0:512]).then_inc(rows_set, 1)

            @block.tensor
            def _(pe):
                pe.wait_ge(counted, 2)
                pe.matmul(m.bank[0][:, 0:NT + 1], m.ones[0:P, :], cnt[:, :], start=True, stop=True)
                pe.matmul(m.bank[0][:, 64:66], m.ones[0:P, :], wrong[:, :], start=True, stop=True).then_inc(summed, 1)
                pe.wait_ge(tabled, 1)
                for h in range(2):
                    for x in range(2):
                        at = (h * 2 + x) * 128
                        ins = pe.transpose(m.bank[1][0:1, at:at + 128], gt[:, x, h:h + 1], m.ident[:, :])
                ins.then_inc(turned, 1)

        order_edges(nc, m, c, unordered, pairs, dstf, first)


def order_edges(nc, m, c, unordered, pairs, dstf, first):
    def sb(n, s, d=F32):
        return c.enter_context(nc.sbuf_tensor("order_" + n, s, d))

    low = sb("low", [P, NT + 1])
    reached = sb("reached", [P, NT + 1])
    own = sb("own", [P, NT])
    front = sb("front", [P, NT])
    place = sb("place", [P, NT])
    place1 = sb("place1", [P, 1])
    slot = sb("slot", [P, 1], I32)
    pair = sb("pair", [P, 2], I32)
    low_set, chain, owned, ranked, placed, moved, gone, go = [
        c.sem("order_" + n) for n in ("low_set", "chain", "owned", "ranked", "placed", "moved", "gone", "go")]

    def flags(eng):
        _, r = nc.values_load_multi_w_load_instructions(unordered[0:1, 0:2], engines=[eng.engine], min_val=0, max_val=P)
        return r[0] + r[1]

    with nc.Block() as block:
        @block.gpsimd
        def _(pool):
            with pool.If(flags(pool) > 0):
                pool.sem_inc(gone, 1)
                pool.iota(low[:, :], pattern=[[P, NT + 1]], base=0, channel_multiplier=0,
                          allow_small_or_imprecise_dtypes=True).then_inc(low_set, 1)
                with pool.Fori(0, EC) as i:
                    pool.wait_ge(placed, i + 1)
                    pool.sem_inc(go, 1)
                    pool.indirect_dma_start(m.edges, bass.IndirectOffsetOnAxis(ap=slot[:, 0:1], axis=0),
                                            pair[:, :], None).then_inc(moved, 16)
                    pool.wait_ge(moved, i * 16 + 16)
                    pool.sem_inc(gone, 1)

        @block.vector
        def _(v):
            with v.If(flags(v) > 0):
                k = Chain(v, chain, 8)
                v.wait_ge(low_set, 1)
                v.tensor_copy(front[:, :], first[0:P, 0:NT]).then_inc(low_set, 1)
                v.wait_ge(low_set, 2)
                with v.Fori(0, EC) as i:
                    k.step(i)
                    k.link(v.tensor_scalar(reached[:, :], low[:, :], dstf[:, bass.ds(i, 1)], None, ALU.is_le))
                    k.link(v.tensor_tensor(own[:, :], reached[:, 0:NT], reached[:, 1:NT + 1], ALU.subtract))
                    v.sem_inc(owned, 1)
                    v.wait_ge(ranked, i + 1)
                    k.link(v.tensor_tensor(place[:, :], m.bank[2][0:P, 0:NT], front[:, :], ALU.add))
                    k.link(v.tensor_tensor(place[:, :], place[:, :], own[:, :], ALU.mult))
                    k.link(v.tensor_reduce(place1[:, :], place[:, :], AX.X, ALU.add))
                    k.link(v.tensor_tensor(front[:, :], front[:, :], m.bank[2][0:P, 64:64 + NT], ALU.add))
                    v.wait_ge(gone, i + 1)
                    k.link(v.tensor_copy(slot[:, :], place1[:, :]))
                    k.link(v.tensor_copy(pair[:, :], pairs[:, bass.ds(i, 1), :].rearrange("p a x -> p (a x)")))
                    v.sem_inc(placed, 1)
                    k.close()

        @block.tensor
        def _(pe):
            with pe.If(flags(pe) > 0):
                with pe.Fori(0, EC) as i:
                    pe.wait_ge(owned, i + 1)
                    pe.matmul(m.bank[2][0:P, 0:NT], m.before[:, :], own[:, :], start=True, stop=True)
                    pe.matmul(m.bank[2][:, 64:64 + NT], m.ones[0:P, :], own[:, :], start=True, stop=True).then_inc(ranked, 1)


def moments(v, chained, stats, mean, var, half, other):
    k = Chain(v, chained, 0)
    k.link(v.tensor_tensor(mean, stats[:, :, 1], stats[:, :, 4], ALU.add))
    k.link(v.tensor_tensor(half, stats[:, :, 1], stats[:, :, 4], ALU.subtract))
    k.link(v.tensor_scalar(mean, mean, 0.5, None, ALU.mult))
    k.link(v.tensor_scalar(half, half, 0.5, None, ALU.mult))
    k.link(v.tensor_tensor(half, half, half, ALU.mult))
    k.link(v.tensor_tensor(other, stats[:, :, 2], stats[:, :, 5], ALU.add))
    k.link(v.scalar_tensor_tensor(var, other, 1.0 / D, half, ALU.mult, ALU.add))
    k.link(v.tensor_scalar(var, var, EPS, None, ALU.add))


def normalise(nc, m, tag, src):
    with Stage(nc) as c:
        stats = c.enter_context(nc.sbuf_tensor(tag + "_stats", [P, NT, 6], F32))
        half = c.enter_context(nc.sbuf_tensor(tag + "_half", [P, NT], F32))
        other = c.enter_context(nc.sbuf_tensor(tag + "_other", [P, NT], F32))
        stated, meaned, powered = [c.sem(tag + n) for n in ("_stated", "_meaned", "_powered")]
        with nc.Block() as block:
            @block.vector
            def _(v):
                with v.Fori(0, NT // 5) as b:
                    for u in range(5):
                        v.bn_stats(row_of(stats, b * 5 + u), row_of(src, b * 5 + u)).then_inc(stated, 1)
                v.wait_ge(stated, NT)
                moments(v, meaned, stats, m.mean[:, :], m.rstd[:, :], half[:, :], other[:, :])

            @block.gpsimd
            def _(pool):
                pool.wait_ge(meaned, 8)
                pool.tensor_tensor(m.rstd[:, :], m.rstd[:, :], m.half[0:P, 0:NT], ALU.pow).then_inc(powered, 1)
                pool.wait_ge(powered, 1)


def load_x(nc, m, x):
    zrow = 16
    with Stage(nc) as c, nc.sbuf_tensor("zrows", [128, zrow, D], F32) as zrows, nc.Block() as block:
        zeroed, cleared, x_loaded = c.sem("zeroed"), c.sem("cleared"), c.sem("x_loaded")

        @block.vector
        def _(v):
            v.memset(zrows[:, :, :], 0.0).then_inc(zeroed, 1)

        @block.scalar
        def _(a):
            a.wait_ge(zeroed, 1)
            for i in range(NB * ROWS // (128 * zrow)):
                a.dma_start(m.xsort[i * 128 * zrow:(i + 1) * 128 * zrow, :].rearrange("(p w) d -> p w d", p=128),
                            zrows[:, :, :]).then_inc(cleared, 16)
            a.wait_ge(cleared, 16 * (NB * ROWS // (128 * zrow)))


        @block.sync
        def _(sp):
            sp.dma_start(m.xs[:, :, :], x.rearrange("(t p) d -> p t d", p=P)).then_inc(x_loaded, 16)
            sp.wait_ge(x_loaded, 16)


def store_x(nc, m, out):
    with Stage(nc) as c, nc.Block() as block:
        out_stored = c.sem("out_stored")

        @block.sync
        def _(sp):
            sp.dma_start(out.rearrange("(t p) d -> p t d", p=P), m.xs[:, :, :]).then_inc(out_stored, 16)
            sp.wait_ge(out_stored, 16)


def weights0(nc, m, c, w):
    def sb(n, s):
        return c.enter_context(nc.sbuf_tensor(n, s, F32))

    m.nodew = sb("w0_node", [128, KD, D + 2])
    m.gatew = sb("w0_gates", [128, KD, 3 * D])
    m.gbias = sb("w0_gbias", [P, D])
    m.wq = sb("w0_q", [128, KD, D])
    m.wkv = sb("w0_kv", [128, KD, 2 * D])
    m.bq = sb("w0_bq", [128, KD])
    m.bkv = sb("w0_bkv", [P, 2 * D])
    m.lng = sb("w0_lng", [P, 2 * D])
    m.lnb = sb("w0_lnb", [P, 2 * D])
    m.w1 = sb("w0_w1", [128, KD, D])
    m.b1 = sb("w0_b1", [128, KD])
    m.w2 = sb("w0_w2", [128, KD, D])
    m.b2 = sb("w0_b2", [P, D])
    with Stage(nc) as c2:
        wn = c2.enter_context(nc.sbuf_tensor("w0_nat", [128, KD, D], F32))
        an = c2.enter_context(nc.sbuf_tensor("w0_att", [128, KD, 2], F32))
        gn = c2.enter_context(nc.sbuf_tensor("w0_gnat", [128, 6, D], F32))
        loaded, turned, kept = [c2.sem("w0_" + n) for n in ("loaded", "turned", "kept")]
        jobs = [(wn[:, :, :], w["L0_gnn_W"].rearrange("(k p) d -> p k d", p=128)),
                (an[:, :, 0], w["L0_gnn_att_src"].rearrange("(k p) -> p k", p=128)),
                (an[:, :, 1], w["L0_gnn_att_dst"].rearrange("(k p) -> p k", p=128)),
                (gn[:, 0:2, :], w["L0_gnn_W_ih"][0:D, :].rearrange("(k p) d -> p k d", p=128)),
                (gn[:, 2:4, :], w["L0_gnn_W_ih"][3 * D:4 * D, :].rearrange("(k p) d -> p k d", p=128)),
                (gn[:, 4:6, :], w["L0_gnn_W_ih"][2 * D:3 * D, :].rearrange("(k p) d -> p k d", p=128)),
                (m.gbias[:, :], w["L0_gnn_bias"].partition_broadcast(P)),
                (m.w1[:, :, :], w["L0_mix_w1"].rearrange("(k p) d -> p k d", p=128)),
                (m.w2[:, :, :], w["L0_mix_w2"].rearrange("(k p) d -> p k d", p=128)),
                (m.b1[:, :], w["L0_mix_b1"].rearrange("(k p) -> p k", p=128)),
                (m.b2[:, :], w["L0_mix_b2"].partition_broadcast(P))]
        qkv = w["L0_mix_w_qkv"].rearrange("(k p) (h x c) -> k p x h c", p=128, x=3, c=HC)
        bqkv = w["L0_mix_b_qkv"].rearrange("(h x c) -> x h c", x=3, c=HC)
        for k in range(KD):
            jobs.append((m.wq[:, k, :].rearrange("p (h c) -> p h c", c=HC), qkv[k, :, 0]))
            for x in range(2):
                jobs.append((m.wkv[:, k, x * D:(x + 1) * D].rearrange("p (h c) -> p h c", c=HC), qkv[k, :, 1 + x]))
            for h in range(4):
                jobs.append((m.bq[h * HC:(h + 1) * HC, k:k + 1], bqkv[0, 4 * k + h, :].rearrange("(c o) -> c o", o=1)))
        for x in range(2):
            jobs.append((m.bkv[:, x * D:(x + 1) * D].rearrange("p (h c) -> p h c", c=HC), bqkv[1 + x].partition_broadcast(P)))
        for x, (g, b) in enumerate((("kln_g", "kln_b"), ("vln_g", "vln_b"))):
            for t, n in ((m.lng, g), (m.lnb, b)):
                jobs.append((t[:, x * D:(x + 1) * D].rearrange("p (h c) -> p h c", c=HC),
                             w["L0_mix_" + n].rearrange("(o c) -> o c", o=1).to_broadcast([HEADS, HC]).partition_broadcast(P)))
        with nc.Block() as block:
            @block.sync
            def _(sp):
                for dst, src in jobs:
                    sp.dma_start(dst, src).then_inc(loaded, 16)
                sp.wait_ge(loaded, 16 * len(jobs))

            @block.tensor
            def _(pe):
                pe.wait_ge(loaded, 16 * len(jobs))
                for k in range(KD):
                    for h in range(KD):
                        pe.transpose(m.bank[k][:, h * 128:(h + 1) * 128], wn[:, h, k * 128:(k + 1) * 128], m.ident[:, :])
                    for h in range(KD):
                        ins = pe.matmul(m.bank[k][:, D:D + 2], wn[:, h, k * 128:(k + 1) * 128], an[:, h, :],
                                        start=(h == 0), stop=(h == KD - 1))
                    ins.then_inc(turned, 1)
                for k in range(KD):
                    for u in range(6):
                        at = 2 + 2 * k + u // 4
                        ins = pe.transpose(m.bank[at][:, (u % 4) * 128:(u % 4 + 1) * 128], gn[:, u, k * 128:(k + 1) * 128], m.ident[:, :])
                    ins.then_inc(turned, 1)

            @block.vector
            def _(v):
                for k in range(KD):
                    v.wait_ge(turned, k + 1)
                    v.tensor_copy(m.nodew[:, k, :], m.bank[k][:, 0:D + 2]).then_inc(kept, 1)
                for k in range(KD):
                    v.wait_ge(turned, KD + k + 1)
                    v.tensor_copy(m.gatew[:, k, 0:2 * D], m.bank[2 + 2 * k][:, 0:512]).then_inc(kept, 1)
                    v.tensor_copy(m.gatew[:, k, 2 * D:3 * D], m.bank[3 + 2 * k][:, 0:D]).then_inc(kept, 1)


def node_tables(nc, m, tag, H, gate=None):
    W = D + 2 * H
    with Stage(nc) as c:
        def sb(n, s):
            return c.enter_context(nc.sbuf_tensor(tag + n, s, F32))

        def sem(n):
            return c.sem(tag + n)

        shift = sb("_shift", [P, NT])
        xn = sb("_xn", [P, 2, D])
        xst = sb("_xst", [128, 2, KD, P])
        chain, normed, turned, staged, xn_used = sem("_chain"), sem("_normed"), sem("_turned"), sem("_staged"), sem("_xn_used")
        rowed, row_kept, ts_free, stored, chain2 = sem("_rowed"), sem("_row_kept"), sem("_ts_free"), sem("_stored"), sem("_chain2")
        with nc.Block() as block:
            @block.vector
            def _(v):
                v.sem_inc(row_kept, 2)
                v.scalar_tensor_tensor(shift[:, :], m.mean[:, :], -1.0, m.rstd[:, :], ALU.mult, ALU.mult).then_inc(chain, 1)
                v.wait_ge(chain, 1)

                def norm(t, s):
                    v.wait_ge(xn_used, t + 1)
                    v.tensor_scalar(xn[:, s, :], m.xs[:, bass.ds(t, 1), :].rearrange("p a d -> p (a d)"),
                                    m.rstd[:, bass.ds(t, 1)], shift[:, bass.ds(t, 1)], ALU.mult, ALU.add).then_inc(normed, 1)
                    if gate is None:
                        v.wait_ge(normed, t + 1)
                        x_t = m.xs[:, bass.ds(t, 1), :].rearrange("p a d -> p (a d)")
                        v.tensor_tensor(x_t, x_t, xn[:, s, :], ALU.add).then_inc(chain2, 1)

                def keep(t, s):
                    v.wait_ge(rowed, t + 1)
                    v.tensor_copy(m.acc[:, bass.ds(t, 1), 0:W].rearrange("p a d -> p (a d)"),
                                  m.bank[2 + s][0:P, 0:W]).then_inc(row_kept, 1)

                norm(0, 0)
                with v.Fori(0, NT // 2) as b:
                    norm(b * 2 + 1, 1)
                    keep(b * 2, 0)
                    norm(b * 2 + 2, 0)
                    keep(b * 2 + 1, 1)
                keep(NT - 1, 0)

            @block.scalar
            def _(a):
                a.sem_inc(staged, 2)

                def stage(t, s):
                    a.wait_ge(turned, t + 1)
                    a.wait_ge(ts_free, t + 1)
                    turn = m.bank[s][:, 0:256].rearrange("p (k n) -> p k n", k=KD)[:, :, 0:P]
                    a.activation(xst[:, s, :, :], turn, ACT.Copy)
                    a.activation(m.xT[:, :, tile_cols(t)], turn, ACT.Copy).then_inc(staged, 1)

                over_tiles(a, stage)

            @block.tensor
            def _(pe):
                pe.sem_inc(xn_used, 2)
                pe.sem_inc(ts_free, 2)

                def turn(t, s):
                    pe.wait_ge(normed, t + 1)
                    pe.wait_ge(staged, t + 1)
                    for k in range(KD):
                        ins = pe.transpose(m.bank[s][:, k * 128:k * 128 + P], xn[:, s, k * 128:(k + 1) * 128],
                                           m.ident[0:P, 0:P])
                    ins.then_inc(turned, 1)
                    pe.wait_ge(turned, t + 1)
                    pe.sem_inc(xn_used, 1)

                def rows(t, s):
                    pe.wait_ge(staged, t + 3)
                    pe.wait_ge(row_kept, t + 1)
                    for k in range(KD):
                        ins = pe.matmul(m.bank[2 + s][0:P, 0:W], xst[:, s, k, :], m.nodew[:, k, 0:W],
                                        start=(k == 0), stop=(k == KD - 1))
                    ins.then_inc(rowed, 1)
                    pe.wait_ge(rowed, t + 1)
                    pe.sem_inc(ts_free, 1)

                turn(0, 0)
                with pe.Fori(0, NT // 2) as b:
                    turn(b * 2 + 1, 1)
                    rows(b * 2, 0)
                    turn(b * 2 + 2, 0)
                    rows(b * 2 + 1, 1)
                rows(NT - 1, 0)

            @block.sync
            def _(sp):
                sp.wait_ge(row_kept, NT + 2)
                sp.dma_start(m.table[H].rearrange("(t p) w -> p t w", p=P), m.acc[:, :, 0:W]).then_inc(stored, 16)
                sp.wait_ge(stored, 16)


def score_bounds(nc, m, tag, H):
    with Stage(nc) as c:
        def sb(n, s, d=F32):
            return c.enter_context(nc.sbuf_tensor(tag + n, s, d))

        def sem(n):
            return c.sem(tag + n)

        ends = sb("_ends", [P, 2, H])
        all_ends = sb("_all_ends", [P, 2, H])
        spread = sb("_spread", [1, H])
        over = sb("_over", [1, 1])
        far = sb("_far", [1, 1], I32)
        z = sb("_z", [P, NT, H])
        es = sb("_es", [P, NT, H])
        chain, ended, maxed, zed, exped, scaled = [sem(n) for n in ("_chain", "_ended", "_maxed", "_zed", "_exped", "_scaled")]
        asrc, adst = m.acc[:, :, D:D + H], m.acc[:, :, D + H:D + 2 * H]
        adm_a = m.adm[:, :, 0:H]
        adm_m = m.adm[:, :, H:2 * H]
        with nc.Block() as block:
            @block.vector
            def _(v):
                k = Chain(v, chain, 0)
                k.link(v.tensor_reduce(ends[:, 0, :], asrc.rearrange("p t h -> p h t"), AX.X, ALU.max))
                k.link(v.tensor_reduce(ends[:, 1, :], asrc.rearrange("p t h -> p h t"), AX.X, ALU.min))
                v.tensor_scalar(ends[:, 1, :], ends[:, 1, :], -1.0, None, ALU.mult).then_inc(ended, 1)
                k.link(v.tensor_copy(adm_a, adst))
                v.wait_ge(maxed, 1)
                k.link(v.tensor_tensor(spread[:, :], all_ends[0:1, 0, :], all_ends[0:1, 1, :], ALU.add))
                k.link(v.tensor_reduce(over[:, :], spread[:, :], AX.X, ALU.max))
                k.link(v.tensor_scalar(over[:, :], over[:, :], SAFE, None, ALU.is_gt))
                k.link(v.tensor_copy(far[:, :], over[:, :]))
                k.link(v.tensor_tensor(adm_m, adm_a, all_ends[:, 0, :].unsqueeze(1).to_broadcast([P, NT, H]), ALU.add))
                k.link(v.tensor_scalar(z[:, :, :], adm_m, SLOPE, None, ALU.mult))
                k.link(v.tensor_tensor(adm_m, adm_m, z[:, :, :], ALU.max))

            @block.gpsimd
            def _(pool):
                pool.wait_ge(ended, 1)
                pool.partition_all_reduce(all_ends[:, :, :].rearrange("p x h -> p (x h)"),
                                          ends[:, :, :].rearrange("p x h -> p (x h)"), P, MAX).then_inc(maxed, 1)

        own_maxima(nc, m, c, tag, H, far)
        with nc.Block() as block:
            @block.vector
            def _(v):
                if H == 1:
                    k = Chain(v, zed, 0)
                    k.link(v.tensor_tensor(z[:, :, :], asrc, adst, ALU.add))
                    k.link(v.tensor_scalar(es[:, :, :], z[:, :, :], SLOPE, None, ALU.mult))
                    k.link(v.tensor_tensor(z[:, :, :], z[:, :, :], es[:, :, :], ALU.max))
                    v.tensor_tensor(z[:, :, :], z[:, :, :], adm_m, ALU.subtract).then_inc(zed, 1)
                    v.wait_ge(exped, 1)
                    v.tensor_copy(m.acc[:, :, D:D + 1], es[:, :, :])
                    with v.Fori(0, NT // 5) as b:
                        for u in range(5):
                            row = row_of(m.acc[:, :, 0:D], b * 5 + u)
                            v.tensor_scalar(row, row, row_of(es, b * 5 + u), None, ALU.mult)
                else:
                    v.memset(m.acc[:, :, :], 0.0)

            @block.scalar
            def _(a):
                if H == 1:
                    a.wait_ge(zed, 4)
                    a.activation(es[:, :, :], z[:, :, :], ACT.Exp).then_inc(exped, 1)


def own_maxima(nc, m, c, tag, H, far):
    def sb(n, s, d=F32):
        return c.enter_context(nc.sbuf_tensor(tag + "_own" + n, s, d))

    def sem(n):
        return c.sem(tag + "_own" + n)

    edges = sb("_edges", [128, WIN, 2], I32)
    idx = sb("_idx", [128, WIN], I32)
    rows = sb("_rows", [128, WIN, D + 2 * H])
    one = sb("_one", [128, WIN, P])
    push = sb("_push", [P, WIN * 128])
    wide = sb("_wide", [128, WIN, P])
    cand = sb("_cand", [P, WIN * 128])
    top = sb("_top", [P, 1])
    best = sb("_best", [P, NT, H])
    low = sb("_low", [P, NT, H])
    edges_in, chain, hot, turned, fetched, widened, spread, used, go = [
        sem(n) for n in ("_edges_in", "_chain", "_hot", "_turned", "_fetched", "_widened", "_spread", "_used", "_go")]
    adm_a, adm_m = m.adm[:, :, 0:H], m.adm[:, :, H:2 * H]

    def flag(eng):
        _, r = nc.values_load_multi_w_load_instructions(far[0:1, 0:1], engines=[eng.engine], min_val=0, max_val=1)
        return r[0]

    def entry(eng, row, g, most):
        _, r = nc.values_load_multi_w_load_instructions(m.gtab[0:1, row, bass.ds(g, 1)], engines=[eng.engine],
                                                        min_val=0, max_val=most)
        return r[0]

    with nc.Block() as block:
        @block.sync
        def _(sp):
            with sp.If(flag(sp) > 0):
                with sp.Fori(0, NG) as g:
                    e0 = entry(sp, 1, g, E)
                    sp.wait_ge(used, g + 1)
                    sp.dma_start(edges[:, :, :], m.edges[bass.ds(e0, GE), :].rearrange("(p w) x -> p w x", w=WIN)).then_inc(edges_in, 16)

        @block.gpsimd
        def _(pool):
            with pool.If(flag(pool) > 0):
                with pool.Fori(0, NG) as g:
                    pool.wait_ge(hot, g + 1)
                    pool.sem_inc(go, 1)
                    for w in range(WIN):
                        pool.indirect_dma_start(rows[:, w, :], None, m.table[H],
                                                bass.IndirectOffsetOnAxis(ap=idx[:, w:w + 1], axis=0)).then_inc(fetched, 16)

        @block.tensor
        def _(pe):
            with pe.If(flag(pe) > 0):
                with pe.Fori(0, NG) as g:
                    pe.wait_ge(hot, g + 1)
                    for w in range(WIN):
                        ins = pe.transpose(m.bank[0][0:P, w * 128:(w + 1) * 128], one[:, w, :], m.ident[:, :])
                    ins.then_inc(turned, 1)
                    for h in range(H):
                        pe.wait_ge(widened, g * H + (h + 1))
                        for w in range(WIN):
                            ins = pe.matmul(m.bank[1][0:P, w * 128:(w + 1) * 128], wide[:, w, :], m.ident[:, :], start=True, stop=True)
                        ins.then_inc(spread, 1)

        @block.vector
        def _(v):
            with v.If(flag(v) > 0):
                k = Chain(v, chain, 1)
                k.step(0)
                if H == 1:
                    k.link(v.tensor_copy(best[:, :, :], m.acc[:, :, D:D + 1]))
                else:
                    k.link(v.memset(best[:, :, :], -FLOOR))
                v.sem_inc(used, 1)
                k = Chain(v, chain, 1 + WIN + 1 + H * (WIN + 3))
                with v.Fori(0, NG) as g:
                    k.step(g)
                    k.base = k.base + 1
                    tile = entry(v, 0, g, NT - 1)
                    v.wait_ge(edges_in, g * 16 + 16)
                    k.link(v.tensor_copy(idx[:, :], edges[:, :, 0]))
                    for w in range(WIN):
                        k.link(v.tensor_scalar(one[:, w, :], m.nodes[:, bass.ds(tile * P, P)], edges[:, w, 1:2], None, ALU.is_equal))
                    v.sem_inc(hot, 1)
                    v.sem_inc(used, 1)
                    v.wait_ge(turned, g + 1)
                    k.link(v.tensor_scalar(push[:, :], m.bank[0][0:P, 0:WIN * 128], -1.0, FLOOR, ALU.add, ALU.mult))
                    v.wait_ge(fetched, g * (16 * WIN) + 16 * WIN)
                    for h in range(H):
                        for w in range(WIN):
                            k.link(v.tensor_scalar(wide[:, w, :], m.ones[:, 0:P], rows[:, w, D + h:D + h + 1], None, ALU.mult))
                        v.sem_inc(widened, 1)
                        v.wait_ge(spread, g * H + (h + 1))
                        k.link(v.tensor_tensor(cand[:, :], m.bank[1][0:P, 0:WIN * 128], push[:, :], ALU.add))
                        k.link(v.tensor_reduce(top[:, :], cand[:, :], AX.X, ALU.max))
                        mine = row_of(best[:, :, h:h + 1], tile)
                        k.link(v.tensor_tensor(mine, mine, top[:, :], ALU.max))
                    k.close()
                k = Chain(v, used, 3)
                k.base = NG + 1
                k.link(v.tensor_tensor(adm_m, adm_a, best[:, :, :], ALU.add))
                k.link(v.tensor_scalar(low[:, :, :], adm_m, SLOPE, None, ALU.mult))
                k.link(v.tensor_tensor(adm_m, adm_m, low[:, :, :], ALU.max))


def edge_sums(nc, m, tag, H, load_edges):
    W = D + 2 * H
    PW = 2 * WIN
    NP = NG // 2
    NT4 = NP // 4
    with Stage(nc) as c:
        def sb(n, s, d=F32):
            return c.enter_context(nc.sbuf_tensor(tag + n, s, d))

        def sem(n):
            return c.sem(tag + n)

        idx = sb("_idx", [128, 4, PW], I32)
        rows = sb("_rows", [128, 4, PW, W])
        one = sb("_one", [128, 4, PW, P])
        oneT = sb("_oneT", [P, 2, PW * 128])
        stage = sb("_stage", [P, 4, 2, 2 * H])
        msg = sb("_msg", [128, 4, PW, D + H])
        z = sb("_z", [128, 2, PW, H])
        y = sb("_y", [128, 2, PW, H])
        edges_in = [sem(f"_edges_in{s}") for s in range(8)]
        gathered = [sem(f"_gathered{r}") for r in range(4)]
        staged, turned, kept, scored, zed, exped = sem("_staged"), sem("_turned"), sem("_kept"), sem("_scored"), sem("_zed"), sem("_exped")
        numbered = sem("_numbered")
        msged, summed, added, chain, go = sem("_msged"), sem("_summed"), sem("_added"), sem("_chain"), sem("_go")
        turn_bank, score_bank = m.bank[0], m.bank[1]
        sum_banks = [m.bank[2:4], m.bank[4:6]]
        scores_of = score_bank[:, 0:PW * 2 * H].rearrange("p (w x) -> p w x", w=PW)

        def valid(q):
            return not isinstance(q, int) or 0 <= q < NP

        def wait(eng, sem, value):
            if not isinstance(value, int) or value > 0:
                eng.wait_ge(sem, value)

        def rounds(eng, body):
            for u in range(4):
                body(0, u)
            with eng.Fori(1, NT4 - 1) as b:
                for u in range(4):
                    body(b, u)
            for u in range(4):
                body(NT4 - 1, u)
            for u in range(3):
                body(NT4, u)

        with nc.Block() as block:
            if load_edges:
                @block.sync
                def _(sp):
                    def load(b, first):
                        _, e0 = nc.values_load_multi_w_load_instructions(m.gtab[0:1, 1, bass.ds(b * 8, 8)], engines=[sp.engine],
                                                                         min_val=0, max_val=E)
                        for s in range(8):
                            if not first:
                                sp.wait_ge(edges_in[s], b * 16)
                            sp.dma_start(m.eall[:, bass.ds((b * 8 + s) * 4, 4)],
                                         m.edges[bass.ds(e0[s], GE), :].rearrange("(p w) x -> p (w x)", w=WIN)).then_inc(edges_in[s], 16)

                    load(0, True)
                    with sp.Fori(1, NG // 8) as b:
                        load(b, False)
                    for s in range(8):
                        sp.wait_ge(edges_in[s], 16 * (NG // 8))

            @block.gpsimd
            def _(pool):
                with pool.Fori(0, NT4) as b:
                    for r in range(4):
                        q = b * 4 + r
                        pool.wait_ge(numbered, q + 1)
                        pool.wait_ge(msged, q + 1)
                        pool.sem_inc(go, 1)
                        for w in range(PW):
                            pool.indirect_dma_start(rows[:, r, w, :], None, m.table[H],
                                                    bass.IndirectOffsetOnAxis(ap=idx[:, r, w:w + 1], axis=0)).then_inc(gathered[r], 16)

            @block.tensor
            def _(pe):
                def body(b, u):
                    q = b * 4 + u
                    if valid(q):
                        pe.wait_ge(staged, q + 1)
                        wait(pe, kept, q)
                        for w in range(PW):
                            ins = pe.transpose(turn_bank[0:P, w * 128:(w + 1) * 128], one[:, u, w, :], m.ident[:, :])
                        ins.then_inc(turned, 1)
                    q2, r2 = q - 2, (u - 2) % 4
                    if valid(q2):
                        pe.wait_ge(msged, q2 + 5)
                        wait(pe, added, q2 * 2 - 2)
                        for w in range(PW):
                            ins = pe.matmul(sum_banks[r2 % 2][w // WIN][0:P, 0:D + H], one[:, r2, w, :], msg[:, r2, w, :],
                                            start=(w % WIN == 0), stop=(w % WIN == WIN - 1))
                        ins.then_inc(summed, 1)
                    if valid(q):
                        pe.wait_ge(kept, q + 1)
                        wait(pe, zed, q)
                        for w in range(PW):
                            ins = pe.matmul(scores_of[:, w, :], oneT[:, u % 2, w * 128:(w + 1) * 128],
                                            stage[:, u, w // WIN, :], start=True, stop=True)
                        ins.then_inc(scored, 1)

                rounds(pe, body)

            @block.scalar
            def _(a):
                def body(b, u):
                    q = b * 4 + u
                    q2, r2 = q - 2, (u - 2) % 4
                    if valid(q2):
                        a.wait_ge(zed, q2 + 1)
                        a.activation(msg[:, r2, :, D:D + H], z[:, r2 % 2, :, :], ACT.Exp).then_inc(exped, 1)
                    if valid(q):
                        a.wait_ge(turned, q + 1)
                        wait(a, scored, q - 1)
                        a.activation(oneT[:, u % 2, :], turn_bank[0:P, 0:PW * 128], ACT.Copy).then_inc(kept, 1)

                rounds(a, body)

            @block.vector
            def _(v):
                v.sem_inc(msged, 4)

                def number(b, u):
                    if load_edges:
                        for i in range(2):
                            v.wait_ge(edges_in[2 * u + i], b * 16 + 16)
                    v.tensor_copy(idx[:, u, :], m.eall[:, bass.ds((b * 4 + u) * 8, 8)].rearrange("p (w x) -> p w x", x=2)[:, :, 0]).then_inc(numbered, 1)

                number(0, 0)
                number(0, 1)

                def body(b, u):
                    q = b * 4 + u
                    if isinstance(b, int):
                        lo, hi = (0, 8) if b == 0 else (b * 8 - 6, NG)
                        at = lo
                    else:
                        lo, hi, at = -6, 8, b * 8 - 6
                    if u == 0:
                        _, regs = nc.values_load_multi_w_load_instructions(
                            m.gtab[0:1, 0, bass.ds(at, hi - lo)], engines=[v.engine], min_val=0, max_val=NT - 1)
                        v_tiles.clear()
                        first = lo - b * 8 if isinstance(b, int) else lo
                        for n, reg in enumerate(regs):
                            v_tiles[first + n] = reg
                    if valid(q):
                        for i in range(2):
                            g, tile = q * 2 + i, v_tiles[2 * u + i]
                            for w in range(WIN):
                                v.tensor_scalar(one[:, u, 2 * i + w, :], m.nodes[:, bass.ds(tile * P, P)],
                                                m.eall[:, bass.ds(g * 4 + 2 * w + 1, 1)], None, ALU.is_equal)
                            ins = v.tensor_copy(stage[:, u, i, :], m.adm[:, bass.ds(tile, 1), 0:2 * H].rearrange("p a x -> p (a x)"))
                        ins.then_inc(staged, 1)
                    q2, r2 = q - 2, (u - 2) % 4
                    b2 = b if u >= 2 else b - 1
                    if valid(q2):
                        zq, yq = z[:, r2 % 2, :, :], y[:, r2 % 2, :, :]
                        v.wait_ge(scored, q2 + 1)
                        v.wait_ge(gathered[r2], b2 * 16 * PW + 16 * PW)
                    if valid(q + 2):
                        number(b if u < 2 else b + 1, r2)
                    if valid(q2):
                        v.tensor_tensor(zq, rows[:, r2, :, D:D + H], scores_of[:, :, 0:H], ALU.add).then_inc(chain, 1)
                        v.wait_ge(chain, q2 * 3 + 1)
                        v.scalar_tensor_tensor(yq, zq, SLOPE, zq, ALU.mult, ALU.max).then_inc(chain, 1)
                        v.wait_ge(chain, q2 * 3 + 2)
                        v.tensor_tensor(zq, yq, scores_of[:, :, H:2 * H], ALU.subtract).then_inc(chain, 1)
                        v.wait_ge(chain, q2 * 3 + 3)
                        v.tensor_scalar(zq, zq, 0.0, None, ALU.min).then_inc(zed, 1)
                    if valid(q2):
                        v.wait_ge(exped, q2 + 1)
                        for w in range(PW):
                            ins = v.tensor_tensor(msg[:, r2, w, 0:D].rearrange("p (h x) -> p h x", h=H),
                                                  rows[:, r2, w, 0:D].rearrange("p (h x) -> p h x", h=H),
                                                  msg[:, r2, w, D:D + H].unsqueeze(2).to_broadcast([128, H, D // H]), ALU.mult)
                        ins.then_inc(msged, 1)
                    q3, u3 = q - 3, u - 3
                    if valid(q3):
                        for i in range(2):
                            tile = v_tiles[2 * u3 + i]
                            v.wait_ge(summed, q3 + 1)
                            wait(v, added, q3 * 2 + i)
                            acc = m.acc[:, bass.ds(tile, 1), 0:D + H].rearrange("p a x -> p (a x)")
                            v.tensor_tensor(acc, acc, sum_banks[u3 % 2][i][0:P, 0:D + H], ALU.add).then_inc(added, 1)

                v_tiles = {}
                rounds(v, body)
                v.wait_ge(added, 2 * NP)


def graph_attention0(nc, m):
    with Stage(nc) as c:
        def sb(n, s):
            return c.enter_context(nc.sbuf_tensor("cell_" + n, s, F32))

        def sem(n):
            return c.sem("cell_" + n)

        rden = sb("rden", [P, NT])
        hb = sb("hb", [P, 2, D])
        hbT = sb("hbT", [128, 2, KD, P])
        gio = sb("gio", [P, 2, 2 * D])
        gg = sb("gg", [P, 2, D])
        cc = sb("cc", [P, 2, D])
        tc = sb("tc", [P, 2, D])
        inv, agged, tanhed, turned, kept, gated, acted = sem("inv"), sem("agged"), sem("tanhed"), sem("turned"), sem("kept"), sem("gated"), sem("acted")
        celled, ctanhed, hid, addd = sem("celled"), sem("ctanhed"), sem("hid"), sem("addd")
        with nc.Block() as block:
            @block.vector
            def _(v):
                v.reciprocal(rden[:, :], m.acc[:, :, D]).then_inc(inv, 1)
                v.wait_ge(inv, 1)

                def step(t, s):
                    v.scalar_tensor_tensor(hb[:, s, :], m.acc[:, bass.ds(t, 1), 0:D].rearrange("p a d -> p (a d)"),
                                           rden[:, bass.ds(t, 1)], m.gbias[:, :], ALU.mult, ALU.add).then_inc(agged, 1)
                    v.wait_ge(acted, t + 1)
                    v.tensor_tensor(cc[:, s, :], gio[:, s, 0:D], gg[:, s, :], ALU.mult).then_inc(celled, 1)
                    v.wait_ge(ctanhed, t + 1)
                    v.tensor_tensor(cc[:, s, :], gio[:, s, D:2 * D], tc[:, s, :], ALU.mult).then_inc(hid, 1)
                    v.wait_ge(hid, t + 1)
                    x = m.xs[:, bass.ds(t, 1), :].rearrange("p a d -> p (a d)")
                    v.tensor_tensor(x, x, cc[:, s, :], ALU.add).then_inc(addd, 1)

                over_tiles(v, step)

            @block.scalar
            def _(a):
                def step(t, s):
                    a.wait_ge(agged, t + 1)
                    a.activation(hb[:, s, :], hb[:, s, :], ACT.Tanh).then_inc(tanhed, 1)
                    a.wait_ge(turned, t + 1)
                    a.activation(hbT[:, s, :, :], m.bank[s][:, 0:256].rearrange("p (k n) -> p k n", k=KD)[:, :, 0:P],
                                 ACT.Copy).then_inc(kept, 1)
                    a.wait_ge(gated, t + 1)
                    a.activation(gio[:, s, :], m.bank[2 + 2 * s][0:P, 0:2 * D], ACT.Sigmoid)
                    a.activation(gg[:, s, :], m.bank[3 + 2 * s][0:P, 0:D], ACT.Tanh).then_inc(acted, 1)
                    a.wait_ge(celled, t + 1)
                    a.activation(tc[:, s, :], cc[:, s, :], ACT.Tanh).then_inc(ctanhed, 1)

                over_tiles(a, step)

            @block.tensor
            def _(pe):
                def step(t, s):
                    pe.wait_ge(tanhed, t + 1)
                    for k in range(KD):
                        ins = pe.transpose(m.bank[s][:, k * 128:k * 128 + P], hb[:, s, k * 128:(k + 1) * 128], m.ident[0:P, 0:P])
                    ins.then_inc(turned, 1)
                    pe.wait_ge(kept, t + 1)
                    for k in range(KD):
                        pe.matmul(m.bank[2 + 2 * s][0:P, 0:2 * D], hbT[:, s, k, :], m.gatew[:, k, 0:2 * D], start=(k == 0), stop=(k == KD - 1))
                    for k in range(KD):
                        ins = pe.matmul(m.bank[3 + 2 * s][0:P, 0:D], hbT[:, s, k, :], m.gatew[:, k, 2 * D:3 * D], start=(k == 0), stop=(k == KD - 1))
                    ins.then_inc(gated, 1)

                over_tiles(pe, step)


def mix0_keys(nc, m):
    G = 2 * HEADS
    with Stage(nc) as c:
        def sb(n, s):
            return c.enter_context(nc.sbuf_tensor("keys_" + n, s, F32))

        def sem(n):
            return c.sem("keys_" + n)

        xst = sb("xst", [128, 2, KD, P])
        kv = sb("kv", [P, 2, 2 * D])
        sq = sb("sq", [P, 2, 2 * D])
        mu = sb("mu", [P, 2, G])
        var = sb("var", [P, 2, G])
        rs = sb("rs", [P, 2, G])
        zeros = sb("zeros", [P, 128])
        xstaged, made, chain, squared, varred, powered, normed, summed, zeroed, done = [
            sem(n) for n in ("staged", "made", "chain", "squared", "varred", "powered", "normed", "summed", "zeroed", "done")]
        norm_chain, kept = sem("norm_chain"), sem("kept")
        with nc.Block() as block:
            @block.scalar
            def _(a):
                def body(t, s):
                    if valid(t):
                        wait_count(a, made, t - 1)
                        a.activation(xst[:, s, :, :], m.xT[:, :, tile_cols(t)], ACT.Copy).then_inc(xstaged, 1)
                    if valid(t - 1):
                        a.wait_ge(chain, (t - 1) * 4 + 4)
                        a.activation(sq[:, 1 - s, :], kv[:, 1 - s, :], ACT.Square).then_inc(squared, 1)

                pipelined(a, body, 1)

            @block.tensor
            def _(pe):
                pe.wait_ge(zeroed, 1)
                pe.matmul(m.bank[2][:, 0:D], zeros[:, :], zeros[:, :].unsqueeze(1).to_broadcast([P, KD, 128]), start=True, stop=False)

                def body(t, s):
                    if valid(t):
                        pe.wait_ge(xstaged, t + 1)
                        wait_count(pe, chain, (t - 2) * 4 + 1)
                        for k in range(KD):
                            ins = pe.matmul(m.bank[s][0:P, :], xst[:, s, k, :], m.wkv[:, k, :], start=(k == 0), stop=(k == KD - 1))
                        ins.then_inc(made, 1)
                    if valid(t - 1):
                        pe.wait_ge(normed, t)
                        for k in range(KD):
                            ins = pe.matmul(m.bank[2][:, k * 128:(k + 1) * 128], kv[:, 1 - s, k * 128:(k + 1) * 128],
                                            kv[:, 1 - s, D + k * 128:D + (k + 1) * 128], start=False, stop=False, skip_group_check=True)
                        ins.then_inc(summed, 1)

                pipelined(pe, body, 1)
                pe.matmul(m.bank[2][:, 0:D], zeros[:, :], zeros[:, :].unsqueeze(1).to_broadcast([P, KD, 128]),
                          start=False, stop=True).then_inc(summed, 1)

            @block.gpsimd
            def _(pool):
                def body(t, s):
                    pool.wait_ge(varred, t + 1)
                    pool.tensor_tensor(rs[:, s, :], var[:, s, :], m.half[0:P, 0:G], ALU.pow).then_inc(powered, 1)

                pipelined(pool, body, 0)

            @block.vector
            def _(v):
                v.memset(zeros[:, :], 0.0).then_inc(zeroed, 1)

                def grouped(x):
                    return x.rearrange("p (g c) -> p g c", c=HC)

                def spread(x):
                    return x.unsqueeze(2).to_broadcast([P, G, HC])

                k = Chain(v, chain, 4)

                def body(t, s):
                    if valid(t - 1):
                        v.wait_ge(squared, t)
                        v.tensor_reduce(mu[:, 1 - s, :], grouped(sq[:, 1 - s, :]), AX.X, ALU.add).then_inc(done, 1)
                        v.wait_ge(done, t)
                        v.tensor_scalar(var[:, 1 - s, :], mu[:, 1 - s, :], 1.0 / HC, EPS, ALU.mult, ALU.add).then_inc(varred, 1)
                    if valid(t):
                        k.step(t)
                        v.wait_ge(made, t + 1)
                        wait_count(v, summed, t - 1)
                        k.link(v.tensor_tensor(kv[:, s, :], m.bank[s][0:P, :], m.bkv[:, :], ALU.add))
                        k.link(v.tensor_reduce(mu[:, s, :], grouped(kv[:, s, :]), AX.X, ALU.add))
                        k.link(v.tensor_scalar(mu[:, s, :], mu[:, s, :], 1.0 / HC, None, ALU.mult))
                        k.link(v.tensor_tensor(grouped(kv[:, s, :]), grouped(kv[:, s, :]), spread(mu[:, s, :]), ALU.subtract))
                        k.close()
                    if valid(t - 1):
                        o = 1 - s
                        v.wait_ge(powered, t)
                        v.tensor_tensor(grouped(kv[:, o, :]), grouped(kv[:, o, :]), spread(rs[:, o, :]), ALU.mult).then_inc(norm_chain, 1)
                        v.wait_ge(norm_chain, t * 2 - 1)
                        v.tensor_tensor(kv[:, o, :], kv[:, o, :], m.lng[:, :], ALU.mult).then_inc(norm_chain, 1)
                        v.wait_ge(norm_chain, t * 2)
                        v.tensor_tensor(kv[:, o, :], kv[:, o, :], m.lnb[:, :], ALU.add).then_inc(normed, 1)

                pipelined(v, body, 1)
                v.wait_ge(summed, NT + 1)
                v.tensor_scalar(m.kv[:, :, :].rearrange("p k n -> p (k n)"), m.bank[2][:, 0:D], 1.0 / N, None, ALU.mult).then_inc(kept, 1)
                v.wait_ge(kept, 1)
                v.tensor_tensor(m.kv[:, :, :], m.kv[:, :, :], m.headmask[:, :].unsqueeze(1).to_broadcast([128, KD, 128]), ALU.mult)


def mix0_queries(nc, m):
    with Stage(nc) as c:
        def sb(n, s):
            return c.enter_context(nc.sbuf_tensor("query_" + n, s, F32))

        def sem(n):
            return c.sem("query_" + n)

        qT = sb("qT", [128, 2, KD, P])
        ret = sb("ret", [128, 2, KD, P])
        queried, qkept, mixed, returned, hidden, hkept = [sem(n) for n in ("queried", "qkept", "mixed", "returned", "hidden", "hkept")]
        with nc.Block() as block:
            @block.tensor
            def _(pe):
                def body(t, s):
                    if valid(t):
                        wait_count(pe, qkept, t - 1)
                        for o in range(KD):
                            for k in range(KD):
                                ins = pe.matmul(m.bank[s][:, o * 128:o * 128 + P], m.wq[:, k, o * 128:(o + 1) * 128],
                                                m.xT[:, k, tile_cols(t)], start=(k == 0), stop=(k == KD - 1))
                        ins.then_inc(queried, 1)
                    if valid(t - 1):
                        pe.wait_ge(qkept, t)
                        wait_count(pe, returned, t - 2)
                        for k in range(KD):
                            ins = pe.matmul(m.bank[3 - s][:, k * 128:k * 128 + P], m.kv[:, k, :], qT[:, 1 - s, k, :], start=True, stop=True)
                        ins.then_inc(mixed, 1)
                    if valid(t - 2):
                        pe.wait_ge(returned, t - 1)
                        wait_count(pe, hkept, t - 3)
                        for o in range(KD):
                            for k in range(KD):
                                ins = pe.matmul(m.bank[4 + s][:, o * 128:o * 128 + P], m.w1[:, k, o * 128:(o + 1) * 128],
                                                ret[:, s, k, :], start=(k == 0), stop=(k == KD - 1))
                        ins.then_inc(hidden, 1)

                pipelined(pe, body, 2)

            @block.scalar
            def _(a):
                def body(t, s):
                    if valid(t):
                        a.wait_ge(queried, t + 1)
                        wait_count(a, mixed, t - 1)
                        for k in range(KD):
                            ins = a.activation(qT[:, s, k, :], m.bank[s][:, k * 128:k * 128 + P], ACT.Identity, bias=m.bq[:, k:k + 1])
                        ins.then_inc(qkept, 1)
                    if valid(t - 2):
                        a.wait_ge(hidden, t - 1)
                        a.activation(m.xT[:, :, tile_cols(t - 2)], by_feature(m.bank[4 + s]), ACT.Copy).then_inc(hkept, 1)

                pipelined(a, body, 2)

            @block.vector
            def _(v):
                def body(t, s):
                    v.wait_ge(mixed, t + 1)
                    wait_count(v, hidden, t - 1)
                    v.tensor_tensor(ret[:, s, :, :], by_feature(m.bank[2 + s]), m.xT[:, :, tile_cols(t)], ALU.add).then_inc(returned, 1)

                pipelined(v, body, 0)


def mix0_out(nc, m):
    with Stage(nc) as c:
        def sb(n, s):
            return c.enter_context(nc.sbuf_tensor("mixout_" + n, s, F32))

        def sem(n):
            return c.sem("mixout_" + n)

        hT = sb("hT", [128, 2, KD, P])
        bent, made, biased, added = [sem(n) for n in ("bent", "made", "biased", "added")]
        with nc.Block() as block:
            @block.scalar
            def _(a):
                def body(t, s):
                    wait_count(a, made, t - 1)
                    for k in range(KD):
                        ins = a.activation(hT[:, s, k, :], m.xT[:, k, tile_cols(t)], ACT.Gelu, bias=m.b1[:, k:k + 1])
                    ins.then_inc(bent, 1)

                pipelined(a, body, 0)

            @block.tensor
            def _(pe):
                def body(t, s):
                    pe.wait_ge(bent, t + 1)
                    wait_count(pe, added, t - 1)
                    for k in range(KD):
                        ins = pe.matmul(m.bank[s][0:P, 0:D], hT[:, s, k, :], m.w2[:, k, :], start=(k == 0), stop=(k == KD - 1))
                    ins.then_inc(made, 1)

                pipelined(pe, body, 0)

            @block.vector
            def _(v):
                def body(t, s):
                    x = row_of(m.xs, t)
                    v.tensor_tensor(x, x, m.b2[:, :], ALU.add).then_inc(biased, 1)
                    v.wait_ge(biased, t + 1)
                    v.wait_ge(made, t + 1)
                    v.tensor_tensor(x, x, m.bank[s][0:P, 0:D], ALU.add).then_inc(added, 1)

                pipelined(v, body, 0)


def experts_route(nc, m, tag, gw, gb, weighted):
    with Stage(nc) as c:
        def sb(n, s, d=F32):
            return c.enter_context(nc.sbuf_tensor(tag + n, s, d))

        def sem(n):
            return c.sem(tag + n)

        gws = sb("_gws", [128, KD, NE])
        gbs = sb("_gbs", [P, NE])
        shift = sb("_shift", [P, NT])
        xn = sb("_xn", [P, 2, D])
        xst = sb("_xst", [128, 2, KD, P])
        lg = sb("_lg", [P, NT, NE])
        ie = sb("_ie", [128, NE])
        jn = sb("_jn", [128, 1])
        loaded, chain, normed, turned, staged, logged, kept, numbered, copied = [
            sem(n) for n in ("_loaded", "_chain", "_normed", "_turned", "_staged", "_logged", "_kept", "_numbered", "_copied")]
        with nc.Block() as block:
            @block.sync
            def _(sp):
                sp.dma_start(gws[:, :, :], gw.rearrange("(k p) e -> p k e", p=128)).then_inc(loaded, 16)
                sp.dma_start(gbs[:, :], gb.partition_broadcast(P)).then_inc(loaded, 16)

            @block.gpsimd
            def _(pool):
                pool.iota(ie[:, :], pattern=[[1, NE]], base=0, channel_multiplier=0,
                          allow_small_or_imprecise_dtypes=True).then_inc(numbered, 1)
                pool.iota(jn[:, :], pattern=[[0, 1]], base=0, channel_multiplier=1,
                          allow_small_or_imprecise_dtypes=True).then_inc(numbered, 1)

                def body(t, s):
                    pool.wait_ge(normed, t + 1)
                    pool.tensor_copy(m.acc[:, bass.ds(t, 1), 0:D].rearrange("p a d -> p (a d)"), xn[:, s, :]).then_inc(copied, 1)

                pipelined(pool, body, 0)

            @block.vector
            def _(v):
                v.scalar_tensor_tensor(shift[:, :], m.mean[:, :], -1.0, m.rstd[:, :], ALU.mult, ALU.mult).then_inc(chain, 1)
                v.wait_ge(chain, 1)
                v.wait_ge(loaded, 32)

                def body(t, s):
                    if valid(t):
                        wait_count(v, turned, t - 1)
                        wait_count(v, copied, t - 1)
                        v.tensor_scalar(xn[:, s, :], row_of(m.xs, t), m.rstd[:, bass.ds(t, 1)], shift[:, bass.ds(t, 1)],
                                        ALU.mult, ALU.add).then_inc(normed, 1)
                    if valid(t - 1):
                        v.wait_ge(logged, t)
                        v.tensor_tensor(row_of(lg, t - 1), m.bank[3 - s][0:P, 0:NE], gbs[:, :], ALU.add).then_inc(kept, 1)

                pipelined(v, body, 1)

            @block.tensor
            def _(pe):
                pe.wait_ge(loaded, 32)

                def body(t, s):
                    if valid(t):
                        pe.wait_ge(normed, t + 1)
                        wait_count(pe, staged, t - 1)
                        for k in range(KD):
                            ins = pe.transpose(m.bank[s][:, k * 128:k * 128 + P], xn[:, s, k * 128:(k + 1) * 128], m.ident[0:P, 0:P])
                        ins.then_inc(turned, 1)
                    if valid(t - 1):
                        pe.wait_ge(staged, t)
                        wait_count(pe, kept, t - 2)
                        for k in range(KD):
                            ins = pe.matmul(m.bank[3 - s][0:P, 0:NE], xst[:, 1 - s, k, :], gws[:, k, :], start=(k == 0), stop=(k == KD - 1))
                        ins.then_inc(logged, 1)

                pipelined(pe, body, 1)

            @block.scalar
            def _(a):
                def body(t, s):
                    a.wait_ge(turned, t + 1)
                    wait_count(a, logged, t - 1)
                    a.activation(xst[:, s, :, :], by_feature(m.bank[s]), ACT.Copy).then_inc(staged, 1)

                pipelined(a, body, 0)

        one = [sb(f"_one{i}", [P, NT, NE]) for i in range(2)]
        eq = sb("_eq", [P, NT, NE])
        mask = sb("_mask", [P, NT, NE])
        best = sb("_best", [P, 2, NT])
        low = sb("_low", [P, NT])
        ex = sb("_ex", [P, NT, NE])
        e2 = sb("_e2", [P, NT])
        zsum = sb("_zsum", [P, NT])
        tot = sb("_tot", [128, NT, NE])
        incl = sb("_incl", [128, NE, NT])
        excl = sb("_excl", [128, NT, NE])
        zero = sb("_zero", [128, NT])
        placef = sb("_placef", [P, 2, NT])
        nbi = sb("_nbi", [128, NE], I32)
        nb = sb("_nb", [128, NE])
        bend = sb("_bend", [128, NE])
        past = sb("_past", [128, NE])
        bt = sb("_bt", [128, 1])
        masked, exped, counted, tabled, turned2, c2 = [sem(n) for n in ("_masked", "_exped", "_counted", "_tabled", "_turned2", "_chain2")]

        def over(x):
            return x.unsqueeze(2).to_broadcast([P, NT, NE])

        with nc.Block() as block:
            @block.vector
            def _(v):
                k = Chain(v, c2, 0)
                src = lg
                for i in range(2):
                    k.link(v.tensor_reduce(best[:, i, :], src[:, :, :], AX.X, ALU.max))
                    k.link(v.tensor_tensor(eq[:, :, :], src[:, :, :], over(best[:, i, :]), ALU.is_equal))
                    k.link(v.tensor_scalar(eq[:, :, :], eq[:, :, :], -100.0, None, ALU.mult))
                    k.link(v.tensor_tensor(eq[:, :, :], eq[:, :, :], ie[0:P, :].unsqueeze(1).to_broadcast([P, NT, NE]), ALU.add))
                    k.link(v.tensor_reduce(low[:, :], eq[:, :, :], AX.X, ALU.min))
                    k.link(v.tensor_tensor(one[i][:, :, :], eq[:, :, :], over(low[:, :]), ALU.is_equal))
                    if i == 0:
                        k.link(v.scalar_tensor_tensor(mask[:, :, :], one[0][:, :, :], -BIG, lg[:, :, :], ALU.mult, ALU.add))
                        src = mask
                k.link(v.tensor_tensor(mask[:, :, :], one[0][:, :, :], one[1][:, :, :], ALU.add))
                if weighted:
                    k.link(v.tensor_tensor(ex[:, :, :], lg[:, :, :], over(best[:, 0, :]), ALU.subtract))
                    k.link(v.tensor_tensor(e2[:, :], best[:, 1, :], best[:, 0, :], ALU.subtract))
                v.sem_inc(masked, 1)
                if weighted:
                    v.wait_ge(exped, 2)
                    k.link(v.tensor_reduce(zsum[:, :], ex[:, :, :], AX.X, ALU.add))
                    k.link(v.reciprocal(m.cw[:, 0, :], zsum[:, :]))
                    k.link(v.tensor_tensor(m.cw[:, 1, :], m.cw[:, 0, :], e2[:, :], ALU.mult))
                k.link(v.memset(zero[:, :], 0.0))
                v.wait_ge(counted, 1)
                k.link(v.tensor_copy(tot[:, :, :].rearrange("p t e -> p (t e)"), m.bank[1][:, 0:NT * NE]))
                for e in range(NE):
                    k.link(v.tensor_tensor_scan(incl[:, e, :], tot[:, :, e], zero[:, :], 0.0, ALU.add, ALU.add))
                k.link(v.tensor_tensor(excl[:, :, :], incl[:, :, :].rearrange("p e t -> p t e"), tot[:, :, :], ALU.subtract))
                k.link(v.tensor_scalar(nbi[:, :], incl[:, :, NT - 1], float(ROWS - 1), None, ALU.add))
                k.link(v.tensor_scalar(nbi[:, :], nbi[:, :], 8, None, ALU.arith_shift_right))
                k.link(v.tensor_copy(nb[:, :], nbi[:, :]))
                k.link(v.tensor_tensor_scan(bend[:, :], nb[:, :], zero[:, 0:NE], 0.0, ALU.add, ALU.add))
                k.link(v.tensor_tensor(past[:, :], bend[:, :], nb[:, :], ALU.subtract))
                k.link(v.tensor_scalar(past[:, :], past[:, :], float(ROWS), None, ALU.mult))
                k.link(v.tensor_tensor(excl[:, :, :], excl[:, :, :], past[:, :].unsqueeze(1).to_broadcast([128, NT, NE]), ALU.add))
                k.link(v.tensor_tensor(eq[:, :, :].rearrange("p t e -> p (t e)"), m.bank[0][0:P, 0:NT * NE],
                                       excl[0:P, :, :].rearrange("p t e -> p (t e)"), ALU.add))
                for i in range(2):
                    k.link(v.tensor_tensor(mask[:, :, :], eq[:, :, :], one[i][:, :, :], ALU.mult))
                    k.link(v.tensor_reduce(placef[:, i, :], mask[:, :, :], AX.X, ALU.add))
                    k.link(v.tensor_copy(m.slots[:, :, i], placef[:, i, :]))
                k.link(v.tensor_scalar(past[:, :], bend[:, :], jn[:, 0:1], None, ALU.is_le))
                k.link(v.tensor_reduce(bt[:, 0:1], past[:, :], AX.X, ALU.add))
                k.link(v.tensor_scalar(bt[:, 0:1], bt[:, 0:1], float(NE - 1), None, ALU.min))
                v.sem_inc(tabled, 1)
                v.wait_ge(turned2, 1)
                k.link(v.tensor_copy(m.btab[:, :], m.bank[2][0:1, 0:NB]))

            @block.scalar
            def _(a):
                if weighted:
                    a.wait_ge(masked, 1)
                    a.activation(ex[:, :, :], ex[:, :, :], ACT.Exp).then_inc(exped, 1)
                    a.activation(e2[:, :], e2[:, :], ACT.Exp).then_inc(exped, 1)

            @block.tensor
            def _(pe):
                pe.wait_ge(masked, 1)
                flat = mask[:, :, :].rearrange("p t e -> p (t e)")
                pe.matmul(m.bank[0][0:P, 0:NT * NE], m.before[:, :], flat, start=True, stop=True)
                pe.matmul(m.bank[1][:, 0:NT * NE], m.ones[0:P, :], flat, start=True, stop=True).then_inc(counted, 1)
                pe.wait_ge(tabled, 1)
                pe.transpose(m.bank[2][0:1, 0:128], bt[:, 0:1], m.ident[:, :]).then_inc(turned2, 1)


def experts_scatter(nc, m, tag):
    with Stage(nc) as c:
        scattered = c.sem(tag + "_scattered")
        with nc.Block() as block:
            @block.gpsimd
            def _(pool):
                for t in range(NT):
                    for i in range(2):
                        pool.indirect_dma_start(m.xsort, bass.IndirectOffsetOnAxis(ap=m.slots[:, t, i:i + 1], axis=0),
                                                m.acc[:, t, 0:D], None).then_inc(scattered, 16)
                pool.wait_ge(scattered, 16 * 2 * NT)


def experts_run(nc, m, tag, W1, b1, W2, b2):
    RW = ROWS // 128
    S = 4
    with Stage(nc) as c:
        def sb(n, s):
            return c.enter_context(nc.sbuf_tensor(tag + n, s, F32))

        def sem(n):
            return c.sem(tag + n)

        xb = sb("_xb", [128, S, RW, D])
        w1 = sb("_w1", [128, S, KD, HID])
        w2 = sb("_w2", [128, S, KH, D])
        b1s = sb("_b1s", [128, S, KH])
        b2s = sb("_b2s", [128, S, D])
        xbT = sb("_xbT", [128, 2, KD, ROWS])
        hT = sb("_hT", [128, 2, KH, ROWS])
        y = sb("_y", [128, 2, RW, D])
        b1t = sb("_b1t", [128, NE, KH])
        b1n = sb("_b1n", [NE * KH, 128])
        loads = [sem(f"_loads{s}") for s in range(S)]
        stored = [sem(f"_stored{s}") for s in range(2)]
        b1_in, b1_turned, b1_kept = sem("_b1_in"), sem("_b1_turned"), sem("_b1_kept")
        turned, staged, hidden, bent, made, summed = [sem(n) for n in ("_turned", "_staged", "_hidden", "_bent", "_made", "_summed")]
        turn_banks, hidden_banks, out_banks = (m.bank[0], m.bank[7]), (m.bank[1:3], m.bank[3:5]), m.bank[5:7]
        LOADS = 5

        def ok(j):
            return not isinstance(j, int) or 0 <= j < NB

        def blocks(eng, body, lag):
            for u in range(S):
                body(0, u)
            with eng.Fori(1, NB // S) as b:
                for u in range(S):
                    body(b, u)
            for u in range(lag):
                body(NB // S, u)

        assert NB % S == 0
        with nc.Block() as block:
            @block.sync
            def _(sp):
                sp.dma_start(b1n[:, :], b1.rearrange("e (k p) -> (e k) p", p=128)).then_inc(b1_in, 16)

                def load(j, s, e):
                    sp.dma_start(xb[:, s, :, :], m.xsort[bass.ds(j * ROWS, ROWS), :].rearrange("(p w) d -> p w d", p=128)).then_inc(loads[s], 16)
                    sp.dma_start(w1[:, s, :, :], W1[bass.ds(e, 1), :, :].rearrange("a (k p) h -> p (a k) h", p=128)).then_inc(loads[s], 16)
                    sp.dma_start(w2[:, s, :, :], W2[bass.ds(e, 1), :, :].rearrange("a (k p) d -> p (a k) d", p=128)).then_inc(loads[s], 16)
                    sp.dma_start(b1s[:, s, :], b1t[:, bass.ds(e, 1), :].rearrange("p a k -> p (a k)")).then_inc(loads[s], 16)
                    sp.dma_start(b2s[:, s, :], b2[bass.ds(e, 1), :].rearrange("a d -> (a d)").partition_broadcast(128)).then_inc(loads[s], 16)

                def store(j, s):
                    sp.wait_ge(summed, j + 1)
                    sp.dma_start(m.ysort[bass.ds(j * ROWS, ROWS), :].rearrange("(p w) d -> p w d", p=128), y[:, s, :, :]).then_inc(stored[s], 16)

                def experts_of(at):
                    _, e = nc.values_load_multi_w_load_instructions(m.btab[0:1, bass.ds(at, S)], engines=[sp.engine], min_val=0, max_val=NE - 1)
                    return e

                e = experts_of(0)
                sp.wait_ge(b1_kept, 1)
                for s in range(S):
                    load(s, s, e[s])
                with sp.Fori(0, NB // S - 1) as b:
                    e = experts_of(b * S + S)
                    for s in range(S):
                        store(b * S + s, s % 2)
                        load(b * S + S + s, s, e[s])
                for s in range(S):
                    store(NB - S + s, s % 2)
                for s in range(2):
                    sp.wait_ge(stored[s], 16 * NB // 2)

            @block.tensor
            def _(pe):
                pe.wait_ge(b1_in, 16)
                pe.transpose(m.bank[0][:, 0:NE * KH], b1n[:, :], m.ident[0:NE * KH, 0:NE * KH]).then_inc(b1_turned, 1)
                pe.wait_ge(b1_kept, 1)

                def body(b, u):
                    j = b * S + u
                    s = u % 2
                    if ok(j):
                        pe.wait_ge(loads[u], b * (16 * LOADS) + 16 * LOADS)
                        wait_count(pe, staged, j - 1)
                        for w in range(RW):
                            for k in range(KD):
                                at = k * ROWS + w * 128
                                ins = pe.transpose(turn_banks[s][:, at:at + 128], xb[:, u, w, k * 128:(k + 1) * 128], m.ident[:, :])
                        ins.then_inc(turned, 1)
                    if ok(j - 1):
                        u1, s1 = (u - 1) % S, 1 - s
                        pe.wait_ge(staged, j)
                        wait_count(pe, bent, j - 2)
                        for h in range(KH):
                            for k in range(KD):
                                ins = pe.matmul(hidden_banks[s1][h // 2][:, (h % 2) * ROWS:(h % 2 + 1) * ROWS],
                                                w1[:, u1, k, h * 128:(h + 1) * 128], xbT[:, s1, k, :],
                                                start=(k == 0), stop=(k == KD - 1))
                        ins.then_inc(hidden, 1)
                    if ok(j - 2):
                        u2 = (u - 2) % S
                        pe.wait_ge(bent, j - 1)
                        wait_count(pe, summed, j - 3)
                        for w in range(RW):
                            for h in range(KH):
                                ins = pe.matmul(out_banks[s][:, w * D:(w + 1) * D], hT[:, s, h, w * 128:(w + 1) * 128], w2[:, u2, h, :],
                                                start=(h == 0), stop=(h == KH - 1))
                        ins.then_inc(made, 1)

                blocks(pe, body, 2)

            @block.scalar
            def _(a):
                def body(b, u):
                    j, s = b * S + u, u % 2
                    a.wait_ge(hidden, j + 1)
                    wait_count(a, made, j - 1)
                    for h in range(KH):
                        ins = a.activation(hT[:, s, h, :], hidden_banks[s][h // 2][:, (h % 2) * ROWS:(h % 2 + 1) * ROWS], ACT.Gelu,
                                           bias=b1s[:, u, h:h + 1])
                    ins.then_inc(bent, 1)

                blocks(a, body, 0)

            @block.vector
            def _(v):
                v.wait_ge(b1_turned, 1)
                v.tensor_copy(b1t[:, :, :].rearrange("p e k -> p (e k)"), m.bank[0][:, 0:NE * KH]).then_inc(b1_kept, 1)

                def body(b, u):
                    j, s = b * S + u, u % 2
                    if ok(j):
                        v.wait_ge(turned, j + 1)
                        wait_count(v, hidden, j - 1)
                        v.tensor_copy(xbT[:, s, :, :].rearrange("p k n -> p (k n)"), turn_banks[s][:, :]).then_inc(staged, 1)
                    if ok(j - 2):
                        u2 = (u - 2) % S
                        v.wait_ge(made, j - 1)
                        wait_count(v, stored[s], b * 32 + (u // 2 - 1) * 16)
                        v.tensor_tensor(y[:, s, :, :], out_banks[s][:, :].rearrange("p (w d) -> p w d", w=RW),
                                        b2s[:, u2, :].unsqueeze(1).to_broadcast([128, RW, D]), ALU.add).then_inc(summed, 1)

                blocks(v, body, 2)


def experts_combine(nc, m, tag, weighted):
    R = 5
    with Stage(nc) as c:
        y = c.enter_context(nc.sbuf_tensor(tag + "_yy", [P, R, 2, D], F32))
        fetched = [c.sem(f"{tag}_fetched{r}") for r in range(R)]
        used, half = [c.sem(tag + n) for n in ("_used", "_halfway")]
        with nc.Block() as block:
            @block.gpsimd
            def _(pool):
                for t in range(NT):
                    if t >= R:
                        pool.wait_ge(used, t - R + 1)
                    for i in range(2):
                        pool.indirect_dma_start(y[:, t % R, i, :], None, m.ysort,
                                                bass.IndirectOffsetOnAxis(ap=m.slots[:, t, i:i + 1], axis=0)).then_inc(fetched[t % R], 16)

            @block.vector
            def _(v):
                with v.Fori(0, NT // R) as b:
                    for r in range(R):
                        t = b * R + r
                        x = row_of(m.xs, t)
                        v.wait_ge(fetched[r], b * 32 + 32)
                        for i, done in ((0, half), (1, used)):
                            if weighted:
                                v.scalar_tensor_tensor(x, y[:, r, i, :], m.cw[:, i, bass.ds(t, 1)], x, ALU.mult, ALU.add).then_inc(done, 1)
                            else:
                                v.tensor_tensor(x, x, y[:, r, i, :], ALU.add).then_inc(done, 1)
                            if i == 0:
                                v.wait_ge(half, t + 1)


def experts(nc, m, tag, gw, gb, W1, b1, W2, b2, weighted):
    normalise(nc, m, tag + "_ln", m.xs)
    experts_route(nc, m, tag + "_route", gw, gb, weighted)
    experts_scatter(nc, m, tag + "_scatter")
    experts_run(nc, m, tag + "_run", W1, b1, W2, b2)
    experts_combine(nc, m, tag + "_combine", weighted)


def weights1(nc, m, c, w):
    def sb(n, s):
        return c.enter_context(nc.sbuf_tensor(n, s, F32))

    GH = D // 4
    m.nodew = sb("w1_node", [128, KD, D + 2 * HEADS])
    m.wqkv = sb("w1_qkv", [128, KD, 3 * D])
    m.wproj = sb("w1_proj", [128, KD, D])
    m.bproj = sb("w1_bproj", [P, D])
    m.wg1 = sb("w1_g1", [128, KD, GH])
    m.wg2 = sb("w1_g2", [GH, D])
    m.bg1 = sb("w1_bg1", [GH, 1])
    m.nbg2 = sb("w1_nbg2", [128, KD])
    m.lngT = sb("w1_lng", [128, KD])
    m.lnbT = sb("w1_lnb", [128, KD])
    with Stage(nc) as c2:
        al = c2.enter_context(nc.sbuf_tensor("w1_attn", [128, 2, D], F32))
        pr = c2.enter_context(nc.sbuf_tensor("w1_prod", [128, KD, 2, D], F32))
        loaded, chain = [c2.sem("w1_" + n) for n in ("loaded", "chain")]
        jobs = [(m.nodew[:, :, 0:D], w["L1_gnn_W"].rearrange("(k p) d -> p k d", p=128)),
                (al[:, 0, :], w["L1_gnn_attn_l"].rearrange("h c -> (h c)").partition_broadcast(128)),
                (al[:, 1, :], w["L1_gnn_attn_r"].rearrange("h c -> (h c)").partition_broadcast(128)),
                (m.wqkv[:, :, :], w["L1_mix_Wqkv"].rearrange("(k p) d -> p k d", p=128)),
                (m.wproj[:, :, :], w["L1_mix_Wproj"].rearrange("(k p) d -> p k d", p=128)),
                (m.bproj[:, :], w["L1_mix_bproj"].partition_broadcast(P)),
                (m.wg1[:, :, :], w["L1_mix_Wg1"].rearrange("(k p) d -> p k d", p=128)),
                (m.wg2[:, :], w["L1_mix_Wg2"]),
                (m.bg1[:, :], w["L1_mix_bg1"].rearrange("(p o) -> p o", o=1)),
                (m.nbg2[:, :], w["L1_mix_bg2"].rearrange("(k p) -> p k", p=128)),
                (m.lngT[:, :], w["L1_mix_ln_g"].rearrange("(k p) -> p k", p=128)),
                (m.lnbT[:, :], w["L1_mix_ln_b"].rearrange("(k p) -> p k", p=128))]
        with nc.Block() as block:
            @block.sync
            def _(sp):
                for dst, src in jobs:
                    sp.dma_start(dst, src).then_inc(loaded, 16)
                sp.wait_ge(loaded, 16 * len(jobs))

            @block.vector
            def _(v):
                k = Chain(v, chain, 0)
                v.wait_ge(loaded, 16 * len(jobs))
                k.link(v.tensor_scalar(m.nbg2[:, :], m.nbg2[:, :], -1.0, None, ALU.mult))
                for b in range(KD):
                    for x in range(2):
                        k.link(v.tensor_tensor(pr[:, b, x, :], m.nodew[:, b, 0:D], al[:, x, :], ALU.mult))
                        at = D + x * HEADS
                        k.link(v.tensor_reduce(m.nodew[:, b, at:at + HEADS], pr[:, b, x, :].rearrange("p (h c) -> p h c", c=HC), AX.X, ALU.add))


def gate_hidden(nc, m):
    GH = D // 4
    with Stage(nc) as c:
        def sb(n, s):
            return c.enter_context(nc.sbuf_tensor("gate_" + n, s, F32))

        def sem(n):
            return c.sem("gate_" + n)

        shift = sb("shift", [P, NT])
        xn = sb("xn", [P, 2, D])
        st = sb("st", [P, NT, 6])
        mean2 = sb("mean2", [P, NT])
        rstd2 = sb("rstd2", [P, NT])
        scale3 = sb("scale3", [P, NT])
        shift3 = sb("shift3", [P, NT])
        x3 = sb("x3", [P, 2, D])
        x3T = sb("x3T", [128, 2, KD, P])
        chain, renormed, stated, normed, turned, scaled, made, bent, powered, rows3 = [
            sem(n) for n in ("chain", "renormed", "stated", "normed", "turned", "scaled", "made", "bent", "powered", "rows3")]
        restated = sem("restated")
        with nc.Block() as block:
            @block.vector
            def _(v):
                k = Chain(v, chain, 0)
                k.link(v.scalar_tensor_tensor(shift[:, :], m.mean[:, :], -1.0, m.rstd[:, :], ALU.mult, ALU.mult))

                def stats(t, s):
                    if valid(t):
                        wait_count(v, stated, t - 1)
                        v.tensor_scalar(xn[:, s, :], row_of(m.xs, t), m.rstd[:, bass.ds(t, 1)], shift[:, bass.ds(t, 1)],
                                        ALU.mult, ALU.add).then_inc(renormed, 1)
                    if valid(t - 1):
                        v.wait_ge(renormed, t)
                        v.bn_stats(row_of(st, t - 1), xn[:, 1 - s, :]).then_inc(stated, 1)

                pipelined(v, stats, 1)
                v.wait_ge(stated, NT)
                moments(v, restated, st, mean2[:, :], rstd2[:, :], scale3[:, :], shift3[:, :])
                v.wait_ge(powered, 1)
                k.link(v.tensor_tensor(scale3[:, :], m.rstd[:, :], rstd2[:, :], ALU.mult))
                k.link(v.tensor_tensor(shift3[:, :], shift[:, :], mean2[:, :], ALU.subtract))
                k.link(v.tensor_tensor(shift3[:, :], shift3[:, :], rstd2[:, :], ALU.mult))

                def rows(t, s):
                    if valid(t):
                        wait_count(v, turned, t - 1)
                        v.tensor_scalar(x3[:, s, :], row_of(m.xs, t), scale3[:, bass.ds(t, 1)], shift3[:, bass.ds(t, 1)],
                                        ALU.mult, ALU.add).then_inc(rows3, 1)
                    if valid(t - 1):
                        v.wait_ge(turned, t)
                        wait_count(v, made, t - 2)
                        for b in range(KD):
                            ins = v.tensor_scalar(x3T[:, 1 - s, b, :], m.bank[1 - s][:, b * 128:b * 128 + P], m.lngT[:, b:b + 1],
                                                  m.lnbT[:, b:b + 1], ALU.mult, ALU.add)
                        ins.then_inc(scaled, 1)

                pipelined(v, rows, 1)

            @block.gpsimd
            def _(pool):
                pool.wait_ge(restated, 8)
                pool.tensor_tensor(rstd2[:, :], rstd2[:, :], m.half[0:P, 0:NT], ALU.pow).then_inc(powered, 1)

            @block.tensor
            def _(pe):
                def body(t, s):
                    if valid(t):
                        pe.wait_ge(rows3, t + 1)
                        wait_count(pe, scaled, t - 1)
                        for b in range(KD):
                            ins = pe.transpose(m.bank[s][:, b * 128:b * 128 + P], x3[:, s, b * 128:(b + 1) * 128], m.ident[0:P, 0:P])
                        ins.then_inc(turned, 1)
                    if valid(t - 1):
                        pe.wait_ge(scaled, t)
                        wait_count(pe, bent, t - 2)
                        for b in range(KD):
                            ins = pe.matmul(m.bank[3 - s][0:GH, 0:P], m.wg1[:, b, :], x3T[:, 1 - s, b, :], start=(b == 0), stop=(b == KD - 1))
                        ins.then_inc(made, 1)

                pipelined(pe, body, 1)

            @block.scalar
            def _(a):
                def body(t, s):
                    a.wait_ge(made, t + 1)
                    a.activation(m.hgT[:, tile_cols(t)], m.bank[2 + s][0:GH, 0:P], ACT.Gelu, bias=m.bg1[:, 0:1]).then_inc(bent, 1)

                pipelined(a, body, 0)


def mix1_keys(nc, m):
    with Stage(nc) as c:
        made, kept, topped = [c.sem("keys1_" + n) for n in ("made", "kept", "topped")]
        with nc.Block() as block:
            @block.tensor
            def _(pe):
                def body(t, s):
                    wait_count(pe, kept, t - 1)
                    for o in range(KD):
                        for k in range(KD):
                            ins = pe.matmul(m.bank[s][:, o * 128:o * 128 + P], m.wqkv[:, k, D + o * 128:D + (o + 1) * 128],
                                            m.xT[:, k, tile_cols(t)], start=(k == 0), stop=(k == KD - 1))
                    ins.then_inc(made, 1)

                pipelined(pe, body, 0)

            @block.scalar
            def _(a):
                def body(t, s):
                    a.wait_ge(made, t + 1)
                    a.activation(m.kT[:, :, tile_cols(t)], by_feature(m.bank[s]), ACT.Copy).then_inc(kept, 1)

                pipelined(a, body, 0)

            @block.vector
            def _(v):
                v.wait_ge(kept, NT)
                v.tensor_reduce(m.nmax[:, :], m.kT[:, :, :], AX.X, ALU.max).then_inc(topped, 1)
                v.wait_ge(topped, 1)
                v.tensor_scalar(m.nmax[:, :], m.nmax[:, :], -1.0, None, ALU.mult)


def mix1_context(nc, m):
    with Stage(nc) as c:
        def sb(n, s):
            return c.enter_context(nc.sbuf_tensor("ctx_" + n, s, F32))

        def sem(n):
            return c.sem("ctx_" + n)

        xst = sb("xst", [128, 2, KD, P])
        ekT = sb("ekT", [128, 2, KD, P])
        ek = sb("ek", [P, 2, D])
        vv = sb("v", [P, 2, D])
        part = sb("part", [128, KD, NT])
        den = sb("den", [128, KD])
        zeros = sb("zeros", [P, 128])
        staged, exped, turned, made, ekept, vkept, summed, zeroed, chain = [
            sem(n) for n in ("staged", "exped", "turned", "made", "ekept", "vkept", "summed", "zeroed", "chain")]
        with nc.Block() as block:
            @block.scalar
            def _(a):
                def body(t, s):
                    wait_count(a, turned, t - 1)
                    for k in range(KD):
                        ins = a.activation(ekT[:, s, k, :], m.kT[:, k, tile_cols(t)], ACT.Exp, bias=m.nmax[:, k:k + 1],
                                           accum_out=part[:, k, bass.ds(t, 1)])
                    ins.then_inc(exped, 1)
                    wait_count(a, made, t - 1)
                    a.activation(xst[:, s, :, :], m.xT[:, :, tile_cols(t)], ACT.Copy).then_inc(staged, 1)

                pipelined(a, body, 0)

            @block.tensor
            def _(pe):
                pe.wait_ge(zeroed, 1)
                pe.matmul(m.bank[4][:, 0:D], zeros[:, :], zeros[:, :].unsqueeze(1).to_broadcast([P, KD, 128]), start=True, stop=False)

                def body(t, s):
                    if valid(t):
                        pe.wait_ge(exped, t + 1)
                        wait_count(pe, ekept, t - 1)
                        for k in range(KD):
                            ins = pe.transpose(m.bank[s][0:P, k * 128:(k + 1) * 128], ekT[:, s, k, :], m.ident[:, :])
                        ins.then_inc(turned, 1)
                        pe.wait_ge(staged, t + 1)
                        wait_count(pe, vkept, t - 1)
                        for k in range(KD):
                            ins = pe.matmul(m.bank[2 + s][0:P, 0:D], xst[:, s, k, :], m.wqkv[:, k, 2 * D:3 * D], start=(k == 0), stop=(k == KD - 1))
                        ins.then_inc(made, 1)
                    if valid(t - 1):
                        pe.wait_ge(vkept, t)
                        for k in range(KD):
                            ins = pe.matmul(m.bank[4][:, k * 128:(k + 1) * 128], ek[:, 1 - s, k * 128:(k + 1) * 128],
                                            vv[:, 1 - s, k * 128:(k + 1) * 128], start=False, stop=False, skip_group_check=True)
                        ins.then_inc(summed, 1)

                pipelined(pe, body, 1)
                pe.matmul(m.bank[4][:, 0:D], zeros[:, :], zeros[:, :].unsqueeze(1).to_broadcast([P, KD, 128]),
                          start=False, stop=True).then_inc(summed, 1)

            @block.vector
            def _(v):
                v.memset(zeros[:, :], 0.0).then_inc(zeroed, 1)

                def body(t, s):
                    v.wait_ge(turned, t + 1)
                    wait_count(v, summed, t - 1)
                    v.tensor_copy(ek[:, s, :], m.bank[s][0:P, 0:D]).then_inc(ekept, 1)
                    v.wait_ge(made, t + 1)
                    v.tensor_copy(vv[:, s, :], m.bank[2 + s][0:P, 0:D]).then_inc(vkept, 1)

                pipelined(v, body, 0)
                k = Chain(v, chain, 0)
                v.wait_ge(exped, NT)
                k.link(v.tensor_reduce(den[:, :], part[:, :, :], AX.X, ALU.add))
                k.link(v.reciprocal(den[:, :], den[:, :]))
                v.wait_ge(summed, NT + 1)
                for b in range(KD):
                    k.link(v.scalar_tensor_tensor(m.kv[:, b, :], m.bank[4][:, b * 128:(b + 1) * 128], den[:, b:b + 1],
                                                  m.headmask[:, :], ALU.mult, ALU.mult))


def mix1_out(nc, m):
    GH = D // 4
    with Stage(nc) as c:
        def sb(n, s):
            return c.enter_context(nc.sbuf_tensor("out1_" + n, s, F32))

        def sem(n):
            return c.sem("out1_" + n)

        qT = sb("qT", [128, 2, KD, P])
        eg = sb("eg", [128, 2, KD, P])
        goT = sb("goT", [128, 2, KD, P])
        queried, qkept, mixed, gated, exped, chain, gone, made, added, biased = [
            sem(n) for n in ("queried", "qkept", "mixed", "gated", "exped", "chain", "gone", "made", "added", "biased")]
        with nc.Block() as block:
            @block.tensor
            def _(pe):
                def body(t, s):
                    if valid(t):
                        wait_count(pe, qkept, t - 1)
                        for o in range(KD):
                            for k in range(KD):
                                ins = pe.matmul(m.bank[s][:, o * 128:o * 128 + P], m.wqkv[:, k, o * 128:(o + 1) * 128],
                                                m.xT[:, k, tile_cols(t)], start=(k == 0), stop=(k == KD - 1))
                        ins.then_inc(queried, 1)
                        wait_count(pe, exped, t)
                        for o in range(KD):
                            ins = pe.matmul(m.bank[6][:, o * 128:o * 128 + P], m.wg2[:, o * 128:(o + 1) * 128], m.hgT[:, tile_cols(t)],
                                            start=True, stop=True)
                        ins.then_inc(gated, 1)
                    if valid(t - 1):
                        pe.wait_ge(qkept, t)
                        wait_count(pe, gone, t - 2)
                        for k in range(KD):
                            ins = pe.matmul(m.bank[3 - s][:, k * 128:k * 128 + P], m.kv[:, k, :], qT[:, 1 - s, k, :], start=True, stop=True)
                        ins.then_inc(mixed, 1)
                    if valid(t - 2):
                        pe.wait_ge(gone, t - 1)
                        wait_count(pe, added, t - 3)
                        for k in range(KD):
                            ins = pe.matmul(m.bank[4 + s][0:P, 0:D], goT[:, s, k, :], m.wproj[:, k, :], start=(k == 0), stop=(k == KD - 1))
                        ins.then_inc(made, 1)

                pipelined(pe, body, 2)

            @block.scalar
            def _(a):
                def body(t, s):
                    a.wait_ge(queried, t + 1)
                    wait_count(a, mixed, t - 1)
                    a.activation(qT[:, s, :, :], by_feature(m.bank[s]), ACT.Copy).then_inc(qkept, 1)
                    a.wait_ge(gated, t + 1)
                    wait_count(a, gone, t - 1)
                    for k in range(KD):
                        ins = a.activation(eg[:, s, k, :], m.bank[6][:, k * 128:k * 128 + P], ACT.Exp, bias=m.nbg2[:, k:k + 1], scale=-1.0)
                    ins.then_inc(exped, 1)

                pipelined(a, body, 0)

            @block.vector
            def _(v):
                k = Chain(v, chain, 2)

                def body(t, s):
                    if valid(t):
                        k.step(t)
                        v.wait_ge(exped, t + 1)
                        k.link(v.tensor_scalar(eg[:, s, :, :], eg[:, s, :, :], 1.0, None, ALU.add))
                        k.link(v.reciprocal(eg[:, s, :, :], eg[:, s, :, :]))
                        k.close()
                        v.wait_ge(mixed, t + 1)
                        wait_count(v, made, t - 1)
                        v.tensor_tensor(goT[:, s, :, :], by_feature(m.bank[2 + s]), eg[:, s, :, :], ALU.mult).then_inc(gone, 1)
                        x = row_of(m.xs, t)
                        v.tensor_tensor(x, x, m.bproj[:, :], ALU.add).then_inc(biased, 1)
                    if valid(t - 1):
                        x = row_of(m.xs, t - 1)
                        v.wait_ge(biased, t)
                        v.wait_ge(made, t)
                        v.tensor_tensor(x, x, m.bank[5 - s][0:P, 0:D], ALU.add).then_inc(added, 1)

                pipelined(v, body, 1)


def graph_attention1(nc, m):
    C = 5
    with Stage(nc) as c:
        def sb(n, s):
            return c.enter_context(nc.sbuf_tensor("elu_" + n, s, F32))

        def sem(n):
            return c.sem("elu_" + n)

        rden = sb("rden", [P, NT, HEADS])
        neg = sb("neg", [P, C, D])
        chain, lowered, exped = sem("chain"), sem("lowered"), sem("exped")
        with nc.Block() as block:
            @block.vector
            def _(v):
                k = Chain(v, chain, 0)
                k.link(v.tensor_scalar(rden[:, :, :], m.acc[:, :, D:D + HEADS], 1e-37, None, ALU.max))
                k.link(v.reciprocal(rden[:, :, :], rden[:, :, :]))
                for i in range(NT // C):
                    for t in range(i * C, (i + 1) * C):
                        o = m.acc[:, t, 0:D].rearrange("p (h c) -> p h c", c=HC)
                        ins = v.tensor_tensor(o, o, rden[:, t, :].unsqueeze(2).to_broadcast([P, HEADS, HC]), ALU.mult)
                    k.link(ins)
                    o = m.acc[:, i * C:(i + 1) * C, 0:D]
                    x = m.xs[:, i * C:(i + 1) * C, :]
                    v.tensor_scalar(neg[:, :, :], o, 0.0, None, ALU.min).then_inc(lowered, 1)
                    k.link(v.tensor_scalar(x, x, -1.0, None, ALU.add))
                    v.wait_ge(exped, i + 1)
                    k.link(v.scalar_tensor_tensor(o, o, 0.0, neg[:, :, :], ALU.max, ALU.add))
                    k.link(v.tensor_tensor(x, x, o, ALU.add))

            @block.scalar
            def _(a):
                for i in range(NT // C):
                    a.wait_ge(lowered, i + 1)
                    a.activation(neg[:, :, :], neg[:, :, :], ACT.Exp).then_inc(exped, 1)


def program(nc, w, out):
    m = Memory()
    m.edges = nc.dram_tensor("edge_list", [E + PAD, 2], I32).ap()
    m.table = {1: nc.dram_tensor("table0", [N, D + 2], F32).ap(), HEADS: nc.dram_tensor("table1", [N, D + 2 * HEADS], F32).ap()}
    m.xsort = nc.dram_tensor("xsort", [NB * ROWS, D], F32).ap()
    m.ysort = nc.dram_tensor("ysort", [NB * ROWS, D], F32).ap()
    with ExitStack() as c:
        c.enter_context(nc.allow_non_contiguous_dma(reason="biases of a few hundred elements, one per partition"))

        def sb(n, s, d=F32):
            return c.enter_context(nc.sbuf_tensor(n, s, d))

        m.bank = [c.enter_context(nc.psum_tensor(f"bank{i}", [128, 512], F32)) for i in range(8)]
        m.ident = sb("ident", [128, 128])
        m.ones = sb("ones", [128, 128])
        m.before = sb("before", [P, P])
        m.headmask = sb("headmask", [128, 128])
        m.nodes = sb("nodes", [128, N])
        m.half = sb("half", [128, 64])
        m.xs = sb("xs", [P, NT, D])
        m.xT = sb("xT", [128, KD, N])
        m.acc = sb("acc", [P, NT, D + 2 * HEADS])
        m.adm = sb("adm", [P, NT, 2 * HEADS])
        m.mean = sb("mean", [P, NT])
        m.rstd = sb("rstd", [P, NT])
        m.grow = sb("grow", [1, 2, 2, 128], I32)
        m.gtab = sb("gtab", [1, 2, NG], I32)
        m.kv = sb("kv", [128, KD, 128])
        m.cw = sb("cw", [P, 2, NT])
        m.slots = sb("slots", [P, NT, 2], I32)
        m.btab = sb("btab", [1, NB], I32)
        m.eall = sb("eall", [128, NG * 4], I32)
        constants(nc, m)
        load_x(nc, m, w["x"])
        edge_tables(nc, m, w["src"], w["dst"])
        with ExitStack() as layer:
            weights0(nc, m, layer, w)
            normalise(nc, m, "ln0", m.xs)
            node_tables(nc, m, "nt0", 1)
            score_bounds(nc, m, "sb0", 1)
            edge_sums(nc, m, "es0", 1, True)
            graph_attention0(nc, m)
            mix0_keys(nc, m)
            mix0_queries(nc, m)
            mix0_out(nc, m)
        experts(nc, m, "ffn0", w["L0_ffn_gate_w"], w["L0_ffn_gate_b"], w["L0_ffn_W1"], w["L0_ffn_b1"],
                w["L0_ffn_W2"], w["L0_ffn_b2"], True)
        with ExitStack() as layer:
            weights1(nc, m, layer, w)
            m.kT = layer.enter_context(nc.sbuf_tensor("kT", [128, KD, N], F32))
            m.hgT = layer.enter_context(nc.sbuf_tensor("hgT", [D // 4, N], F32))
            m.nmax = layer.enter_context(nc.sbuf_tensor("nmax", [128, KD], F32))
            normalise(nc, m, "ln1", m.xs)
            gate_hidden(nc, m)
            node_tables(nc, m, "nt1", HEADS, True)
            score_bounds(nc, m, "sb1", HEADS)
            edge_sums(nc, m, "es1", HEADS, False)
            mix1_keys(nc, m)
            mix1_context(nc, m)
            mix1_out(nc, m)
            graph_attention1(nc, m)
        experts(nc, m, "ffn1", w["L1_ffn_Wg"], w["L1_ffn_bg"], w["L1_ffn_W1"], w["L1_ffn_b1"],
                w["L1_ffn_W2"], w["L1_ffn_b2"], False)
        store_x(nc, m, out)


_INS = ["x", "src", "dst", "L0_gnn_W", "L0_gnn_att_src", "L0_gnn_att_dst", "L0_gnn_bias", "L0_gnn_W_ih",
        "L0_mix_w_qkv", "L0_mix_b_qkv", "L0_mix_kln_g", "L0_mix_kln_b", "L0_mix_vln_g", "L0_mix_vln_b",
        "L0_mix_w1", "L0_mix_b1", "L0_mix_w2", "L0_mix_b2", "L0_ffn_gate_w", "L0_ffn_gate_b", "L0_ffn_W1",
        "L0_ffn_b1", "L0_ffn_W2", "L0_ffn_b2", "L1_gnn_W", "L1_gnn_attn_l", "L1_gnn_attn_r", "L1_mix_Wqkv",
        "L1_mix_Wproj", "L1_mix_bproj", "L1_mix_ln_g", "L1_mix_ln_b", "L1_mix_Wg1", "L1_mix_bg1",
        "L1_mix_Wg2", "L1_mix_bg2", "L1_ffn_Wg", "L1_ffn_bg", "L1_ffn_W1", "L1_ffn_b1", "L1_ffn_W2", "L1_ffn_b2"]


def kernel(**inputs):
    import numpy as np
    import concourse.bacc as bacc
    from concourse.bass_utils import run_bass_kernel_spmd

    nc = bacc.Bacc("TRN2", target_bir_lowering=False, num_devices=1)
    arrays, args = {}, {}
    for name in _INS:
        a = np.ascontiguousarray(inputs[name])
        arrays[f"in_{name}"] = a
        args[name] = nc.dram_tensor(f"in_{name}", a.shape, mybir.dt.from_np(a.dtype), kind="ExternalInput").ap()
    out = nc.dram_tensor("out_x", (N, D), F32, kind="ExternalOutput").ap()
    program(nc, args, out)
    r = run_bass_kernel_spmd(nc, [arrays], core_ids=[0])
    return r.results[0]["out_x"]
```

```python
from contextlib import ExitStack

import concourse.bass as bass
from concourse import mybir

F32 = mybir.dt.float32
I32 = mybir.dt.int32
ALU = mybir.AluOpType
ACT = mybir.ActivationFunctionType
AX = mybir.AxisListType
MAX = bass.bass_isa.ReduceOp.max

N, E = 3125, 50000
P, NT = 125, 25
D = 256
KD = D // 128
HEADS, HC = 8, 32
NE, HID = 8, 512
KH = HID // 128
EPS = 1e-5
SLOPE = 0.2
BIG = 3.0e38
SAFE = 60.0
FLOOR = 1.0e30

PAD = 256
FAR = 8000
WIN = 2
GE = WIN * 128
NG = (E + NT * (GE - 1)) // GE + 1
NG += -NG % 16

EDGE_PARTS = [(0, NG // 64 + 2), (NG // 64 + 2, NG // 16 + 5), (NG // 16 + 5, NG // 8 - 2), (NG // 8 - 2, NG // 8)]

ROWS = 256
NB = (2 * N + NE * (ROWS - 1)) // ROWS
REGION = -(-N // ROWS) + 1
SPARE = NB - 2 * N // ROWS
SORTED = (NE * REGION + SPARE) * ROWS
EC = E // P


class Chain:

    def __init__(self, eng, sem, per):
        self.eng, self.sem, self.per = eng, sem, per
        self.base, self.n = 0, 0

    def step(self, t):
        self.base, self.n = t * self.per, 0

    def link(self, ins):
        ins.then_inc(self.sem, 1)
        self.n += 1
        self.eng.wait_ge(self.sem, self.base + self.n)

    def close(self):
        assert self.n == self.per, self.n


class Stage(ExitStack):

    def __init__(self, nc):
        super().__init__()
        self.nc, self.sems = nc, []

    def sem(self, name):
        self.sems.append(self.nc.alloc_semaphore(name))
        return self.sems[-1]

    def __exit__(self, *error):
        super().__exit__(*error)
        if not error[0]:
            self.nc.clear_and_free_semaphores(self.sems)
            self.nc.all_engine_barrier()


class Memory:
    pass


def table_width(H):
    return D + 2 if H == 1 else D + H


def tile_cols(t):
    return bass.ds(t * P, P)


def valid(t):
    return not isinstance(t, int) or 0 <= t < NT


def pipelined(eng, body, lag, slots=2):
    first = 1 + (lag + 1) // 2 if slots == 2 else -(-(lag + 2) // slots)
    for t in range(slots * first):
        body(t, t % slots)
    with eng.Fori(first, NT // slots) as b:
        for u in range(slots):
            body(b * slots + u, u)
    for t in range(NT // slots * slots, NT + lag):
        body(t, t % slots)


def wait_count(eng, sem, value):
    if not isinstance(value, int) or value > 0:
        eng.wait_ge(sem, value)


def row_of(t3, t):
    return t3[:, bass.ds(t, 1), :].rearrange("p a d -> p (a d)")


def by_feature(bank):
    return bank[:, 0:KD * 128].rearrange("p (k n) -> p k n", k=KD)[:, :, 0:P]


def constants(nc, m):
    with Stage(nc) as c, nc.Block() as block:
        const_set = c.sem("const_set")

        @block.gpsimd
        def _(pool):
            c = Chain(pool, const_set, 0)
            c.link(pool.memset(m.ident[:, :], 0.0))
            c.link(pool.affine_select(out=m.ident[:, :], in_=m.ident[:, :], pattern=[[-1, 128]],
                                      compare_op=ALU.not_equal, fill=1.0, base=0, channel_multiplier=1))
            c.link(pool.memset(m.ones[:, :], 1.0))
            c.link(pool.memset(m.before[:, :], 1.0))
            c.link(pool.affine_select(out=m.before[:, :], in_=m.before[:, :], pattern=[[1, P]],
                                      compare_op=ALU.is_ge, fill=0.0, base=-1, channel_multiplier=-1))
            c.link(pool.memset(m.headmask[:, :], 1.0))
            hm = m.headmask[:, :].rearrange("p (g c) -> p g c", c=HC)
            c.link(pool.affine_select(out=hm, in_=hm, pattern=[[-HC, 4], [0, HC]], compare_op=ALU.is_ge,
                                      fill=0.0, base=0, channel_multiplier=1))
            c.link(pool.affine_select(out=hm, in_=hm, pattern=[[HC, 4], [0, HC]], compare_op=ALU.is_ge,
                                      fill=0.0, base=HC - 1, channel_multiplier=-1))
            c.link(pool.iota(m.count[:, :], pattern=[[1, P]], base=0, channel_multiplier=0,
                             allow_small_or_imprecise_dtypes=True))
            c.link(pool.memset(m.half[:, :], -0.5))


def run_loads(eng, jobs, loaded):
    for dst, src in jobs:
        eng.dma_start(dst, src).then_inc(loaded, 16)
    eng.wait_ge(loaded, 16 * len(jobs))


def edge_tables(nc, m, src, dst, x, jobs):
    with Stage(nc) as c:
        def sb(n, s, d=F32):
            return c.enter_context(nc.sbuf_tensor(n, s, d))

        def sem(n):
            return c.sem(n)

        pairs = sb("edge_pairs", [P, EC, 2], I32)
        ends = sb("edge_ends", [P, 2, EC], I32)
        dstf = sb("edge_dstf", [P, EC])
        hit = sb("edge_hit", [P, EC])
        cnt = sb("edge_cnt", [P, NT + 1])
        pad = sb("edge_pad", [128, PAD // 128, 2], I32)
        first = sb("edge_first", [128, NT + 1])
        size_i = sb("edge_size_i", [128, NT], I32)
        groups = sb("edge_groups", [128, NT])
        gend = sb("edge_gend", [128, NT])
        base = sb("edge_base", [128, NT + 1])
        gcol = sb("edge_gcol", [128, 2, NT])
        gnum = sb("edge_gnum", [128, 2])
        past = sb("edge_past", [128, 2, NT])
        gt = sb("edge_gt", [128, 2, 2])
        zero = sb("edge_zero", [128, NT])
        next_first = sb("edge_next_first", [P, 1], I32)
        next_f = sb("edge_next_f", [P, 1])
        wrong = sb("edge_wrong", [P, 2])
        unordered = sb("edge_unordered", [1, 2], I32)
        loaded, chain, counted, summed = sem("edge_loaded"), sem("edge_chain"), sem("edge_counted"), sem("edge_summed")
        joined, stored, setup, tabled, turned = sem("edge_joined"), sem("edge_stored"), sem("edge_setup"), sem("edge_tabled"), sem("edge_turned")
        rows_set, moved, last_set = sem("edge_rows_set"), sem("edge_moved"), sem("edge_last_set")
        GH = NG // 2
        jobs_in, x_in = sem("edge_jobs_in"), sem("edge_x_in")
        with nc.Block() as block:
            @block.scalar
            def _(a):
                a.dma_start(m.xs[:, :, :], x.rearrange("(t p) d -> p t d", p=P)).then_inc(x_in, 16)
                run_loads(a, jobs, jobs_in)

            @block.sync
            def _(sp):
                sp.dma_start(ends[:, 0, :], src.rearrange("(p c) -> p c", c=EC)).then_inc(loaded, 16)
                sp.dma_start(ends[:, 1, :], dst.rearrange("(p c) -> p c", c=EC)).then_inc(loaded, 16)
                sp.wait_ge(last_set, 1)
                sp.dma_start(next_first[0:P - 1, :], dst.rearrange("(p c) -> p c", c=EC)[1:P, 0:1]).then_inc(loaded, 16)
                sp.wait_ge(joined, 2)
                sp.dma_start(m.edges[0:E, :].rearrange("(p c) x -> p c x", c=EC), pairs[:, :, :]).then_inc(stored, 16)
                sp.wait_ge(setup, 4)
                sp.dma_start(m.edges[E:E + PAD, :].rearrange("(p c) x -> p c x", p=128), pad[:, :, :]).then_inc(stored, 16)
                sp.wait_ge(stored, 32)
                sp.wait_ge(rows_set, 1)
                for h in range(2):
                    sp.dma_start(m.gtab[0:1, 0, h * GH:(h + 1) * GH], m.grow[0:1, h, 0, 0:GH]).then_inc(moved, 16)
                    sp.dma_start(m.gtab[0:1, 1, h * GH:(h + 1) * GH], m.grow[0:1, h, 1, 0:GH]).then_inc(moved, 16)
                sp.wait_ge(moved, 64)

            @block.gpsimd
            def _(pool):
                pool.memset(next_first[:, :], N).then_inc(last_set, 1)
                pool.memset(pad[:, :, 0], 0).then_inc(setup, 1)
                pool.memset(pad[:, :, 1], FAR).then_inc(setup, 1)
                pool.memset(zero[:, :], 0.0).then_inc(setup, 1)
                pool.iota(gnum[:, :], pattern=[[GH, 2]], base=0, channel_multiplier=1,
                          allow_small_or_imprecise_dtypes=True).then_inc(setup, 1)

            @block.vector
            def _(v):
                k = Chain(v, chain, 0)
                v.wait_ge(loaded, 48)
                v.tensor_copy(pairs[:, :, 0], ends[:, 0, :]).then_inc(joined, 1)
                v.tensor_copy(pairs[:, :, 1], ends[:, 1, :]).then_inc(joined, 1)
                k.link(v.tensor_copy(dstf[:, :], ends[:, 1, :]))
                k.link(v.tensor_copy(next_f[:, :], next_first[:, :]))
                k.link(v.tensor_tensor(wrong[:, 0:1], next_f[:, :], dstf[:, EC - 1:EC], ALU.is_lt))
                k.link(v.tensor_tensor(hit[:, 0:EC - 1], dstf[:, 1:EC], dstf[:, 0:EC - 1], ALU.is_lt))
                k.link(v.tensor_reduce(wrong[:, 1:2], hit[:, 0:EC - 1], AX.X, ALU.max))
                v.memset(cnt[:, 0:1], 0.0).then_inc(counted, 1)
                for t in range(1, NT + 1):
                    k.link(v.tensor_scalar(hit[:, :], dstf[:, :], float(t * P), 0.0, ALU.is_lt, ALU.add,
                                           accum_out=cnt[:, t:t + 1]))
                v.sem_inc(counted, 1)
                v.wait_ge(summed, 1)
                k.link(v.tensor_copy(first[:, :], m.bank[0][:, 0:NT + 1]))
                k.link(v.tensor_copy(unordered[:, :], m.bank[0][0:1, 64:66]))
                k.link(v.tensor_tensor(groups[:, :], first[:, 1:NT + 1], first[:, 0:NT], ALU.subtract))
                k.link(v.tensor_scalar(size_i[:, :], groups[:, :], float(GE - 1), None, ALU.add))
                k.link(v.tensor_scalar(size_i[:, :], size_i[:, :], 8, None, ALU.arith_shift_right))
                k.link(v.tensor_copy(groups[:, :], size_i[:, :]))
                v.wait_ge(setup, 4)
                k.link(v.tensor_tensor_scan(gend[:, :], groups[:, :], zero[:, :], 0.0, ALU.add, ALU.add))
                k.link(v.tensor_copy(base[:, 0:1], first[:, 0:1]))
                k.link(v.scalar_tensor_tensor(base[:, 1:NT + 1], gend[:, :], -float(GE), first[:, 1:NT + 1],
                                              ALU.mult, ALU.add))
                for h in range(2):
                    k.link(v.tensor_scalar(past[:, h, :], gend[:, :], gnum[:, h:h + 1], None, ALU.is_le))
                    k.link(v.tensor_reduce(gt[:, 0, h:h + 1], past[:, h, :], AX.X, ALU.add))
                    k.link(v.tensor_scalar(gt[:, 0, h:h + 1], gt[:, 0, h:h + 1], float(NT - 1), None, ALU.min))
                    k.link(v.tensor_tensor(gcol[:, h, :], base[:, 1:NT + 1], base[:, 0:NT], ALU.subtract))
                    k.link(v.tensor_tensor(gcol[:, h, :], gcol[:, h, :], past[:, h, :], ALU.mult))
                    k.link(v.tensor_reduce(gt[:, 1, h:h + 1], gcol[:, h, :], AX.X, ALU.add))
                    k.link(v.scalar_tensor_tensor(gt[:, 1, h:h + 1], gnum[:, h:h + 1], float(GE), gt[:, 1, h:h + 1],
                                                  ALU.mult, ALU.add))
                    k.link(v.tensor_scalar(gt[:, 1, h:h + 1], gt[:, 1, h:h + 1], float(E), None, ALU.min))
                v.sem_inc(tabled, 1)
                v.wait_ge(turned, 1)
                v.tensor_copy(m.grow[:, :, :, :].rearrange("o h x g -> o (h x g)"),
                              m.bank[1][0:1, 0:512]).then_inc(rows_set, 1)
                v.wait_ge(x_in, 16)
                with v.Fori(0, NT // 5) as b:
                    for u in range(5):
                        v.bn_stats(row_of(m.stats, b * 5 + u), row_of(m.xs, b * 5 + u))

            @block.tensor
            def _(pe):
                pe.wait_ge(counted, 2)
                pe.matmul(m.bank[0][:, 0:NT + 1], m.ones[0:P, :], cnt[:, :], start=True, stop=True)
                pe.matmul(m.bank[0][:, 64:66], m.ones[0:P, :], wrong[:, :], start=True, stop=True).then_inc(summed, 1)
                pe.wait_ge(tabled, 1)
                for h in range(2):
                    for x in range(2):
                        at = (h * 2 + x) * 128
                        ins = pe.transpose(m.bank[1][0:1, at:at + 128], gt[:, x, h:h + 1], m.ident[:, :])
                ins.then_inc(turned, 1)

        order_edges(nc, m, c, unordered, pairs, dstf, first)


def order_edges(nc, m, c, unordered, pairs, dstf, first):
    def sb(n, s, d=F32):
        return c.enter_context(nc.sbuf_tensor("order_" + n, s, d))

    low = sb("low", [P, NT + 1])
    reached = sb("reached", [P, NT + 1])
    own = sb("own", [P, NT])
    front = sb("front", [P, NT])
    place = sb("place", [P, NT])
    place1 = sb("place1", [P, 1])
    slot = sb("slot", [P, 1], I32)
    pair = sb("pair", [P, 2], I32)
    low_set, chain, owned, ranked, placed, moved, gone, go = [
        c.sem("order_" + n) for n in ("low_set", "chain", "owned", "ranked", "placed", "moved", "gone", "go")]

    def flags(eng):
        _, r = nc.values_load_multi_w_load_instructions(unordered[0:1, 0:2], engines=[eng.engine], min_val=0, max_val=P)
        return r[0] + r[1]

    with nc.Block() as block:
        @block.gpsimd
        def _(pool):
            with pool.If(flags(pool) > 0):
                pool.sem_inc(gone, 1)
                pool.iota(low[:, :], pattern=[[P, NT + 1]], base=0, channel_multiplier=0,
                          allow_small_or_imprecise_dtypes=True).then_inc(low_set, 1)
                with pool.Fori(0, EC) as i:
                    pool.wait_ge(placed, i + 1)
                    pool.sem_inc(go, 1)
                    pool.indirect_dma_start(m.edges, bass.IndirectOffsetOnAxis(ap=slot[:, 0:1], axis=0),
                                            pair[:, :], None).then_inc(moved, 16)
                    pool.wait_ge(moved, i * 16 + 16)
                    pool.sem_inc(gone, 1)

        @block.vector
        def _(v):
            with v.If(flags(v) > 0):
                k = Chain(v, chain, 8)
                v.wait_ge(low_set, 1)
                v.tensor_copy(front[:, :], first[0:P, 0:NT]).then_inc(low_set, 1)
                v.wait_ge(low_set, 2)
                with v.Fori(0, EC) as i:
                    k.step(i)
                    k.link(v.tensor_scalar(reached[:, :], low[:, :], dstf[:, bass.ds(i, 1)], None, ALU.is_le))
                    k.link(v.tensor_tensor(own[:, :], reached[:, 0:NT], reached[:, 1:NT + 1], ALU.subtract))
                    v.sem_inc(owned, 1)
                    v.wait_ge(ranked, i + 1)
                    k.link(v.tensor_tensor(place[:, :], m.bank[2][0:P, 0:NT], front[:, :], ALU.add))
                    k.link(v.tensor_tensor(place[:, :], place[:, :], own[:, :], ALU.mult))
                    k.link(v.tensor_reduce(place1[:, :], place[:, :], AX.X, ALU.add))
                    k.link(v.tensor_tensor(front[:, :], front[:, :], m.bank[2][0:P, 64:64 + NT], ALU.add))
                    v.wait_ge(gone, i + 1)
                    k.link(v.tensor_copy(slot[:, :], place1[:, :]))
                    k.link(v.tensor_copy(pair[:, :], pairs[:, bass.ds(i, 1), :].rearrange("p a x -> p (a x)")))
                    v.sem_inc(placed, 1)
                    k.close()

        @block.tensor
        def _(pe):
            with pe.If(flags(pe) > 0):
                with pe.Fori(0, EC) as i:
                    pe.wait_ge(owned, i + 1)
                    pe.matmul(m.bank[2][0:P, 0:NT], m.before[:, :], own[:, :], start=True, stop=True)
                    pe.matmul(m.bank[2][:, 64:64 + NT], m.ones[0:P, :], own[:, :], start=True, stop=True).then_inc(ranked, 1)


def moments(v, chained, stats, mean, var, half, other):
    k = Chain(v, chained, 0)
    k.link(v.tensor_tensor(mean, stats[:, :, 1], stats[:, :, 4], ALU.add))
    k.link(v.tensor_tensor(half, stats[:, :, 1], stats[:, :, 4], ALU.subtract))
    k.link(v.tensor_scalar(mean, mean, 0.5, None, ALU.mult))
    k.link(v.tensor_scalar(half, half, 0.5, None, ALU.mult))
    k.link(v.tensor_tensor(half, half, half, ALU.mult))
    k.link(v.tensor_tensor(other, stats[:, :, 2], stats[:, :, 5], ALU.add))
    k.link(v.scalar_tensor_tensor(var, other, 1.0 / D, half, ALU.mult, ALU.add))


def normalise(nc, m, tag):
    with Stage(nc) as c:
        half = c.enter_context(nc.sbuf_tensor(tag + "_half", [P, NT], F32))
        other = c.enter_context(nc.sbuf_tensor(tag + "_other", [P, NT], F32))
        shifted = c.enter_context(nc.sbuf_tensor(tag + "_shifted", [P, NT], F32))
        meaned, powered = [c.sem(tag + n) for n in ("_meaned", "_powered")]
        with nc.Block() as block:
            @block.vector
            def _(v):
                moments(v, meaned, m.stats, m.mean[:, :], m.var[:, :], half[:, :], other[:, :])
                v.tensor_scalar(shifted[:, :], m.var[:, :], EPS, None, ALU.add).then_inc(meaned, 1)

            @block.gpsimd
            def _(pool):
                pool.wait_ge(meaned, 8)
                pool.tensor_tensor(m.rstd[:, :], shifted[:, :], m.half[0:P, 0:NT], ALU.pow).then_inc(powered, 1)
                pool.wait_ge(powered, 1)


def weights0(nc, m, c, w):
    def sb(n, s):
        return c.enter_context(nc.sbuf_tensor(n, s, F32))

    m.nodew = sb("w0_node", [128, KD, D + 2])
    m.gatew = sb("w0_gates", [128, KD, 3 * D])
    m.gbias = sb("w0_gbias", [P, D])
    m.wq = sb("w0_q", [128, KD, D])
    m.wkv = sb("w0_kv", [128, KD, 2 * D])
    m.bq = sb("w0_bq", [128, KD])
    m.bkv = sb("w0_bkv", [P, 2 * D])
    m.lng = sb("w0_lng", [P, 2 * D])
    m.lnb = sb("w0_lnb", [P, 2 * D])
    m.w1 = sb("w0_w1", [128, KD, D])
    m.b1 = sb("w0_b1", [128, KD])
    m.w2 = sb("w0_w2", [128, KD, D])
    m.b2 = sb("w0_b2", [P, D])
    wn = m.wn = sb("w0_nat", [128, KD, D])
    an = m.an = sb("w0_att", [128, KD, 2])
    gn = m.gn = sb("w0_gnat", [128, 6, D])
    jobs = [(wn[:, :, :], w["L0_gnn_W"].rearrange("(k p) d -> p k d", p=128)),
            (an[:, :, 0], w["L0_gnn_att_src"].rearrange("(k p) -> p k", p=128)),
            (an[:, :, 1], w["L0_gnn_att_dst"].rearrange("(k p) -> p k", p=128)),
            (gn[:, 0:2, :], w["L0_gnn_W_ih"][0:D, :].rearrange("(k p) d -> p k d", p=128)),
            (gn[:, 2:4, :], w["L0_gnn_W_ih"][3 * D:4 * D, :].rearrange("(k p) d -> p k d", p=128)),
            (gn[:, 4:6, :], w["L0_gnn_W_ih"][2 * D:3 * D, :].rearrange("(k p) d -> p k d", p=128)),
            (m.gbias[:, :], w["L0_gnn_bias"].partition_broadcast(P)),
            (m.w1[:, :, :], w["L0_mix_w1"].rearrange("(k p) d -> p k d", p=128)),
            (m.w2[:, :, :], w["L0_mix_w2"].rearrange("(k p) d -> p k d", p=128)),
            (m.b1[:, :], w["L0_mix_b1"].rearrange("(k p) -> p k", p=128)),
            (m.b2[:, :], w["L0_mix_b2"].partition_broadcast(P))]
    qkv = w["L0_mix_w_qkv"].rearrange("(k p) (h x c) -> k p x h c", p=128, x=3, c=HC)
    bqkv = w["L0_mix_b_qkv"].rearrange("(h x c) -> x h c", x=3, c=HC)
    for k in range(KD):
        jobs.append((m.wq[:, k, :].rearrange("p (h c) -> p h c", c=HC), qkv[k, :, 0]))
        for x in range(2):
            jobs.append((m.wkv[:, k, x * D:(x + 1) * D].rearrange("p (h c) -> p h c", c=HC), qkv[k, :, 1 + x]))
        for h in range(4):
            jobs.append((m.bq[h * HC:(h + 1) * HC, k:k + 1], bqkv[0, 4 * k + h, :].rearrange("(c o) -> c o", o=1)))
    for x in range(2):
        jobs.append((m.bkv[:, x * D:(x + 1) * D].rearrange("p (h c) -> p h c", c=HC), bqkv[1 + x].partition_broadcast(P)))
    for x, (g, b) in enumerate((("kln_g", "kln_b"), ("vln_g", "vln_b"))):
        for t, n in ((m.lng, g), (m.lnb, b)):
            jobs.append((t[:, x * D:(x + 1) * D].rearrange("p (h c) -> p h c", c=HC),
                         w["L0_mix_" + n].rearrange("(o c) -> o c", o=1).to_broadcast([HEADS, HC]).partition_broadcast(P)))
    return jobs


def weights0_turned(nc, m):
    wn, an, gn = m.wn, m.an, m.gn
    with Stage(nc) as c2:
        mean = c2.enter_context(nc.sbuf_tensor("w0_mean", [128, 2 * HEADS], F32))
        turned, kept, chain = [c2.sem("w0_" + n) for n in ("turned", "kept", "chain")]
        with nc.Block() as block:
            @block.tensor
            def _(pe):
                for k in range(KD):
                    for h in range(KD):
                        pe.transpose(m.bank[k][:, h * 128:(h + 1) * 128], wn[:, h, k * 128:(k + 1) * 128], m.ident[:, :])
                    for h in range(KD):
                        ins = pe.matmul(m.bank[k][:, D:D + 2], wn[:, h, k * 128:(k + 1) * 128], an[:, h, :],
                                        start=(h == 0), stop=(h == KD - 1))
                    ins.then_inc(turned, 1)
                for k in range(KD):
                    for u in range(6):
                        at = 2 + 2 * k + u // 4
                        ins = pe.transpose(m.bank[at][:, (u % 4) * 128:(u % 4 + 1) * 128], gn[:, u, k * 128:(k + 1) * 128], m.ident[:, :])
                    ins.then_inc(turned, 1)

            @block.vector
            def _(v):
                for k in range(KD):
                    v.wait_ge(turned, k + 1)
                    v.tensor_copy(m.nodew[:, k, :], m.bank[k][:, 0:D + 2]).then_inc(kept, 1)
                for k in range(KD):
                    v.wait_ge(turned, KD + k + 1)
                    v.tensor_copy(m.gatew[:, k, 0:2 * D], m.bank[2 + 2 * k][:, 0:512]).then_inc(kept, 1)
                    v.tensor_copy(m.gatew[:, k, 2 * D:3 * D], m.bank[3 + 2 * k][:, 0:D]).then_inc(kept, 1)
                k = Chain(v, chain, 0)
                for part, rows in ((m.wkv[:, 0, :], 128), (m.wkv[:, 1, :], 128), (m.bkv[:, :], P)):
                    heads = part.rearrange("p (g c) -> p g c", c=HC)
                    mu = mean[0:rows, :]
                    k.link(v.tensor_reduce(mu, heads, AX.X, ALU.add))
                    k.link(v.tensor_scalar(mu, mu, 1.0 / HC, None, ALU.mult))
                    k.link(v.tensor_tensor(heads, heads, mu.unsqueeze(2).to_broadcast([rows, 2 * HEADS, HC]), ALU.subtract))


def load_edges(nc, m, eng, edges_in, lo, hi):
    S = len(edges_in)

    def load(b, first):
        _, e0 = nc.values_load_multi_w_load_instructions(m.gtab[0:1, 1, bass.ds(b * S, S)], engines=[eng.engine],
                                                         min_val=0, max_val=E)
        for s in range(S):
            if not first:
                eng.wait_ge(edges_in[s], (b - lo) * 16)
            eng.dma_start(m.eall[:, bass.ds((b * S + s) * 4, 4)],
                          m.edges[bass.ds(e0[s], GE), :].rearrange("(p w) x -> p (w x)", w=WIN)).then_inc(edges_in[s], 16)

    load(lo, True)
    with eng.Fori(lo + 1, hi) as b:
        load(b, False)
    for s in range(S):
        eng.wait_ge(edges_in[s], 16 * (hi - lo))


def edge_columns(nc, m):
    with Stage(nc) as c, nc.sbuf_tensor("edge_tiles", [1, NG], F32) as tiles, nc.Block() as block:
        copied, spread, chain = c.sem("edge_tiles_copied"), c.sem("edge_tiles_spread"), c.sem("edge_local_chain")
        dsts = m.eall[:, :].rearrange("p (g x) -> p g x", x=2)[:, :, 1]

        @block.vector
        def _(v):
            v.tensor_copy(tiles[:, :], m.gtab[0:1, 0, :]).then_inc(copied, 1)
            k = Chain(v, chain, 0)
            k.link(v.tensor_copy(m.local[:, :], dsts))
            v.wait_ge(spread, 1)
            v.scalar_tensor_tensor(m.local[:, :].rearrange("p (g w) -> p g w", w=WIN),
                                   m.bank[0][:, 0:NG].unsqueeze(2).to_broadcast([128, NG, WIN]), -float(P),
                                   m.local[:, :].rearrange("p (g w) -> p g w", w=WIN), ALU.mult, ALU.add)

        @block.tensor
        def _(pe):
            pe.wait_ge(copied, 1)
            pe.matmul(m.bank[0][:, 0:NG], m.ones[0:1, :], tiles[:, :], start=True, stop=True).then_inc(spread, 1)


class GateHidden:

    def __init__(self, nc, m, c):
        def sb(n, s):
            return c.enter_context(nc.sbuf_tensor("gate_" + n, s, F32))

        self.m = m
        self.rstd2, self.scale3, self.shift3 = [sb(n, [P, NT]) for n in ("rstd2", "scale3", "shift3")]
        self.x3 = sb("x3", [P, 2, D])
        self.x3T = sb("x3T", [128, 2, KD, P])
        (self.chain, self.varred, self.powered, self.rows3, self.turned, self.scaled, self.made, self.bent) = [
            c.sem("gate_" + n) for n in ("chain", "varred", "powered", "rows3", "turned", "scaled", "made", "bent")]

    def vector_start(self, v):
        m, rstd2 = self.m, self.rstd2
        k = Chain(v, self.chain, 0)
        k.link(v.tensor_tensor(rstd2[:, :], m.rstd[:, :], m.rstd[:, :], ALU.mult))
        k.link(v.tensor_tensor(rstd2[:, :], rstd2[:, :], m.var[:, :], ALU.mult))
        v.tensor_scalar(rstd2[:, :], rstd2[:, :], EPS, None, ALU.add).then_inc(self.varred, 1)
        v.wait_ge(self.powered, 1)
        k.link(v.tensor_tensor(self.scale3[:, :], m.rstd[:, :], rstd2[:, :], ALU.mult))
        k.link(v.scalar_tensor_tensor(self.shift3[:, :], m.mean[:, :], -1.0, self.scale3[:, :], ALU.mult, ALU.mult))

    def pool_start(self, pool):
        pool.wait_ge(self.varred, 1)
        pool.tensor_tensor(self.rstd2[:, :], self.rstd2[:, :], self.m.half[0:P, 0:NT], ALU.pow).then_inc(self.powered, 1)

    def vector(self, v, t, s):
        m = self.m
        if valid(t):
            wait_count(v, self.turned, t - 1)
            v.tensor_scalar(self.x3[:, s, :], row_of(m.xs, t), self.scale3[:, bass.ds(t, 1)], self.shift3[:, bass.ds(t, 1)],
                            ALU.mult, ALU.add).then_inc(self.rows3, 1)
        if valid(t - 1):
            v.wait_ge(self.turned, t)
            wait_count(v, self.made, t - 2)
            for b in range(KD):
                ins = v.tensor_scalar(self.x3T[:, 1 - s, b, :], m.bank[5 - s][:, b * 128:b * 128 + P], m.lngT[:, b:b + 1],
                                      m.lnbT[:, b:b + 1], ALU.mult, ALU.add)
            ins.then_inc(self.scaled, 1)

    def tensor(self, pe, t, s):
        m = self.m
        if valid(t):
            pe.wait_ge(self.rows3, t + 1)
            wait_count(pe, self.scaled, t - 1)
            for b in range(KD):
                ins = pe.transpose(m.bank[4 + s][:, b * 128:b * 128 + P], self.x3[:, s, b * 128:(b + 1) * 128], m.ident[0:P, 0:P])
            ins.then_inc(self.turned, 1)
        if valid(t - 2):
            pe.wait_ge(self.scaled, t - 1)
            wait_count(pe, self.bent, t - 3)
            for b in range(KD):
                ins = pe.matmul(m.bank[6 + s][0:D // 4, 0:P], m.wg1[:, b, :], self.x3T[:, s, b, :], start=(b == 0), stop=(b == KD - 1))
            ins.then_inc(self.made, 1)

    def scalar(self, a, t, s):
        m = self.m
        if valid(t - 3):
            a.wait_ge(self.made, t - 2)
            a.activation(m.hgT[:, tile_cols(t - 3)], m.bank[7 - s][0:D // 4, 0:P], ACT.Gelu, bias=m.bg1[:, 0:1]).then_inc(self.bent, 1)


def node_tables(nc, m, tag, H, with_gate=False, edge_part=None):
    W = D + 2 * H
    C = 5
    with Stage(nc) as c:
        def sb(n, s):
            return c.enter_context(nc.sbuf_tensor(tag + n, s, F32))

        def sem(n):
            return c.sem(tag + n)

        shift = sb("_shift", [P, NT])
        xn = sb("_xn", [P, 2, D])
        xst = sb("_xst", [128, 2, KD, P])
        chain, normed, added, turned, staged, rowed, row_kept, ones_set, stored = [
            sem(n) for n in ("_chain", "_normed", "_added", "_turned", "_staged", "_rowed", "_row_kept", "_ones_set", "_stored")]
        edges_in = [sem(f"_edges_in{s}") for s in range(8)] if edge_part else []
        gate = GateHidden(nc, m, c) if with_gate else None
        with nc.Block() as block:
            if with_gate:
                @block.gpsimd
                def _(pool):
                    gate.pool_start(pool)

            @block.vector
            def _(v):
                if with_gate:
                    gate.vector_start(v)
                v.scalar_tensor_tensor(shift[:, :], m.mean[:, :], -1.0, m.rstd[:, :], ALU.mult, ALU.mult).then_inc(chain, 1)
                v.wait_ge(chain, 1)
                if H == 1:
                    v.memset(m.acc[:, :, D + 1:D + 2], 1.0).then_inc(ones_set, 1)

                def body(t, s):
                    if valid(t):
                        wait_count(v, turned, t - 1)
                        v.tensor_scalar(xn[:, s, :], row_of(m.xs, t), m.rstd[:, bass.ds(t, 1)], shift[:, bass.ds(t, 1)],
                                        ALU.mult, ALU.add).then_inc(normed, 1)
                    if valid(t - 3):
                        v.wait_ge(rowed, t - 2)
                        v.tensor_copy(row_of(m.adm[:, :, 0:H], t - 3), m.bank[3 - s][0:P, D + H:W])
                        v.tensor_copy(row_of(m.acc[:, :, 0:D + H], t - 3), m.bank[3 - s][0:P, 0:D + H]).then_inc(row_kept, 1)
                    if valid(t) and not with_gate:
                        v.wait_ge(normed, t + 1)
                        x_t = row_of(m.xs, t)
                        v.tensor_tensor(x_t, x_t, xn[:, s, :], ALU.add).then_inc(added, 1)
                    if with_gate:
                        gate.vector(v, t, s)

                pipelined(v, body, 3)

            @block.scalar
            def _(a):
                def body(t, s):
                    if valid(t):
                        a.wait_ge(turned, t + 1)
                        wait_count(a, rowed, t - 1)
                        a.activation(xst[:, s, :, :], by_feature(m.bank[s]), ACT.Copy)
                        a.activation(m.xT[:, :, tile_cols(t)], by_feature(m.bank[s]), ACT.Copy).then_inc(staged, 1)
                    if with_gate:
                        gate.scalar(a, t, s)

                pipelined(a, body, 3 if with_gate else 0)

            @block.tensor
            def _(pe):
                def body(t, s):
                    if valid(t):
                        pe.wait_ge(normed, t + 1)
                        wait_count(pe, staged, t - 1)
                        for k in range(KD):
                            ins = pe.transpose(m.bank[s][:, k * 128:k * 128 + P], xn[:, s, k * 128:(k + 1) * 128], m.ident[0:P, 0:P])
                        ins.then_inc(turned, 1)
                    if valid(t - 2):
                        pe.wait_ge(staged, t - 1)
                        wait_count(pe, row_kept, t - 3)
                        for k in range(KD):
                            ins = pe.matmul(m.bank[2 + s][0:P, 0:W], xst[:, s, k, :], m.nodew[:, k, 0:W], start=(k == 0), stop=(k == KD - 1))
                        ins.then_inc(rowed, 1)
                    if with_gate:
                        gate.tensor(pe, t, s)

                pipelined(pe, body, 2)

            @block.sync
            def _(sp):
                if edge_part:
                    load_edges(nc, m, sp, edges_in, *edge_part)
                if H == 1:
                    sp.wait_ge(ones_set, 1)
                for i in range(0, NT, C):
                    sp.wait_ge(row_kept, i + C)
                    sp.dma_start(m.table[H].rearrange("(t p) w -> p t w", p=P)[:, i:i + C, :],
                                 m.acc[:, i:i + C, 0:table_width(H)]).then_inc(stored, 16)
                sp.wait_ge(stored, 16 * (NT // C))


def score_bounds(nc, m, tag, H):
    with Stage(nc) as c:
        def sb(n, s, d=F32):
            return c.enter_context(nc.sbuf_tensor(tag + n, s, d))

        def sem(n):
            return c.sem(tag + n)

        ends = sb("_ends", [P, 2, H])
        all_ends = sb("_all_ends", [P, 2, H])
        spread = sb("_spread", [1, H])
        over = sb("_over", [1, 1])
        far = sb("_far", [1, 1], I32)
        z = sb("_z", [P, NT, H])
        es = sb("_es", [P, NT, H])
        chain, ended, maxed, zed, exped = [sem(n) for n in ("_chain", "_ended", "_maxed", "_zed", "_exped")]
        asrc = m.acc[:, :, D:D + H]
        adm_a = m.adm[:, :, 0:H]
        adm_m = m.adm[:, :, H:2 * H]
        with nc.Block() as block:
            @block.vector
            def _(v):
                k = Chain(v, chain, 0)
                k.link(v.tensor_reduce(ends[:, 0, :], asrc.rearrange("p t h -> p h t"), AX.X, ALU.max))
                k.link(v.tensor_reduce(ends[:, 1, :], asrc.rearrange("p t h -> p h t"), AX.X, ALU.min))
                v.tensor_scalar(ends[:, 1, :], ends[:, 1, :], -1.0, None, ALU.mult).then_inc(ended, 1)
                v.wait_ge(maxed, 1)
                k.link(v.tensor_tensor(spread[:, :], all_ends[0:1, 0, :], all_ends[0:1, 1, :], ALU.add))
                k.link(v.tensor_reduce(over[:, :], spread[:, :], AX.X, ALU.max))
                k.link(v.tensor_scalar(over[:, :], over[:, :], SAFE, None, ALU.is_gt))
                k.link(v.tensor_copy(far[:, :], over[:, :]))
                k.link(v.tensor_tensor(adm_m, adm_a, all_ends[:, 0, :].unsqueeze(1).to_broadcast([P, NT, H]), ALU.add))
                k.link(v.tensor_scalar(z[:, :, :], adm_m, SLOPE, None, ALU.mult))
                k.link(v.tensor_tensor(adm_m, adm_m, z[:, :, :], ALU.max))

            @block.gpsimd
            def _(pool):
                pool.wait_ge(ended, 1)
                pool.partition_all_reduce(all_ends[:, :, :].rearrange("p x h -> p (x h)"),
                                          ends[:, :, :].rearrange("p x h -> p (x h)"), P, MAX).then_inc(maxed, 1)

        own_maxima(nc, m, c, tag, H, far)
        with nc.Block() as block:
            @block.vector
            def _(v):
                if H == 1:
                    k = Chain(v, zed, 0)
                    k.link(v.tensor_tensor(z[:, :, :], asrc, adm_a, ALU.add))
                    k.link(v.tensor_scalar(es[:, :, :], z[:, :, :], SLOPE, None, ALU.mult))
                    k.link(v.tensor_tensor(z[:, :, :], z[:, :, :], es[:, :, :], ALU.max))
                    v.tensor_tensor(z[:, :, :], z[:, :, :], adm_m, ALU.subtract).then_inc(zed, 1)
                    v.wait_ge(exped, 1)
                    with v.Fori(0, NT // 5) as b:
                        for u in range(5):
                            row = row_of(m.acc[:, :, 0:D + 2], b * 5 + u)
                            v.tensor_scalar(row, row, row_of(es, b * 5 + u), None, ALU.mult)
                else:
                    v.memset(m.acc[:, :, :], 0.0)

            @block.scalar
            def _(a):
                if H == 1:
                    a.wait_ge(zed, 4)
                    a.activation(es[:, :, :], z[:, :, :], ACT.Exp).then_inc(exped, 1)


def own_maxima(nc, m, c, tag, H, far):
    def sb(n, s, d=F32):
        return c.enter_context(nc.sbuf_tensor(tag + "_own" + n, s, d))

    def sem(n):
        return c.sem(tag + "_own" + n)

    idx = sb("_idx", [128, WIN], I32)
    rows = sb("_rows", [128, WIN, table_width(H)])
    one = sb("_one", [128, WIN, P])
    push = sb("_push", [P, WIN * 128])
    wide = sb("_wide", [128, WIN, P])
    cand = sb("_cand", [P, WIN * 128])
    top = sb("_top", [P, 1])
    best = sb("_best", [P, NT, H])
    low = sb("_low", [P, NT, H])
    chain, hot, turned, fetched, widened, spread, bound, go = [
        sem(n) for n in ("_chain", "_hot", "_turned", "_fetched", "_widened", "_spread", "_bound", "_go")]
    adm_a, adm_m = m.adm[:, :, 0:H], m.adm[:, :, H:2 * H]

    def flag(eng):
        _, r = nc.values_load_multi_w_load_instructions(far[0:1, 0:1], engines=[eng.engine], min_val=0, max_val=1)
        return r[0]

    with nc.Block() as block:
        @block.gpsimd
        def _(pool):
            with pool.If(flag(pool) > 0):
                with pool.Fori(0, NG) as g:
                    pool.wait_ge(hot, g + 1)
                    pool.sem_inc(go, 1)
                    for w in range(WIN):
                        pool.indirect_dma_start(rows[:, w, :], None, m.table[H],
                                                bass.IndirectOffsetOnAxis(ap=idx[:, w:w + 1], axis=0)).then_inc(fetched, 16)

        @block.tensor
        def _(pe):
            with pe.If(flag(pe) > 0):
                with pe.Fori(0, NG) as g:
                    pe.wait_ge(hot, g + 1)
                    for w in range(WIN):
                        ins = pe.transpose(m.bank[0][0:P, w * 128:(w + 1) * 128], one[:, w, :], m.ident[:, :])
                    ins.then_inc(turned, 1)
                    for h in range(H):
                        pe.wait_ge(widened, g * H + (h + 1))
                        for w in range(WIN):
                            ins = pe.matmul(m.bank[1][0:P, w * 128:(w + 1) * 128], wide[:, w, :], m.ident[:, :], start=True, stop=True)
                        ins.then_inc(spread, 1)

        @block.vector
        def _(v):
            with v.If(flag(v) > 0):
                k = Chain(v, chain, 1)
                k.step(0)
                if H == 1:
                    k.link(v.tensor_copy(best[:, :, :], m.acc[:, :, D:D + 1]))
                else:
                    k.link(v.memset(best[:, :, :], -FLOOR))
                k = Chain(v, chain, 1 + WIN + 1 + H * (WIN + 3))
                with v.Fori(0, NG) as g:
                    k.step(g)
                    k.base = k.base + 1
                    _, tile = nc.values_load_multi_w_load_instructions(m.gtab[0:1, 0, bass.ds(g, 1)], engines=[v.engine],
                                                                       min_val=0, max_val=NT - 1)
                    k.link(v.tensor_copy(idx[:, :], m.eall[:, bass.ds(g * 4, 4)].rearrange("p (w x) -> p w x", x=2)[:, :, 0]))
                    for w in range(WIN):
                        k.link(v.tensor_scalar(one[:, w, :], m.count[:, :], m.local[:, bass.ds(g * WIN + w, 1)], None, ALU.is_equal))
                    v.sem_inc(hot, 1)
                    v.wait_ge(turned, g + 1)
                    k.link(v.tensor_scalar(push[:, :], m.bank[0][0:P, 0:WIN * 128], -1.0, FLOOR, ALU.add, ALU.mult))
                    v.wait_ge(fetched, g * (16 * WIN) + 16 * WIN)
                    for h in range(H):
                        for w in range(WIN):
                            k.link(v.tensor_scalar(wide[:, w, :], m.ones[:, 0:P], rows[:, w, D + h:D + h + 1], None, ALU.mult))
                        v.sem_inc(widened, 1)
                        v.wait_ge(spread, g * H + (h + 1))
                        k.link(v.tensor_tensor(cand[:, :], m.bank[1][0:P, 0:WIN * 128], push[:, :], ALU.add))
                        k.link(v.tensor_reduce(top[:, :], cand[:, :], AX.X, ALU.max))
                        mine = row_of(best[:, :, h:h + 1], tile[0])
                        k.link(v.tensor_tensor(mine, mine, top[:, :], ALU.max))
                    k.close()
                k = Chain(v, bound, 3)
                k.link(v.tensor_tensor(adm_m, adm_a, best[:, :, :], ALU.add))
                k.link(v.tensor_scalar(low[:, :, :], adm_m, SLOPE, None, ALU.mult))
                k.link(v.tensor_tensor(adm_m, adm_m, low[:, :, :], ALU.max))


def edge_sums(nc, m, tag, H):
    T, R = 8, 8
    W = table_width(H)
    PW = 2 * WIN
    NP = NG // 2
    NR = NP // T
    with Stage(nc) as c:
        def sb(n, s, d=F32):
            return c.enter_context(nc.sbuf_tensor(tag + n, s, d))

        def sem(n):
            return c.sem(tag + n)

        idx = sb("_idx", [128, R, PW], I32)
        rows = sb("_rows", [128, R, PW, W])
        one = sb("_one", [128, T, PW, P])
        oneT = sb("_oneT", [P, 2, PW * 128])
        stage = sb("_stage", [P, 4, 2, 2 * H])
        if H == 1:
            wts = sb("_wts", [128, 2, PW, 1])
            won = sb("_won", [128, 2, PW, P])
        else:
            msg = sb("_msg", [128, 2, PW, D + H])
        z = sb("_z", [128, 2, PW, H])
        y = sb("_y", [128, 2, PW, H])
        gathered = [sem(f"_gathered{r}") for r in range(R)]
        staged, turned, kept, scored, zed, exped = sem("_staged"), sem("_turned"), sem("_kept"), sem("_scored"), sem("_zed"), sem("_exped")
        numbered = sem("_numbered")
        msged, summed, added, chain, go = sem("_msged"), sem("_summed"), sem("_added"), sem("_chain"), sem("_go")
        turn_banks = (m.bank[0], m.bank[7])
        sum_banks = [m.bank[2:4], m.bank[4:6]]
        scores_of = [m.bank[i][:, 0:PW * 2 * H].rearrange("p (w x) -> p w x", w=PW) for i in (1, 6)]

        def valid(q):
            return not isinstance(q, int) or 0 <= q < NP

        def wait(eng, sem, value):
            if not isinstance(value, int) or value > 0:
                eng.wait_ge(sem, value)

        def rounds(eng, body):
            for u in range(T):
                body(0, u)
            with eng.Fori(1, NR - 1) as b:
                for u in range(T):
                    body(b, u)
            for u in range(T):
                body(NR - 1, u)
            for u in range(4):
                body(NR, u)

        def tiles_of(eng, g, n):
            _, tiles = nc.values_load_multi_w_load_instructions(m.gtab[0:1, 0, bass.ds(g, n)], engines=[eng.engine],
                                                                min_val=0, max_val=NT - 1)
            return tiles

        with nc.Block() as block:
            @block.gpsimd
            def _(pool):
                def body(b, r):
                    q = b * T + r
                    pool.wait_ge(numbered, q + 1)
                    wait(pool, summed if H == 1 else msged, q - (R - 1))
                    pool.sem_inc(go, 1)
                    for w in range(PW):
                        pool.indirect_dma_start(rows[:, r % R, w, :], None, m.table[H],
                                                bass.IndirectOffsetOnAxis(ap=idx[:, r % R, w:w + 1], axis=0)).then_inc(gathered[r % R], 16)

                for r in range(T):
                    body(0, r)
                with pool.Fori(1, NR) as b:
                    for r in range(T):
                        body(b, r)

            @block.tensor
            def _(pe):
                def body(b, u):
                    q = b * T + u
                    if valid(q):
                        pe.wait_ge(staged, q + 1)
                        wait(pe, kept, q - 1)
                        for w in range(PW):
                            ins = pe.transpose(turn_banks[u % 2][0:P, w * 128:(w + 1) * 128], one[:, u, w, :], m.ident[:, :])
                        ins.then_inc(turned, 1)
                    if valid(q - 1):
                        u1 = (u - 1) % T
                        pe.wait_ge(kept, q)
                        wait(pe, zed, q - 2)
                        for w in range(PW):
                            ins = pe.matmul(scores_of[u1 % 2][:, w, :], oneT[:, u1 % 2, w * 128:(w + 1) * 128],
                                            stage[:, u1 % 4, w // WIN, :], start=True, stop=True)
                        ins.then_inc(scored, 1)
                    q3, u3 = q - 3, (u - 3) % T
                    if valid(q3):
                        pe.wait_ge(msged, q3 + 1)
                        wait(pe, added, q3 * 2 - 2)
                        for w in range(PW):
                            left, right = (won[:, u3 % 2, w, :], rows[:, u3 % R, w, :]) if H == 1 else (one[:, u3, w, :], msg[:, u3 % 2, w, :])
                            ins = pe.matmul(sum_banks[u3 % 2][w // WIN][0:P, 0:W], left, right,
                                            start=(w % WIN == 0), stop=(w % WIN == WIN - 1))
                        ins.then_inc(summed, 1)

                rounds(pe, body)

            @block.scalar
            def _(a):
                def body(b, u):
                    q = b * T + u
                    q3, u3 = q - 3, (u - 3) % T
                    if valid(q3):
                        a.wait_ge(zed, q3 + 1)
                        a.activation(wts[:, u3 % 2, :, :] if H == 1 else msg[:, u3 % 2, :, D:D + H], z[:, u3 % 2, :, :],
                                     ACT.Exp).then_inc(exped, 1)
                    if valid(q):
                        tiles = tiles_of(a, q * 2, 2)
                        wait(a, scored, q - 1)
                        for i in range(2):
                            a.activation(stage[:, u % 4, i, :], row_of(m.adm[:, :, 0:2 * H], tiles[i]), ACT.Copy)
                        a.wait_ge(turned, q + 1)
                        a.activation(oneT[:, u % 2, :], turn_banks[u % 2][0:P, 0:PW * 128], ACT.Copy).then_inc(kept, 1)

                rounds(a, body)

            @block.vector
            def _(v):
                def number(q, u):
                    v.tensor_copy(idx[:, u, :], m.eall[:, bass.ds(q * 8, 8)].rearrange("p (w x) -> p w x", x=2)[:, :, 0]).then_inc(numbered, 1)

                def add(q, u, i):
                    wait(v, added, q * 2 + i)
                    acc = row_of(m.acc[:, :, 0:W], tiles[2 * (u % 4) + i])
                    v.tensor_tensor(acc, acc, sum_banks[u % 2][i][0:P, 0:W], ALU.add).then_inc(added, 1)

                for q in range(R - 3):
                    number(q, q)
                tiles = []

                def body(b, u):
                    q = b * T + u
                    q3, u3 = q - 3, (u - 3) % T
                    q4, q5 = q - 4, q - 5
                    turn = q3 // R if isinstance(q3, int) else b * (T // R) + (u - 3) // R
                    zq, yq = z[:, u3 % 2, :, :], y[:, u3 % 2, :, :]
                    if valid(q3):
                        v.wait_ge(scored, q3 + 1)
                        v.wait_ge(gathered[u3 % R], turn * (16 * PW) + 16 * PW)
                    if valid(q5):
                        v.wait_ge(summed, q5 + 1)
                    for w in range(PW):
                        if valid(q3) and w == 0:
                            v.tensor_tensor(zq, rows[:, u3 % R, :, D:D + H], scores_of[u3 % 2][:, :, 0:H], ALU.add).then_inc(chain, 1)
                        if valid(q3) and w == 1:
                            v.wait_ge(chain, q3 * 3 + 1)
                            v.scalar_tensor_tensor(yq, zq, SLOPE, zq, ALU.mult, ALU.max).then_inc(chain, 1)
                        if valid(q3) and w == 2:
                            v.wait_ge(chain, q3 * 3 + 2)
                            v.tensor_tensor(zq, yq, scores_of[u3 % 2][:, :, H:2 * H], ALU.subtract).then_inc(chain, 1)
                        if valid(q3) and w == 3:
                            v.wait_ge(chain, q3 * 3 + 3)
                            v.tensor_scalar(zq, zq, 0.0, None, ALU.min).then_inc(zed, 1)
                        if valid(q):
                            ins = v.tensor_scalar(one[:, u, w, :], m.count[:, :], m.local[:, bass.ds(q * PW + w, 1)], None, ALU.is_equal)
                            if w == PW - 1:
                                ins.then_inc(staged, 1)
                    if valid(q + R - 3):
                        number(q + R - 3, u3 % R)
                    if valid(q3) and H == 1:
                        v.wait_ge(exped, q3 + 1)
                        for w in range(PW):
                            ins = v.tensor_scalar(won[:, u3 % 2, w, :], m.count[:, :], m.local[:, bass.ds(q3 * PW + w, 1)],
                                                  wts[:, u3 % 2, w, :], ALU.is_equal, ALU.mult)
                        ins.then_inc(msged, 1)
                    if valid(q3) and H > 1:
                        v.wait_ge(exped, q3 + 1)
                        for w in range(PW):
                            ins = v.tensor_tensor(msg[:, u3 % 2, w, 0:D].rearrange("p (h x) -> p h x", h=H),
                                                  rows[:, u3 % R, w, 0:D].rearrange("p (h x) -> p h x", h=H),
                                                  msg[:, u3 % 2, w, D:D + H].unsqueeze(2).to_broadcast([128, H, D // H]), ALU.mult)
                        ins.then_inc(msged, 1)
                    if valid(q4):
                        if u % 4 == 0:
                            tiles[:] = tiles_of(v, q4 * 2, 8)
                        v.wait_ge(summed, q4 + 1)
                        add(q4, u, 0)
                        add(q4, u, 1)

                rounds(v, body)
                v.wait_ge(added, 2 * NP)


def graph_attention0(nc, m):
    with Stage(nc) as c:
        def sb(n, s):
            return c.enter_context(nc.sbuf_tensor("cell_" + n, s, F32))

        def sem(n):
            return c.sem("cell_" + n)

        rden = sb("rden", [P, NT])
        hb = sb("hb", [P, 2, D])
        hbT = sb("hbT", [128, 2, KD, P])
        gio = sb("gio", [P, 2, 2 * D])
        gg = sb("gg", [P, 2, D])
        cc = sb("cc", [P, 2, D])
        tc = sb("tc", [P, 2, D])
        inv, agged, tanhed, turned, kept, gated, acted = sem("inv"), sem("agged"), sem("tanhed"), sem("turned"), sem("kept"), sem("gated"), sem("acted")
        celled, ctanhed, hid, addd = sem("celled"), sem("ctanhed"), sem("hid"), sem("addd")
        zrow = SPARE * ROWS // 128
        zrows = c.enter_context(nc.sbuf_tensor("cell_zrows", [128, zrow, D], F32))
        zeroed, cleared = sem("zeroed"), sem("cleared")
        with nc.Block() as block:
            @block.gpsimd
            def _(pool):
                pool.memset(zrows[:, :, :], 0.0).then_inc(zeroed, 1)

            @block.sync
            def _(sp):
                sp.wait_ge(zeroed, 1)
                sp.dma_start(m.xsort[SORTED - SPARE * ROWS:SORTED, :].rearrange("(p w) d -> p w d", p=128), zrows[:, :, :]).then_inc(cleared, 16)
                sp.wait_ge(cleared, 16)

            @block.vector
            def _(v):
                v.reciprocal(rden[:, :], m.acc[:, :, D + 1]).then_inc(inv, 1)
                v.wait_ge(inv, 1)

                def body(t, s):
                    if valid(t - 5):
                        v.wait_ge(ctanhed, t - 4)
                        v.tensor_tensor(cc[:, 1 - s, :], gio[:, 1 - s, D:2 * D], tc[:, 1 - s, :], ALU.mult).then_inc(hid, 1)
                    if valid(t):
                        wait_count(v, turned, t - 1)
                        v.scalar_tensor_tensor(hb[:, s, :], row_of(m.acc[:, :, 0:D], t), rden[:, bass.ds(t, 1)], m.gbias[:, :],
                                               ALU.mult, ALU.add).then_inc(agged, 1)
                    if valid(t - 5):
                        v.wait_ge(hid, t - 4)
                        x = row_of(m.xs, t - 5)
                        v.tensor_tensor(x, x, cc[:, 1 - s, :], ALU.add).then_inc(addd, 1)
                    if valid(t - 6):
                        wait_count(v, addd, t - 5)
                        v.bn_stats(row_of(m.stats, t - 6), row_of(m.xs, t - 6))
                    if valid(t - 3):
                        v.wait_ge(acted, t - 2)
                        wait_count(v, addd, t - 4)
                        v.tensor_tensor(cc[:, 1 - s, :], gio[:, 1 - s, 0:D], gg[:, 1 - s, :], ALU.mult).then_inc(celled, 1)

                pipelined(v, body, 6)

            @block.scalar
            def _(a):
                def body(t, s):
                    if valid(t):
                        a.wait_ge(agged, t + 1)
                        a.activation(hb[:, s, :], hb[:, s, :], ACT.Tanh).then_inc(tanhed, 1)
                    if valid(t - 3):
                        a.wait_ge(gated, t - 2)
                        wait_count(a, hid, t - 4)
                        a.activation(gio[:, 1 - s, :], m.bank[4 - 2 * s][0:P, 0:2 * D], ACT.Sigmoid)
                        a.activation(gg[:, 1 - s, :], m.bank[5 - 2 * s][0:P, 0:D], ACT.Tanh).then_inc(acted, 1)
                    if valid(t - 1):
                        a.wait_ge(turned, t)
                        wait_count(a, gated, t - 2)
                        a.activation(hbT[:, 1 - s, :, :], by_feature(m.bank[1 - s]), ACT.Copy).then_inc(kept, 1)
                    if valid(t - 4):
                        a.wait_ge(celled, t - 3)
                        a.activation(tc[:, s, :], cc[:, s, :], ACT.Tanh).then_inc(ctanhed, 1)

                pipelined(a, body, 4)

            @block.tensor
            def _(pe):
                def body(t, s):
                    if valid(t - 1):
                        pe.wait_ge(tanhed, t)
                        wait_count(pe, kept, t - 2)
                        for k in range(KD):
                            ins = pe.transpose(m.bank[1 - s][:, k * 128:k * 128 + P], hb[:, 1 - s, k * 128:(k + 1) * 128], m.ident[0:P, 0:P])
                        ins.then_inc(turned, 1)
                    if valid(t - 2):
                        pe.wait_ge(kept, t - 1)
                        wait_count(pe, acted, t - 3)
                        for k in range(KD):
                            pe.matmul(m.bank[2 + 2 * s][0:P, 0:2 * D], hbT[:, s, k, :], m.gatew[:, k, 0:2 * D], start=(k == 0), stop=(k == KD - 1))
                        for k in range(KD):
                            ins = pe.matmul(m.bank[3 + 2 * s][0:P, 0:D], hbT[:, s, k, :], m.gatew[:, k, 2 * D:3 * D], start=(k == 0), stop=(k == KD - 1))
                        ins.then_inc(gated, 1)

                pipelined(pe, body, 2)


def mix0_keys(nc, m):
    G = 2 * HEADS
    with Stage(nc) as c:
        def sb(n, s):
            return c.enter_context(nc.sbuf_tensor("keys_" + n, s, F32))

        def sem(n):
            return c.sem("keys_" + n)

        xst = sb("xst", [128, 2, KD, P])
        kv = sb("kv", [P, 4, 2 * D])
        sq = sb("sq", [P, 2, 2 * D])
        var = sb("var", [P, 2, G])
        rs = sb("rs", [P, 2, G])
        zeros = sb("zeros", [P, 128])
        xstaged, made, biased, squared, reduced, varred, powered, normed, summed, zeroed = [
            sem(n) for n in ("staged", "made", "biased", "squared", "reduced", "varred", "powered", "normed", "summed", "zeroed")]
        norm_chain, kept = sem("norm_chain"), sem("kept")
        edges_in = [sem(f"edges_in{s}") for s in range(8)]
        with nc.Block() as block:
            @block.sync
            def _(sp):
                load_edges(nc, m, sp, edges_in, *EDGE_PARTS[1])

            @block.scalar
            def _(a):
                def body(t, s):
                    if valid(t):
                        wait_count(a, made, t - 1)
                        a.activation(xst[:, s % 2, :, :], m.xT[:, :, tile_cols(t)], ACT.Copy).then_inc(xstaged, 1)
                    if valid(t - 1):
                        a.wait_ge(biased, t)
                        wait_count(a, reduced, t - 2)
                        a.activation(sq[:, (s - 1) % 2, :], kv[:, (s - 1) % 4, :], ACT.Square).then_inc(squared, 1)

                pipelined(a, body, 1, 4)

            @block.tensor
            def _(pe):
                pe.wait_ge(zeroed, 1)
                pe.matmul(m.bank[2][:, 0:D], zeros[:, :], zeros[:, :].unsqueeze(1).to_broadcast([P, KD, 128]), start=True, stop=False)

                def body(t, s):
                    if valid(t):
                        pe.wait_ge(xstaged, t + 1)
                        wait_count(pe, biased, t - 1)
                        for k in range(KD):
                            ins = pe.matmul(m.bank[s % 2][0:P, :], xst[:, s % 2, k, :], m.wkv[:, k, :], start=(k == 0), stop=(k == KD - 1))
                        ins.then_inc(made, 1)
                    if valid(t - 4):
                        o = s
                        pe.wait_ge(normed, t - 3)
                        for k in range(KD):
                            ins = pe.matmul(m.bank[2][:, k * 128:(k + 1) * 128], kv[:, o, k * 128:(k + 1) * 128],
                                            kv[:, o, D + k * 128:D + (k + 1) * 128], start=False, stop=False, skip_group_check=True)
                        ins.then_inc(summed, 1)

                pipelined(pe, body, 4, 4)
                pe.matmul(m.bank[2][:, 0:D], zeros[:, :], zeros[:, :].unsqueeze(1).to_broadcast([P, KD, 128]),
                          start=False, stop=True).then_inc(summed, 1)

            @block.gpsimd
            def _(pool):
                def body(t, s):
                    pool.wait_ge(varred, t + 1)
                    wait_count(pool, norm_chain, (t - 2) * 2 + 1)
                    pool.tensor_tensor(rs[:, s, :], var[:, s, :], m.half[0:P, 0:G], ALU.pow).then_inc(powered, 1)

                pipelined(pool, body, 0)

            @block.vector
            def _(v):
                v.memset(zeros[:, :], 0.0).then_inc(zeroed, 1)

                def grouped(x):
                    return x.rearrange("p (g c) -> p g c", c=HC)

                def body(t, s):
                    o1, o3 = (s - 1) % 2, (s - 3) % 4
                    if valid(t - 1):
                        v.wait_ge(squared, t)
                        wait_count(v, powered, t - 2)
                        v.tensor_reduce(var[:, o1, :], grouped(sq[:, o1, :]), AX.X, ALU.add).then_inc(reduced, 1)
                    if valid(t - 3):
                        v.wait_ge(powered, t - 2)
                        v.tensor_tensor(grouped(kv[:, o3, :]), grouped(kv[:, o3, :]),
                                        rs[:, o3 % 2, :].unsqueeze(2).to_broadcast([P, G, HC]), ALU.mult).then_inc(norm_chain, 1)
                    if valid(t - 1):
                        v.wait_ge(reduced, t)
                        v.tensor_scalar(var[:, o1, :], var[:, o1, :], 1.0 / HC, EPS, ALU.mult, ALU.add).then_inc(varred, 1)
                    if valid(t - 3):
                        v.wait_ge(norm_chain, t * 2 - 5)
                        v.tensor_tensor(kv[:, o3, :], kv[:, o3, :], m.lng[:, :], ALU.mult).then_inc(norm_chain, 1)
                    if valid(t):
                        v.wait_ge(made, t + 1)
                        wait_count(v, summed, t - 3)
                        v.tensor_tensor(kv[:, s, :], m.bank[s % 2][0:P, :], m.bkv[:, :], ALU.add).then_inc(biased, 1)
                    if valid(t - 3):
                        v.wait_ge(norm_chain, t * 2 - 4)
                        v.tensor_tensor(kv[:, o3, :], kv[:, o3, :], m.lnb[:, :], ALU.add).then_inc(normed, 1)

                pipelined(v, body, 3, 4)
                v.wait_ge(summed, NT + 1)
                v.tensor_scalar(m.kv[:, :, :].rearrange("p k n -> p (k n)"), m.bank[2][:, 0:D], 1.0 / N, None, ALU.mult).then_inc(kept, 1)
                v.wait_ge(kept, 1)
                v.tensor_tensor(m.kv[:, :, :], m.kv[:, :, :], m.headmask[:, :].unsqueeze(1).to_broadcast([128, KD, 128]), ALU.mult)


def mix0_queries(nc, m):
    with Stage(nc) as c:
        def sb(n, s):
            return c.enter_context(nc.sbuf_tensor("query_" + n, s, F32))

        def sem(n):
            return c.sem("query_" + n)

        qT = sb("qT", [128, 2, KD, P])
        ret = sb("ret", [128, 2, KD, P])
        queried, qkept, mixed, returned, hidden, hkept = [sem(n) for n in ("queried", "qkept", "mixed", "returned", "hidden", "hkept")]
        edges_in = [sem(f"edges_in{s}") for s in range(8)]
        with nc.Block() as block:
            @block.sync
            def _(sp):
                load_edges(nc, m, sp, edges_in, *EDGE_PARTS[2])

            @block.tensor
            def _(pe):
                def body(t, s):
                    if valid(t):
                        wait_count(pe, qkept, t - 1)
                        for o in range(KD):
                            for k in range(KD):
                                ins = pe.matmul(m.bank[s][:, o * 128:o * 128 + P], m.wq[:, k, o * 128:(o + 1) * 128],
                                                m.xT[:, k, tile_cols(t)], start=(k == 0), stop=(k == KD - 1))
                        ins.then_inc(queried, 1)
                    if valid(t - 1):
                        pe.wait_ge(qkept, t)
                        wait_count(pe, returned, t - 2)
                        for k in range(KD):
                            ins = pe.matmul(m.bank[3 - s][:, k * 128:k * 128 + P], m.kv[:, k, :], qT[:, 1 - s, k, :], start=True, stop=True)
                        ins.then_inc(mixed, 1)
                    if valid(t - 2):
                        pe.wait_ge(returned, t - 1)
                        wait_count(pe, hkept, t - 3)
                        for o in range(KD):
                            for k in range(KD):
                                ins = pe.matmul(m.bank[4 + s][:, o * 128:o * 128 + P], m.w1[:, k, o * 128:(o + 1) * 128],
                                                ret[:, s, k, :], start=(k == 0), stop=(k == KD - 1))
                        ins.then_inc(hidden, 1)

                pipelined(pe, body, 2)

            @block.scalar
            def _(a):
                def body(t, s):
                    if valid(t):
                        a.wait_ge(queried, t + 1)
                        wait_count(a, mixed, t - 1)
                        for k in range(KD):
                            ins = a.activation(qT[:, s, k, :], m.bank[s][:, k * 128:k * 128 + P], ACT.Identity, bias=m.bq[:, k:k + 1])
                        ins.then_inc(qkept, 1)
                    if valid(t - 2):
                        a.wait_ge(hidden, t - 1)
                        a.activation(m.xT[:, :, tile_cols(t - 2)], by_feature(m.bank[4 + s]), ACT.Copy).then_inc(hkept, 1)

                pipelined(a, body, 2)

            @block.vector
            def _(v):
                def body(t, s):
                    v.wait_ge(mixed, t + 1)
                    wait_count(v, hidden, t - 1)
                    v.tensor_tensor(ret[:, s, :, :], by_feature(m.bank[2 + s]), m.xT[:, :, tile_cols(t)], ALU.add).then_inc(returned, 1)

                pipelined(v, body, 0)


def mix0_out(nc, m):
    with Stage(nc) as c:
        def sb(n, s):
            return c.enter_context(nc.sbuf_tensor("mixout_" + n, s, F32))

        def sem(n):
            return c.sem("mixout_" + n)

        hT = sb("hT", [128, 2, KD, P])
        bent, made, biased, added = [sem(n) for n in ("bent", "made", "biased", "added")]
        edges_in = [sem(f"edges_in{s}") for s in range(8)]
        with nc.Block() as block:
            @block.sync
            def _(sp):
                load_edges(nc, m, sp, edges_in, *EDGE_PARTS[3])

            @block.scalar
            def _(a):
                def body(t, s):
                    wait_count(a, made, t - 1)
                    for k in range(KD):
                        ins = a.activation(hT[:, s, k, :], m.xT[:, k, tile_cols(t)], ACT.Gelu, bias=m.b1[:, k:k + 1])
                    ins.then_inc(bent, 1)

                pipelined(a, body, 0)

            @block.tensor
            def _(pe):
                def body(t, s):
                    pe.wait_ge(bent, t + 1)
                    wait_count(pe, added, t - 1)
                    for k in range(KD):
                        ins = pe.matmul(m.bank[s][0:P, 0:D], hT[:, s, k, :], m.w2[:, k, :], start=(k == 0), stop=(k == KD - 1))
                    ins.then_inc(made, 1)

                pipelined(pe, body, 0)

            @block.vector
            def _(v):
                def body(t, s):
                    x = row_of(m.xs, t)
                    v.tensor_tensor(x, x, m.b2[:, :], ALU.add).then_inc(biased, 1)
                    v.wait_ge(biased, t + 1)
                    v.wait_ge(made, t + 1)
                    v.tensor_tensor(x, x, m.bank[s][0:P, 0:D], ALU.add).then_inc(added, 1)

                pipelined(v, body, 0)


def experts_route(nc, m, tag, gw, gb, weighted):
    B = 5
    with Stage(nc) as c:
        def sb(n, s, d=F32):
            return c.enter_context(nc.sbuf_tensor(tag + n, s, d))

        def sem(n):
            return c.sem(tag + n)

        gws = sb("_gws", [128, KD, NE])
        gbs = sb("_gbs", [P, NE])
        shift = sb("_shift", [P, NT])
        xn = sb("_xn", [P, 2, D])
        xst = sb("_xst", [128, 2, KD, P])
        lg = sb("_lg", [P, NT, NE])
        ie = sb("_ie", [128, NE])
        region = sb("_region", [128, NE])
        jn = sb("_jn", [128, 1])
        one = [sb(f"_one{i}", [P, NT, NE]) for i in range(2)]
        part = sb("_part", [P, NT, NE])
        first = sb("_first", [128, NE])
        yplace = sb("_yplace", [P, NT])
        eq = sb("_eq", [P, B, NE])
        mask = sb("_mask", [P, B, NE])
        cum = sb("_cum", [P, B + 1, NE])
        best = sb("_best", [P, 2, NT])
        low = sb("_low", [P, B])
        placef = sb("_placef", [P, B])
        ex = sb("_ex", [P, NT, NE])
        e2 = sb("_e2", [P, NT])
        zsum = sb("_zsum", [P, NT])
        zero = sb("_zero", [128, NE])
        zrows = sb("_zrows", [128, ROWS // 128, D])
        count = sb("_count", [128, NE])
        tail = sb("_tail", [128, NE])
        tail_i = sb("_tail_i", [1, NE], I32)
        nbi = sb("_nbi", [128, NE], I32)
        nb = sb("_nb", [128, NE])
        bend = sb("_bend", [128, NE])
        past = sb("_past", [128, NE])
        bt = sb("_bt", [128, 2])
        loaded, chain, normed, turned, staged, logged, kept, numbered, copied, zeroed = [
            sem(n) for n in ("_loaded", "_chain", "_normed", "_turned", "_staged", "_logged", "_kept", "_numbered", "_copied", "_zeroed")]
        masked, ranked, placed, scattered, chosen, exped, counted, tailed, tails_in, tabled, turned2 = [
            sem(n) for n in ("_masked", "_ranked", "_placed", "_scattered", "_chosen", "_exped", "_counted", "_tailed",
                             "_tails_in", "_tabled", "_turned2")]

        def over(x, n):
            return x.unsqueeze(2).to_broadcast([P, n, NE])

        with nc.Block() as block:
            @block.sync
            def _(sp):
                sp.dma_start(gws[:, :, :], gw.rearrange("(k p) e -> p k e", p=128)).then_inc(loaded, 16)
                sp.dma_start(gbs[:, :], gb.partition_broadcast(P)).then_inc(loaded, 16)
                sp.wait_ge(zeroed, 1)
                sp.wait_ge(tailed, 1)
                _, at = nc.values_load_multi_w_load_instructions(tail_i[0:1, 0:NE], engines=[sp.engine], min_val=0,
                                                                 max_val=NE * REGION * ROWS - ROWS)
                for e in range(NE):
                    sp.dma_start(m.xsort[bass.ds(at[e], ROWS), :].rearrange("(p w) d -> p w d", p=128), zrows[:, :, :]).then_inc(tails_in, 16)
                sp.wait_ge(tails_in, 16 * NE)

            @block.gpsimd
            def _(pool):
                pool.iota(ie[:, :], pattern=[[1, NE]], base=0, channel_multiplier=0,
                          allow_small_or_imprecise_dtypes=True).then_inc(numbered, 1)
                pool.iota(region[:, :], pattern=[[REGION * ROWS, NE]], base=0, channel_multiplier=0,
                          allow_small_or_imprecise_dtypes=True).then_inc(numbered, 1)
                pool.iota(jn[:, :], pattern=[[0, 1]], base=0, channel_multiplier=1,
                          allow_small_or_imprecise_dtypes=True).then_inc(numbered, 1)
                pool.memset(zrows[:, :, :], 0.0).then_inc(zeroed, 1)
                for t in range(NT):
                    if t % B == 0:
                        pool.wait_ge(placed, t // B + 1)
                        pool.wait_ge(copied, t + B)
                    for i in range(2):
                        pool.indirect_dma_start(m.xsort, bass.IndirectOffsetOnAxis(ap=m.slots[:, t, i:i + 1], axis=0),
                                                m.acc[:, t, 0:D], None).then_inc(scattered, 16)
                pool.wait_ge(scattered, 16 * 2 * NT)

            @block.tensor
            def _(pe):
                pe.wait_ge(loaded, 32)

                def turn(t):
                    pe.wait_ge(normed, t + 1)
                    if t >= 2:
                        pe.wait_ge(staged, t - 1)
                    for k in range(KD):
                        ins = pe.transpose(m.bank[t % 2][:, k * 128:k * 128 + P], xn[:, t % 2, k * 128:(k + 1) * 128], m.ident[0:P, 0:P])
                    ins.then_inc(turned, 1)

                def score(t):
                    pe.wait_ge(staged, t + 1)
                    if t >= 2:
                        pe.wait_ge(kept, t - 1)
                    for k in range(KD):
                        ins = pe.matmul(m.bank[2 + t % 2][0:P, 0:NE], xst[:, t % 2, k, :], gws[:, k, :], start=(k == 0), stop=(k == KD - 1))
                    ins.then_inc(logged, 1)

                def rank(i):
                    pe.wait_ge(masked, i + 1)
                    out = m.bank[4][0:P, 0:B * NE]
                    pe.matmul(out, m.before[:, :], mask[:, :, :].rearrange("p t e -> p (t e)"), start=True, stop=False)
                    pe.matmul(out, m.ones[0:P, 0:P], cum[:, 0:B, :].rearrange("p t e -> p (t e)"), start=False, stop=True).then_inc(ranked, 1)

                for i in range(NT // B + 1):
                    if i < NT // B:
                        for t in range(i * B, (i + 1) * B):
                            turn(t)
                            if t > i * B:
                                score(t - 1)
                        score((i + 1) * B - 1)
                    if i > 0:
                        rank(i - 1)
                pe.matmul(m.bank[5][:, 0:NE], m.ones[0:P, :], cum[:, B, :], start=True, stop=True).then_inc(counted, 1)
                pe.wait_ge(tabled, 1)
                for x in range(2):
                    ins = pe.transpose(m.bank[6][0:1, x * 128:(x + 1) * 128], bt[:, x:x + 1], m.ident[:, :])
                ins.then_inc(turned2, 1)

            @block.scalar
            def _(a):
                def body(t, s):
                    a.wait_ge(normed, t + 1)
                    a.activation(row_of(m.acc[:, :, 0:D], t), xn[:, s, :], ACT.Copy).then_inc(copied, 1)
                    a.wait_ge(turned, t + 1)
                    wait_count(a, logged, t - 1)
                    a.activation(xst[:, s, :, :], by_feature(m.bank[s]), ACT.Copy).then_inc(staged, 1)

                pipelined(a, body, 0)
                if weighted:
                    a.wait_ge(chosen, 1)
                    a.activation(ex[:, :, :], ex[:, :, :], ACT.Exp).then_inc(exped, 1)
                    a.activation(e2[:, :], e2[:, :], ACT.Exp).then_inc(exped, 1)

            @block.vector
            def _(v):
                k = Chain(v, chain, 0)
                k.link(v.scalar_tensor_tensor(shift[:, :], m.mean[:, :], -1.0, m.rstd[:, :], ALU.mult, ALU.mult))
                k.link(v.memset(zero[:, :], 0.0))
                k.link(v.memset(cum[:, B, :], 0.0))
                v.wait_ge(loaded, 32)
                v.wait_ge(numbered, 3)

                def norm(t):
                    if t >= 2:
                        v.wait_ge(turned, t - 1)
                        v.wait_ge(copied, t - 1)
                    v.tensor_scalar(xn[:, t % 2, :], row_of(m.xs, t), m.rstd[:, t:t + 1], shift[:, t:t + 1],
                                    ALU.mult, ALU.add).then_inc(normed, 1)

                def keep(t):
                    v.wait_ge(logged, t + 1)
                    v.tensor_tensor(row_of(lg, t), m.bank[2 + t % 2][0:P, 0:NE], gbs[:, :], ALU.add).then_inc(kept, 1)

                def choose(i):
                    src = lg[:, i * B:(i + 1) * B, :]
                    if i > 0:
                        v.wait_ge(ranked, i)
                    k.link(v.tensor_copy(cum[:, 0, :], cum[:, B, :]))
                    for x in range(2):
                        top = best[:, x, i * B:(i + 1) * B]
                        k.link(v.tensor_reduce(top, src, AX.X, ALU.max))
                        k.link(v.tensor_tensor(eq[:, :, :], src, over(top, B), ALU.is_equal))
                        yield
                        k.link(v.scalar_tensor_tensor(eq[:, :, :], eq[:, :, :], -100.0, ie[0:P, :].unsqueeze(1).to_broadcast([P, B, NE]),
                                                      ALU.mult, ALU.add))
                        k.link(v.tensor_reduce(low[:, :], eq[:, :, :], AX.X, ALU.min))
                        yield
                        k.link(v.tensor_tensor(one[x][:, i * B:(i + 1) * B, :], eq[:, :, :], over(low[:, :], B), ALU.is_equal))
                        if x == 0:
                            k.link(v.scalar_tensor_tensor(mask[:, :, :], one[0][:, i * B:(i + 1) * B, :], -BIG, src, ALU.mult, ALU.add))
                            src = mask[:, :, :]
                    yield
                    k.link(v.tensor_tensor(mask[:, :, :], one[0][:, i * B:(i + 1) * B, :], one[1][:, i * B:(i + 1) * B, :], ALU.add))
                    for t in range(B):
                        k.link(v.tensor_tensor(cum[:, t + 1, :], cum[:, t, :], mask[:, t, :], ALU.add))
                    v.sem_inc(masked, 1)

                def place(i):
                    v.wait_ge(ranked, i + 1)
                    k.link(v.tensor_tensor(eq[:, :, :], m.bank[4][0:P, 0:B * NE].rearrange("p (t e) -> p t e", e=NE),
                                           region[0:P, :].unsqueeze(1).to_broadcast([P, B, NE]), ALU.add))
                    for x in range(2):
                        k.link(v.tensor_tensor(part[:, 0:B, :], one[x][:, i * B:(i + 1) * B, :], eq[:, :, :], ALU.mult))
                        k.link(v.tensor_reduce(placef[:, :], part[:, 0:B, :], AX.X, ALU.add))
                        k.link(v.tensor_copy(m.slots[:, i * B:(i + 1) * B, x], placef[:, :]))
                    v.sem_inc(placed, 1)

                for i in range(NT // B + 1):
                    steps = choose(i - 1) if i > 0 else iter(())
                    if i < NT // B:
                        for t in range(i * B, (i + 1) * B):
                            norm(t)
                            next(steps, None)
                            if t >= i * B + 2:
                                keep(t - 2)
                    for _ in steps:
                        pass
                    if i < NT // B:
                        keep((i + 1) * B - 2)
                        keep((i + 1) * B - 1)
                    if i > 0:
                        place(i - 1)
                v.wait_ge(counted, 1)
                k.link(v.tensor_copy(count[:, :], m.bank[5][:, 0:NE]))
                k.link(v.tensor_tensor(tail[:, :], count[:, :], region[:, :], ALU.add))
                v.tensor_copy(tail_i[:, :], tail[0:1, :]).then_inc(tailed, 1)
                k.link(v.tensor_scalar(nbi[:, :], count[:, :], float(ROWS - 1), None, ALU.add))
                k.link(v.tensor_scalar(nbi[:, :], nbi[:, :], 8, None, ALU.arith_shift_right))
                k.link(v.tensor_copy(nb[:, :], nbi[:, :]))
                k.link(v.tensor_tensor_scan(bend[:, :], nb[:, :], zero[:, :], 0.0, ALU.add, ALU.add))
                k.link(v.tensor_scalar(past[:, :], bend[:, :], jn[:, 0:1], None, ALU.is_le))
                k.link(v.tensor_reduce(bt[:, 0:1], past[:, :], AX.X, ALU.add))
                k.link(v.tensor_scalar(bt[:, 0:1], bt[:, 0:1], float(NE - 1), None, ALU.min))
                k.link(v.tensor_scalar(nb[:, :], nb[:, :], -1.0, float(REGION), ALU.mult, ALU.add))
                k.link(v.tensor_tensor(nb[:, :], nb[:, :], past[:, :], ALU.mult))
                k.link(v.tensor_reduce(bt[:, 1:2], nb[:, :], AX.X, ALU.add))
                k.link(v.tensor_tensor(bt[:, 1:2], bt[:, 1:2], jn[:, :], ALU.add))
                v.sem_inc(tabled, 1)
                v.wait_ge(turned2, 1)
                k.link(v.tensor_copy(m.btab[:, :, :], m.bank[6][0:1, 0:256].rearrange("o (x j) -> o x j", x=2)[:, :, 0:NB]))
                k.link(v.tensor_scalar(first[:, :], region[:, :], -1.0, None, ALU.mult))
                k.link(v.tensor_copy(nb[:, :], nbi[:, :]))
                k.link(v.tensor_tensor(bend[:, :], bend[:, :], nb[:, :], ALU.subtract))
                k.link(v.scalar_tensor_tensor(first[:, :], bend[:, :], float(ROWS), first[:, :], ALU.mult, ALU.add))
                for x in range(2):
                    k.link(v.tensor_tensor(part[:, :, :], one[x][:, :, :], first[0:P, :].unsqueeze(1).to_broadcast([P, NT, NE]), ALU.mult))
                    k.link(v.tensor_reduce(yplace[:, :], part[:, :, :], AX.X, ALU.add))
                    k.link(v.tensor_tensor(yplace[:, :], yplace[:, :], m.slots[:, :, x], ALU.add))
                    k.link(v.tensor_copy(m.yslots[:, :, x], yplace[:, :]))
                if weighted:
                    k.link(v.tensor_tensor(ex[:, :, :], lg[:, :, :], over(best[:, 0, :], NT), ALU.subtract))
                    k.link(v.tensor_tensor(e2[:, :], best[:, 1, :], best[:, 0, :], ALU.subtract))
                    v.sem_inc(chosen, 1)
                    v.wait_ge(exped, 2)
                    k.link(v.tensor_reduce(zsum[:, :], ex[:, :, :], AX.X, ALU.add))
                    k.link(v.reciprocal(m.cw[:, 0, :], zsum[:, :]))
                    k.link(v.tensor_tensor(m.cw[:, 1, :], m.cw[:, 0, :], e2[:, :], ALU.mult))


def experts_run(nc, m, tag, W1, b1, W2, b2):
    RW = ROWS // 128
    S = 4
    with Stage(nc) as c:
        def sb(n, s):
            return c.enter_context(nc.sbuf_tensor(tag + n, s, F32))

        def sem(n):
            return c.sem(tag + n)

        xb = sb("_xb", [128, S, RW, D])
        w1 = sb("_w1", [128, S, KD, HID])
        w2 = sb("_w2", [128, S, KH, D])
        b1s = sb("_b1s", [128, S, KH])
        b2s = sb("_b2s", [128, S, D])
        xbT = sb("_xbT", [128, 2, KD, ROWS])
        hT = sb("_hT", [128, 2, KH, ROWS])
        y = sb("_y", [128, 2, RW, D])
        b1t = sb("_b1t", [128, NE, KH])
        b1n = sb("_b1n", [NE * KH, 128])
        loads = [sem(f"_loads{s}") for s in range(S)]
        stored = [sem(f"_stored{s}") for s in range(2)]
        b1_in, b1_turned, b1_kept = sem("_b1_in"), sem("_b1_turned"), sem("_b1_kept")
        turned, staged, hidden, bent, made, summed = [sem(n) for n in ("_turned", "_staged", "_hidden", "_bent", "_made", "_summed")]
        turn_banks, hidden_banks, out_banks = (m.bank[0], m.bank[7]), (m.bank[1:3], m.bank[3:5]), m.bank[5:7]
        LOADS = 5

        def ok(j):
            return not isinstance(j, int) or 0 <= j < NB

        def blocks(eng, body, lag):
            for u in range(S):
                body(0, u)
            with eng.Fori(1, NB // S) as b:
                for u in range(S):
                    body(b, u)
            for u in range(lag):
                body(NB // S, u)

        assert NB % S == 0
        with nc.Block() as block:
            @block.sync
            def _(sp):
                sp.dma_start(b1n[:, :], b1.rearrange("e (k p) -> (e k) p", p=128)).then_inc(b1_in, 16)

                def load_matrices(s, e, at):
                    sp.dma_start(xb[:, s, :, :], m.xsort[bass.ds(at * ROWS, ROWS), :].rearrange("(p w) d -> p w d", p=128)).then_inc(loads[s], 16)
                    sp.dma_start(w1[:, s, :, :], W1[bass.ds(e, 1), :, :].rearrange("a (k p) h -> p (a k) h", p=128)).then_inc(loads[s], 16)
                    sp.dma_start(w2[:, s, :, :], W2[bass.ds(e, 1), :, :].rearrange("a (k p) d -> p (a k) d", p=128)).then_inc(loads[s], 16)

                def load_biases(s, e):
                    sp.dma_start(b1s[:, s, :], b1t[:, bass.ds(e, 1), :].rearrange("p a k -> p (a k)")).then_inc(loads[s], 16)
                    sp.dma_start(b2s[:, s, :], b2[bass.ds(e, 1), :].rearrange("a d -> (a d)").partition_broadcast(128)).then_inc(loads[s], 16)

                def store(j, s):
                    sp.wait_ge(summed, j + 1)
                    sp.dma_start(m.ysort[bass.ds(j * ROWS, ROWS), :].rearrange("(p w) d -> p w d", p=128), y[:, s, :, :]).then_inc(stored[s], 16)

                def table(x, at, most):
                    _, regs = nc.values_load_multi_w_load_instructions(m.btab[0:1, x, bass.ds(at, S)], engines=[sp.engine],
                                                                       min_val=0, max_val=most)
                    return regs

                def experts_of(at):
                    return table(0, at, NE - 1)

                def places_of(at):
                    return table(1, at, SORTED // ROWS - 1)

                e, to = experts_of(0), places_of(0)
                for s in range(S):
                    load_matrices(s, e[s], to[s])
                    if s == 0:
                        sp.wait_ge(b1_kept, 1)
                    load_biases(s, e[s])
                with sp.Fori(0, NB // S - 1) as b:
                    e, to = experts_of(b * S + S), places_of(b * S + S)
                    for s in range(S):
                        store(b * S + s, s % 2)
                        load_matrices(s, e[s], to[s])
                        load_biases(s, e[s])
                for s in range(S):
                    store(NB - S + s, s % 2)
                for s in range(2):
                    sp.wait_ge(stored[s], 16 * NB // 2)

            @block.tensor
            def _(pe):
                pe.wait_ge(b1_in, 16)
                pe.transpose(m.bank[0][:, 0:NE * KH], b1n[:, :], m.ident[0:NE * KH, 0:NE * KH]).then_inc(b1_turned, 1)
                pe.wait_ge(b1_kept, 1)

                def body(b, u):
                    j = b * S + u
                    s = u % 2
                    if ok(j):
                        pe.wait_ge(loads[u], b * (16 * LOADS) + 16 * LOADS)
                        wait_count(pe, staged, j - 1)
                        for w in range(RW):
                            for k in range(KD):
                                at = k * ROWS + w * 128
                                ins = pe.transpose(turn_banks[s][:, at:at + 128], xb[:, u, w, k * 128:(k + 1) * 128], m.ident[:, :])
                        ins.then_inc(turned, 1)
                    if ok(j - 1):
                        u1, s1 = (u - 1) % S, 1 - s
                        pe.wait_ge(staged, j)
                        wait_count(pe, bent, j - 2)
                        for h in range(KH):
                            for k in range(KD):
                                ins = pe.matmul(hidden_banks[s1][h // 2][:, (h % 2) * ROWS:(h % 2 + 1) * ROWS],
                                                w1[:, u1, k, h * 128:(h + 1) * 128], xbT[:, s1, k, :],
                                                start=(k == 0), stop=(k == KD - 1))
                        ins.then_inc(hidden, 1)
                    if ok(j - 2):
                        u2 = (u - 2) % S
                        pe.wait_ge(bent, j - 1)
                        wait_count(pe, summed, j - 3)
                        for w in range(RW):
                            for h in range(KH):
                                ins = pe.matmul(out_banks[s][:, w * D:(w + 1) * D], hT[:, s, h, w * 128:(w + 1) * 128], w2[:, u2, h, :],
                                                start=(h == 0), stop=(h == KH - 1))
                        ins.then_inc(made, 1)

                blocks(pe, body, 2)

            @block.scalar
            def _(a):
                def body(b, u):
                    j, s = b * S + u, u % 2
                    a.wait_ge(hidden, j + 1)
                    wait_count(a, made, j - 1)
                    for h in range(KH):
                        ins = a.activation(hT[:, s, h, :], hidden_banks[s][h // 2][:, (h % 2) * ROWS:(h % 2 + 1) * ROWS], ACT.Gelu,
                                           bias=b1s[:, u, h:h + 1])
                    ins.then_inc(bent, 1)

                blocks(a, body, 0)

            @block.vector
            def _(v):
                v.wait_ge(b1_turned, 1)
                v.tensor_copy(b1t[:, :, :].rearrange("p e k -> p (e k)"), m.bank[0][:, 0:NE * KH]).then_inc(b1_kept, 1)

                def body(b, u):
                    j, s = b * S + u, u % 2
                    if ok(j):
                        v.wait_ge(turned, j + 1)
                        wait_count(v, hidden, j - 1)
                        v.tensor_copy(xbT[:, s, :, :].rearrange("p k n -> p (k n)"), turn_banks[s][:, :]).then_inc(staged, 1)
                    if ok(j - 2):
                        u2 = (u - 2) % S
                        v.wait_ge(made, j - 1)
                        wait_count(v, stored[s], b * 32 + (u // 2 - 1) * 16)
                        v.tensor_tensor(y[:, s, :, :], out_banks[s][:, :].rearrange("p (w d) -> p w d", w=RW),
                                        b2s[:, u2, :].unsqueeze(1).to_broadcast([128, RW, D]), ALU.add).then_inc(summed, 1)

                blocks(v, body, 2)


def experts_combine(nc, m, tag, weighted, jobs, out):
    R = 5
    with Stage(nc) as c:
        y = c.enter_context(nc.sbuf_tensor(tag + "_yy", [P, R, 2, D], F32))
        fetched = [c.sem(f"{tag}_fetched{r}") for r in range(R)]
        used, half, jobs_in, out_stored = [c.sem(tag + n) for n in ("_used", "_halfway", "_jobs_in", "_out_stored")]
        with nc.Block() as block:
            @block.sync
            def _(sp):
                if out is None:
                    run_loads(sp, jobs, jobs_in)
                else:
                    for t in range(0, NT, R):
                        sp.wait_ge(used, t + R)
                        sp.dma_start(out.rearrange("(t p) d -> p t d", p=P)[:, t:t + R, :], m.xs[:, t:t + R, :]).then_inc(out_stored, 16)
                    sp.wait_ge(out_stored, 16 * (NT // R))

            @block.gpsimd
            def _(pool):
                for t in range(NT):
                    if t >= R:
                        pool.wait_ge(used, t - R + 1)
                    for i in range(2):
                        pool.indirect_dma_start(y[:, t % R, i, :], None, m.ysort,
                                                bass.IndirectOffsetOnAxis(ap=m.yslots[:, t, i:i + 1], axis=0)).then_inc(fetched[t % R], 16)

            @block.vector
            def _(v):
                with v.Fori(0, NT // R) as b:
                    for r in range(R):
                        t = b * R + r
                        x = row_of(m.xs, t)
                        v.wait_ge(fetched[r], b * 32 + 32)
                        for i, done in ((0, half), (1, used)):
                            if weighted:
                                v.scalar_tensor_tensor(x, y[:, r, i, :], m.cw[:, i, bass.ds(t, 1)], x, ALU.mult, ALU.add).then_inc(done, 1)
                            else:
                                v.tensor_tensor(x, x, y[:, r, i, :], ALU.add).then_inc(done, 1)
                            if i == 0:
                                v.wait_ge(half, t + 1)
                        if out is None:
                            v.wait_ge(used, t + 1)
                            v.bn_stats(row_of(m.stats, t), x)


def experts(nc, m, tag, gw, gb, W1, b1, W2, b2, weighted, jobs, out):
    normalise(nc, m, tag + "_ln")
    experts_route(nc, m, tag + "_route", gw, gb, weighted)
    experts_run(nc, m, tag + "_run", W1, b1, W2, b2)
    experts_combine(nc, m, tag + "_combine", weighted, jobs, out)


def weights1(nc, m, c, w):
    def sb(n, s):
        return c.enter_context(nc.sbuf_tensor(n, s, F32))

    GH = D // 4
    m.nodew = sb("w1_node", [128, KD, D + 2 * HEADS])
    m.wqkv = sb("w1_qkv", [128, KD, 3 * D])
    m.wproj = sb("w1_proj", [128, KD, D])
    m.bproj = sb("w1_bproj", [P, D])
    m.wg1 = sb("w1_g1", [128, KD, GH])
    m.wg2 = sb("w1_g2", [GH, D])
    m.bg1 = sb("w1_bg1", [GH, 1])
    m.bg2 = sb("w1_bg2", [128, KD])
    m.lngT = sb("w1_lng", [128, KD])
    m.lnbT = sb("w1_lnb", [128, KD])
    al = m.al = sb("w1_attn", [128, 2, D])
    jobs = [(m.nodew[:, :, 0:D], w["L1_gnn_W"].rearrange("(k p) d -> p k d", p=128)),
            (al[:, 0, :], w["L1_gnn_attn_l"].rearrange("h c -> (h c)").partition_broadcast(128)),
            (al[:, 1, :], w["L1_gnn_attn_r"].rearrange("h c -> (h c)").partition_broadcast(128)),
            (m.wqkv[:, :, :], w["L1_mix_Wqkv"].rearrange("(k p) d -> p k d", p=128)),
            (m.wproj[:, :, :], w["L1_mix_Wproj"].rearrange("(k p) d -> p k d", p=128)),
            (m.bproj[:, :], w["L1_mix_bproj"].partition_broadcast(P)),
            (m.wg1[:, :, :], w["L1_mix_Wg1"].rearrange("(k p) d -> p k d", p=128)),
            (m.wg2[:, :], w["L1_mix_Wg2"]),
            (m.bg1[:, :], w["L1_mix_bg1"].rearrange("(p o) -> p o", o=1)),
            (m.bg2[:, :], w["L1_mix_bg2"].rearrange("(k p) -> p k", p=128)),
            (m.lngT[:, :], w["L1_mix_ln_g"].rearrange("(k p) -> p k", p=128)),
            (m.lnbT[:, :], w["L1_mix_ln_b"].rearrange("(k p) -> p k", p=128))]
    return jobs


def score_columns1(nc, m):
    al = m.al
    with Stage(nc) as c2:
        pr = c2.enter_context(nc.sbuf_tensor("w1_prod", [128, KD, 2, D], F32))
        chain = c2.sem("w1_chain")
        with nc.Block() as block:
            @block.vector
            def _(v):
                k = Chain(v, chain, 0)
                for b in range(KD):
                    for x in range(2):
                        k.link(v.tensor_tensor(pr[:, b, x, :], m.nodew[:, b, 0:D], al[:, x, :], ALU.mult))
                        at = D + x * HEADS
                        k.link(v.tensor_reduce(m.nodew[:, b, at:at + HEADS], pr[:, b, x, :].rearrange("p (h c) -> p h c", c=HC), AX.X, ALU.add))


def mix1_keys(nc, m):
    C = 5
    with Stage(nc) as c:
        def sb(n, s):
            return c.enter_context(nc.sbuf_tensor("keys1_" + n, s, F32))

        def sem(n):
            return c.sem("keys1_" + n)

        rden = sb("rden", [P, NT, HEADS])
        neg = sb("neg", [P, 2, C, D])
        made, kept, topped, chain, lowered, exped = [sem(n) for n in ("made", "kept", "topped", "chain", "lowered", "exped")]
        with nc.Block() as block:
            @block.tensor
            def _(pe):
                def body(t, s):
                    wait_count(pe, kept, t - 4)
                    for o in range(KD):
                        for k in range(KD):
                            ins = pe.matmul(m.bank[s][:, o * 128:o * 128 + P], m.wqkv[:, k, D + o * 128:D + (o + 1) * 128],
                                            m.xT[:, k, tile_cols(t)], start=(k == 0), stop=(k == KD - 1))
                    ins.then_inc(made, 1)

                pipelined(pe, body, 0, C)

            @block.scalar
            def _(a):
                for i in range(NT // C):
                    a.wait_ge(lowered, i + 1)
                    a.activation(neg[:, i % 2, :, :], neg[:, i % 2, :, :], ACT.Exp).then_inc(exped, 1)
                    for t in range(i * C, (i + 1) * C):
                        a.wait_ge(made, t + 1)
                        a.activation(m.kT[:, :, tile_cols(t)], by_feature(m.bank[t % C]), ACT.Copy).then_inc(kept, 1)

            @block.vector
            def _(v):
                k = Chain(v, chain, 0)
                k.link(v.tensor_scalar(rden[:, :, :], m.acc[:, :, D:D + HEADS], 1e-37, None, ALU.max))
                k.link(v.reciprocal(rden[:, :, :], rden[:, :, :]))

                def lower(i):
                    for t in range(i * C, (i + 1) * C):
                        o = m.acc[:, t, 0:D].rearrange("p (h c) -> p h c", c=HC)
                        ins = v.tensor_tensor(o, o, rden[:, t, :].unsqueeze(2).to_broadcast([P, HEADS, HC]), ALU.mult)
                    k.link(ins)
                    v.tensor_scalar(neg[:, i % 2, :, :], m.acc[:, i * C:(i + 1) * C, 0:D], 0.0, None, ALU.min).then_inc(lowered, 1)

                lower(0)
                for i in range(NT // C):
                    if i + 1 < NT // C:
                        lower(i + 1)
                    o = m.acc[:, i * C:(i + 1) * C, 0:D]
                    v.wait_ge(exped, i + 1)
                    k.link(v.scalar_tensor_tensor(o, o, 0.0, neg[:, i % 2, :, :], ALU.max, ALU.add))
                v.wait_ge(kept, NT)
                v.tensor_reduce(m.nmax[:, :], m.kT[:, :, :], AX.X, ALU.max).then_inc(topped, 1)
                v.wait_ge(topped, 1)
                v.tensor_scalar(m.nmax[:, :], m.nmax[:, :], -1.0, None, ALU.mult)


def mix1_context(nc, m):
    with Stage(nc) as c:
        def sb(n, s):
            return c.enter_context(nc.sbuf_tensor("ctx_" + n, s, F32))

        def sem(n):
            return c.sem("ctx_" + n)

        xst = sb("xst", [128, 2, KD, P])
        ekT = sb("ekT", [128, 2, KD, P])
        ek = sb("ek", [P, 2, D])
        vv = sb("v", [P, 2, D])
        part = sb("part", [128, KD, NT])
        den = sb("den", [128, KD])
        zeros = sb("zeros", [P, 128])
        staged, exped, turned, made, ekept, vkept, summed, zeroed, chain = [
            sem(n) for n in ("staged", "exped", "turned", "made", "ekept", "vkept", "summed", "zeroed", "chain")]
        bias_chain, added = sem("bias_chain"), sem("added")
        with nc.Block() as block:
            @block.scalar
            def _(a):
                def body(t, s):
                    wait_count(a, turned, t - 1)
                    for k in range(KD):
                        ins = a.activation(ekT[:, s, k, :], m.kT[:, k, tile_cols(t)], ACT.Exp, bias=m.nmax[:, k:k + 1],
                                           accum_out=part[:, k, bass.ds(t, 1)])
                    ins.then_inc(exped, 1)
                    wait_count(a, made, t - 1)
                    a.activation(xst[:, s, :, :], m.xT[:, :, tile_cols(t)], ACT.Copy).then_inc(staged, 1)

                pipelined(a, body, 0)

            @block.tensor
            def _(pe):
                pe.wait_ge(zeroed, 1)
                pe.matmul(m.bank[4][:, 0:D], zeros[:, :], zeros[:, :].unsqueeze(1).to_broadcast([P, KD, 128]), start=True, stop=False)

                def body(t, s):
                    if valid(t):
                        pe.wait_ge(exped, t + 1)
                        wait_count(pe, ekept, t - 1)
                        for k in range(KD):
                            ins = pe.transpose(m.bank[s][0:P, k * 128:(k + 1) * 128], ekT[:, s, k, :], m.ident[:, :])
                        ins.then_inc(turned, 1)
                        pe.wait_ge(staged, t + 1)
                        wait_count(pe, vkept, t - 1)
                        for k in range(KD):
                            ins = pe.matmul(m.bank[2 + s][0:P, 0:D], xst[:, s, k, :], m.wqkv[:, k, 2 * D:3 * D], start=(k == 0), stop=(k == KD - 1))
                        ins.then_inc(made, 1)
                    if valid(t - 1):
                        pe.wait_ge(vkept, t)
                        for k in range(KD):
                            ins = pe.matmul(m.bank[4][:, k * 128:(k + 1) * 128], ek[:, 1 - s, k * 128:(k + 1) * 128],
                                            vv[:, 1 - s, k * 128:(k + 1) * 128], start=False, stop=False, skip_group_check=True)
                        ins.then_inc(summed, 1)

                pipelined(pe, body, 1)
                pe.matmul(m.bank[4][:, 0:D], zeros[:, :], zeros[:, :].unsqueeze(1).to_broadcast([P, KD, 128]),
                          start=False, stop=True).then_inc(summed, 1)

            @block.vector
            def _(v):
                v.memset(zeros[:, :], 0.0).then_inc(zeroed, 1)

                def body(t, s):
                    x = row_of(m.xs, t)
                    v.scalar_tensor_tensor(x, x, -1.0, m.bproj[:, :], ALU.add, ALU.add).then_inc(bias_chain, 1)
                    v.wait_ge(turned, t + 1)
                    wait_count(v, summed, t - 1)
                    v.tensor_copy(ek[:, s, :], m.bank[s][0:P, 0:D]).then_inc(ekept, 1)
                    v.wait_ge(made, t + 1)
                    v.tensor_copy(vv[:, s, :], m.bank[2 + s][0:P, 0:D]).then_inc(vkept, 1)
                    v.wait_ge(bias_chain, t + 1)
                    x = row_of(m.xs, t)
                    v.tensor_tensor(x, x, row_of(m.acc[:, :, 0:D], t), ALU.add).then_inc(added, 1)

                pipelined(v, body, 0)
                k = Chain(v, chain, 0)
                v.wait_ge(exped, NT)
                k.link(v.tensor_reduce(den[:, :], part[:, :, :], AX.X, ALU.add))
                k.link(v.reciprocal(den[:, :], den[:, :]))
                v.wait_ge(summed, NT + 1)
                for b in range(KD):
                    k.link(v.scalar_tensor_tensor(m.kv[:, b, :], m.bank[4][:, b * 128:(b + 1) * 128], den[:, b:b + 1],
                                                  m.headmask[:, :], ALU.mult, ALU.mult))


def mix1_out(nc, m):
    with Stage(nc) as c:
        def sb(n, s):
            return c.enter_context(nc.sbuf_tensor("out1_" + n, s, F32))

        def sem(n):
            return c.sem("out1_" + n)

        qT = sb("qT", [128, 2, KD, P])
        eg = sb("eg", [128, 2, KD, P])
        goT = sb("goT", [128, 2, KD, P])
        queried, qkept, mixed, gated, opened, gone, made, added = [
            sem(n) for n in ("queried", "qkept", "mixed", "gated", "opened", "gone", "made", "added")]
        with nc.Block() as block:
            @block.tensor
            def _(pe):
                def body(t, s):
                    if valid(t):
                        wait_count(pe, qkept, t - 1)
                        for o in range(KD):
                            for k in range(KD):
                                ins = pe.matmul(m.bank[s][:, o * 128:o * 128 + P], m.wqkv[:, k, o * 128:(o + 1) * 128],
                                                m.xT[:, k, tile_cols(t)], start=(k == 0), stop=(k == KD - 1))
                        ins.then_inc(queried, 1)
                        wait_count(pe, opened, t)
                        for o in range(KD):
                            ins = pe.matmul(m.bank[6][:, o * 128:o * 128 + P], m.wg2[:, o * 128:(o + 1) * 128], m.hgT[:, tile_cols(t)],
                                            start=True, stop=True)
                        ins.then_inc(gated, 1)
                    if valid(t - 1):
                        pe.wait_ge(qkept, t)
                        wait_count(pe, gone, t - 2)
                        for k in range(KD):
                            ins = pe.matmul(m.bank[3 - s][:, k * 128:k * 128 + P], m.kv[:, k, :], qT[:, 1 - s, k, :], start=True, stop=True)
                        ins.then_inc(mixed, 1)
                    if valid(t - 2):
                        pe.wait_ge(gone, t - 1)
                        wait_count(pe, added, t - 3)
                        for k in range(KD):
                            ins = pe.matmul(m.bank[4 + s][0:P, 0:D], goT[:, s, k, :], m.wproj[:, k, :], start=(k == 0), stop=(k == KD - 1))
                        ins.then_inc(made, 1)

                pipelined(pe, body, 2)

            @block.scalar
            def _(a):
                def body(t, s):
                    a.wait_ge(queried, t + 1)
                    wait_count(a, mixed, t - 1)
                    a.activation(qT[:, s, :, :], by_feature(m.bank[s]), ACT.Copy).then_inc(qkept, 1)
                    a.wait_ge(gated, t + 1)
                    wait_count(a, gone, t - 1)
                    for k in range(KD):
                        ins = a.activation(eg[:, s, k, :], m.bank[6][:, k * 128:k * 128 + P], ACT.Sigmoid, bias=m.bg2[:, k:k + 1])
                    ins.then_inc(opened, 1)

                pipelined(a, body, 0)

            @block.vector
            def _(v):
                def body(t, s):
                    if valid(t):
                        v.wait_ge(opened, t + 1)
                        v.wait_ge(mixed, t + 1)
                        wait_count(v, made, t - 1)
                        v.tensor_tensor(goT[:, s, :, :], by_feature(m.bank[2 + s]), eg[:, s, :, :], ALU.mult).then_inc(gone, 1)
                    if valid(t - 1):
                        x = row_of(m.xs, t - 1)
                        v.wait_ge(made, t)
                        v.tensor_tensor(x, x, m.bank[5 - s][0:P, 0:D], ALU.add).then_inc(added, 1)
                    if valid(t - 2):
                        v.wait_ge(added, t - 1)
                        v.bn_stats(row_of(m.stats, t - 2), row_of(m.xs, t - 2))

                pipelined(v, body, 2)


def program(nc, w, out):
    m = Memory()
    m.edges = nc.dram_tensor("edge_list", [E + PAD, 2], I32).ap()
    m.table = {H: nc.dram_tensor(f"table{H}", [N, table_width(H)], F32).ap() for H in (1, HEADS)}
    m.xsort = nc.dram_tensor("xsort", [SORTED, D], F32).ap()
    m.ysort = nc.dram_tensor("ysort", [NB * ROWS, D], F32).ap()
    with ExitStack() as c:
        c.enter_context(nc.allow_non_contiguous_dma(reason="biases of a few hundred elements, one per partition"))

        def sb(n, s, d=F32):
            return c.enter_context(nc.sbuf_tensor(n, s, d))

        m.bank = [c.enter_context(nc.psum_tensor(f"bank{i}", [128, 512], F32)) for i in range(8)]
        m.ident = sb("ident", [128, 128])
        m.ones = sb("ones", [128, 128])
        m.before = sb("before", [P, P])
        m.headmask = sb("headmask", [128, 128])
        m.count = sb("count", [128, P])
        m.local = sb("local", [128, NG * WIN])
        m.half = sb("half", [128, 64])
        m.xs = sb("xs", [P, NT, D])
        m.xT = sb("xT", [128, KD, N])
        m.acc = sb("acc", [P, NT, D + HEADS])
        m.adm = sb("adm", [P, NT, 2 * HEADS])
        m.mean = sb("mean", [P, NT])
        m.rstd = sb("rstd", [P, NT])
        m.var = sb("var", [P, NT])
        m.stats = sb("stats", [P, NT, 6])
        m.grow = sb("grow", [1, 2, 2, 128], I32)
        m.gtab = sb("gtab", [1, 2, NG], I32)
        m.kv = sb("kv", [128, KD, 128])
        m.cw = sb("cw", [P, 2, NT])
        m.slots = sb("slots", [P, NT, 2], I32)
        m.yslots = sb("yslots", [P, NT, 2], I32)
        m.btab = sb("btab", [1, 2, NB], I32)
        m.eall = sb("eall", [128, NG * 4], I32)
        constants(nc, m)
        with ExitStack() as layer:
            jobs = weights0(nc, m, layer, w)
            edge_tables(nc, m, w["src"], w["dst"], w["x"], jobs)
            weights0_turned(nc, m)
            normalise(nc, m, "ln0")
            node_tables(nc, m, "nt0", 1, edge_part=EDGE_PARTS[0])
            mix0_keys(nc, m)
            mix0_queries(nc, m)
            mix0_out(nc, m)
            edge_columns(nc, m)
            score_bounds(nc, m, "sb0", 1)
            edge_sums(nc, m, "es0", 1)
            graph_attention0(nc, m)
        with ExitStack() as layer:
            jobs = weights1(nc, m, layer, w)
            experts(nc, m, "ffn0", w["L0_ffn_gate_w"], w["L0_ffn_gate_b"], w["L0_ffn_W1"], w["L0_ffn_b1"],
                    w["L0_ffn_W2"], w["L0_ffn_b2"], True, jobs, None)
            score_columns1(nc, m)
            m.kT = layer.enter_context(nc.sbuf_tensor("kT", [128, KD, N], F32))
            m.hgT = layer.enter_context(nc.sbuf_tensor("hgT", [D // 4, N], F32))
            m.nmax = layer.enter_context(nc.sbuf_tensor("nmax", [128, KD], F32))
            normalise(nc, m, "ln1")
            node_tables(nc, m, "nt1", HEADS, True)
            score_bounds(nc, m, "sb1", HEADS)
            edge_sums(nc, m, "es1", HEADS)
            mix1_keys(nc, m)
            mix1_context(nc, m)
            mix1_out(nc, m)
        experts(nc, m, "ffn1", w["L1_ffn_Wg"], w["L1_ffn_bg"], w["L1_ffn_W1"], w["L1_ffn_b1"],
                w["L1_ffn_W2"], w["L1_ffn_b2"], False, [], out)


_INS = ["x", "src", "dst", "L0_gnn_W", "L0_gnn_att_src", "L0_gnn_att_dst", "L0_gnn_bias", "L0_gnn_W_ih",
        "L0_mix_w_qkv", "L0_mix_b_qkv", "L0_mix_kln_g", "L0_mix_kln_b", "L0_mix_vln_g", "L0_mix_vln_b",
        "L0_mix_w1", "L0_mix_b1", "L0_mix_w2", "L0_mix_b2", "L0_ffn_gate_w", "L0_ffn_gate_b", "L0_ffn_W1",
        "L0_ffn_b1", "L0_ffn_W2", "L0_ffn_b2", "L1_gnn_W", "L1_gnn_attn_l", "L1_gnn_attn_r", "L1_mix_Wqkv",
        "L1_mix_Wproj", "L1_mix_bproj", "L1_mix_ln_g", "L1_mix_ln_b", "L1_mix_Wg1", "L1_mix_bg1",
        "L1_mix_Wg2", "L1_mix_bg2", "L1_ffn_Wg", "L1_ffn_bg", "L1_ffn_W1", "L1_ffn_b1", "L1_ffn_W2", "L1_ffn_b2"]


def kernel(**inputs):
    import numpy as np
    import concourse.bacc as bacc
    from concourse.bass_utils import run_bass_kernel_spmd

    nc = bacc.Bacc("TRN2", target_bir_lowering=False, num_devices=1)
    arrays, args = {}, {}
    for name in _INS:
        a = np.ascontiguousarray(inputs[name])
        arrays[f"in_{name}"] = a
        args[name] = nc.dram_tensor(f"in_{name}", a.shape, mybir.dt.from_np(a.dtype), kind="ExternalInput").ap()
    out = nc.dram_tensor("out_x", (N, D), F32, kind="ExternalOutput").ap()
    program(nc, args, out)
    r = run_bass_kernel_spmd(nc, [arrays], core_ids=[0])
    return r.results[0]["out_x"]
```
